# Optimizing a Trainium2 kernel written in Bass

```python
import numpy as np
import jax
import jax.numpy as jnp

def _softmax(x, axis=-1):
    return jax.nn.softmax(x, axis=axis)

def _gelu(x):
    return jax.nn.gelu(x, approximate=True)

def _silu(x):
    return jax.nn.silu(x)

def _sigmoid(x):
    return jax.nn.sigmoid(x)

def _layernorm(x, axis=-1, eps=1e-05):
    m = jnp.mean(x, axis=axis, keepdims=True)
    v = jnp.var(x, axis=axis, keepdims=True)
    return (x - m) / jnp.sqrt(v + eps)

def _scatter_add(tgt, idx, src, axis=0):
    return tgt.at[idx].add(src)

def _segment_sum(src, seg, n):
    return jax.ops.segment_sum(src, seg, n)
kernel_name = 'mk_gnn_preln_d2_gnn_r16_4d0414'

def setup_inputs(seed: int=0):
    np.random.seed(seed)
    _w = jnp.asarray

    def _rec_inputs():
        import jax
        import jax.numpy as jnp
        _gk = jax.random.key(seed)
        x = -0.000202 + 1 * jax.random.normal(jax.random.fold_in(_gk, 1), (6250, 128), jnp.float32)
        src = jax.random.randint(jax.random.fold_in(_gk, 2), (200000,), 0, 6250, jnp.int32)
        dst = jax.random.randint(jax.random.fold_in(_gk, 3), (200000,), 0, 6250, jnp.int32)
        _o = jnp.argsort(dst, stable=True)
        src = src[_o]
        dst = dst[_o]
        return (x, src, dst)
    x, src, dst = _rec_inputs()

    def _L0_gnn_setup():
        import jax, jax.numpy as jnp
        import numpy as np
        N, E = (3125, 50000)
        IN_F, OUT_F, H = (128, 128, 10)
        DH = 13

        def _layer_norm(x, w, b):
            mu = jnp.mean(x, axis=-1, keepdims=True)
            var = jnp.var(x, axis=-1, keepdims=True)
            return (x - mu) * jax.lax.rsqrt(var + 1e-05) * w + b
        key = jax.random.key(seed)
        ks = jax.random.split(key, 12)
        s = 0.05
        return {'h': jax.random.normal(ks[0], (N, IN_F), jnp.float32), 'src': jax.random.randint(ks[1], (E,), 0, N, jnp.int32), 'dst': jax.random.randint(ks[2], (E,), 0, N, jnp.int32), 'ln1_w': jnp.ones((IN_F,), jnp.float32), 'ln1_b': jnp.zeros((IN_F,), jnp.float32), 'W_att': jax.random.normal(ks[3], (IN_F, H * DH), jnp.float32) * s, 'hr_w': jax.random.normal(ks[4], (H * DH, OUT_F), jnp.float32) * s, 'hr_b': jnp.zeros((OUT_F,), jnp.float32), 'in_w': jnp.ones((OUT_F,), jnp.float32), 'in_b': jnp.zeros((OUT_F,), jnp.float32), 'w1': jax.random.normal(ks[5], (OUT_F, 4 * OUT_F), jnp.float32) * s, 'b1': jnp.zeros((4 * OUT_F,), jnp.float32), 'w2': jax.random.normal(ks[6], (4 * OUT_F, OUT_F), jnp.float32) * s, 'b2': jnp.zeros((OUT_F,), jnp.float32)}
    _L0_gnn_all = _L0_gnn_setup()
    _L0_gnn_in = {k: v for k, v in _L0_gnn_all.items() if k in ('ln1_w', 'ln1_b', 'W_att', 'hr_w', 'hr_b', 'in_w', 'in_b', 'w1', 'b1', 'w2', 'b2')}
    del _L0_gnn_all

    def _L1_gnn_setup():
        import jax, jax.numpy as jnp
        import numpy as np
        N_NODES = 6250
        N_EDGES = 37500
        D = 128
        EPS = 1e-05

        def _gcn_conv(x, src, dst, W, b, n_nodes):
            h = x @ W
            loops = jnp.arange(n_nodes, dtype=src.dtype)
            s = jnp.concatenate([src, loops])
            d = jnp.concatenate([dst, loops])
            deg = jax.ops.segment_sum(jnp.ones_like(d, dtype=h.dtype), d, num_segments=n_nodes)
            dis = jnp.where(deg > 0, jax.lax.rsqrt(deg), 0.0)
            norm = dis[s] * dis[d]
            msg = h[s] * norm[:, None]
            out = jax.ops.segment_sum(msg, d, num_segments=n_nodes)
            return out + b

        def _batch_norm(x, gamma, beta):
            mean = jnp.mean(x, axis=0)
            var = jnp.mean(jnp.square(x - mean), axis=0)
            return (x - mean) * jax.lax.rsqrt(var + EPS) * gamma + beta
        key = jax.random.key(seed)
        ks = jax.random.split(key, 16)
        glorot = lambda k, i, o: jax.random.normal(k, (i, o), jnp.float32) * np.sqrt(2.0 / (i + o))
        return {'x': jax.random.normal(ks[0], (N_NODES, D), jnp.float32), 'edge_src': jax.random.randint(ks[1], (N_EDGES,), 0, N_NODES, jnp.int32), 'edge_dst': jax.random.randint(ks[2], (N_EDGES,), 0, N_NODES, jnp.int32), 'W1': glorot(ks[3], D, D), 'b1': jnp.zeros((D,), jnp.float32), 'g1': jnp.ones((D,), jnp.float32), 'be1': jnp.zeros((D,), jnp.float32), 'W2': glorot(ks[4], D, D), 'b2': jnp.zeros((D,), jnp.float32), 'g2': jnp.ones((D,), jnp.float32), 'be2': jnp.zeros((D,), jnp.float32), 'W3': glorot(ks[5], D, D), 'b3': jnp.zeros((D,), jnp.float32)}
    _L1_gnn_all = _L1_gnn_setup()
    _L1_gnn_in = {k: v for k, v in _L1_gnn_all.items() if k in ('W1', 'b1', 'g1', 'be1', 'W2', 'b2', 'g2', 'be2', 'W3', 'b3')}
    del _L1_gnn_all
    return {'x': x, 'src': src, 'dst': dst, 'L0_gnn_ln1_w': _L0_gnn_in['ln1_w'], 'L0_gnn_ln1_b': _L0_gnn_in['ln1_b'], 'L0_gnn_W_att': _L0_gnn_in['W_att'], 'L0_gnn_hr_w': _L0_gnn_in['hr_w'], 'L0_gnn_hr_b': _L0_gnn_in['hr_b'], 'L0_gnn_in_w': _L0_gnn_in['in_w'], 'L0_gnn_in_b': _L0_gnn_in['in_b'], 'L0_gnn_w1': _L0_gnn_in['w1'], 'L0_gnn_b1': _L0_gnn_in['b1'], 'L0_gnn_w2': _L0_gnn_in['w2'], 'L0_gnn_b2': _L0_gnn_in['b2'], 'L1_gnn_W1': _L1_gnn_in['W1'], 'L1_gnn_b1': _L1_gnn_in['b1'], 'L1_gnn_g1': _L1_gnn_in['g1'], 'L1_gnn_be1': _L1_gnn_in['be1'], 'L1_gnn_W2': _L1_gnn_in['W2'], 'L1_gnn_b2': _L1_gnn_in['b2'], 'L1_gnn_g2': _L1_gnn_in['g2'], 'L1_gnn_be2': _L1_gnn_in['be2'], 'L1_gnn_W3': _L1_gnn_in['W3'], 'L1_gnn_b3': _L1_gnn_in['b3']}

def reference(x, src, dst, L0_gnn_ln1_w, L0_gnn_ln1_b, L0_gnn_W_att, L0_gnn_hr_w, L0_gnn_hr_b, L0_gnn_in_w, L0_gnn_in_b, L0_gnn_w1, L0_gnn_b1, L0_gnn_w2, L0_gnn_b2, L1_gnn_W1, L1_gnn_b1, L1_gnn_g1, L1_gnn_be1, L1_gnn_W2, L1_gnn_b2, L1_gnn_g2, L1_gnn_be2, L1_gnn_W3, L1_gnn_b3):
    import jax
    import jax.numpy as jnp

    def _L0_gnn_ref(h, src, dst, ln1_w, ln1_b, W_att, hr_w, hr_b, in_w, in_b, w1, b1, w2, b2):
        import jax, jax.numpy as jnp
        import numpy as np
        N, E = (3125, 50000)
        IN_F, OUT_F, H = (128, 128, 10)
        DH = 13

        def _layer_norm(x, w, b):
            mu = jnp.mean(x, axis=-1, keepdims=True)
            var = jnp.var(x, axis=-1, keepdims=True)
            return (x - mu) * jax.lax.rsqrt(var + 1e-05) * w + b
        n = h.shape[0]
        hn = _layer_norm(h, ln1_w, ln1_b)
        h_skip = hn
        ft = (hn @ W_att).reshape(n, H, DH)
        ft_s = ft[src]
        ft_d = ft[dst]
        scores = jnp.einsum('ehd,ehd->eh', ft_s, ft_d) / jnp.sqrt(jnp.float32(DH))
        m = jax.ops.segment_max(scores, dst, num_segments=n)
        ex = jnp.exp(scores - m[dst])
        z = jax.ops.segment_sum(ex, dst, num_segments=n)
        a = ex / z[dst]
        agg = jax.ops.segment_sum(ft_s * a[:, :, None], dst, num_segments=n)
        out = jax.nn.elu(agg)
        out = out.reshape(n, H * DH) @ hr_w + hr_b
        out = out + h_skip
        out = _layer_norm(out, in_w, in_b)
        skip2 = out
        out = jax.nn.elu(out @ w1 + b1)
        out = jax.nn.elu(out @ w2 + b2)
        return out + skip2

    def _L1_gnn_ref(x, edge_src, edge_dst, W1, b1, g1, be1, W2, b2, g2, be2, W3, b3):
        import jax, jax.numpy as jnp
        import numpy as np
        N_NODES = 6250
        N_EDGES = 37500
        D = 128
        EPS = 1e-05

        def _gcn_conv(x, src, dst, W, b, n_nodes):
            h = x @ W
            loops = jnp.arange(n_nodes, dtype=src.dtype)
            s = jnp.concatenate([src, loops])
            d = jnp.concatenate([dst, loops])
            deg = jax.ops.segment_sum(jnp.ones_like(d, dtype=h.dtype), d, num_segments=n_nodes)
            dis = jnp.where(deg > 0, jax.lax.rsqrt(deg), 0.0)
            norm = dis[s] * dis[d]
            msg = h[s] * norm[:, None]
            out = jax.ops.segment_sum(msg, d, num_segments=n_nodes)
            return out + b

        def _batch_norm(x, gamma, beta):
            mean = jnp.mean(x, axis=0)
            var = jnp.mean(jnp.square(x - mean), axis=0)
            return (x - mean) * jax.lax.rsqrt(var + EPS) * gamma + beta
        n = x.shape[0]
        h = _gcn_conv(x, edge_src, edge_dst, W1, b1, n)
        h = jax.nn.relu(_batch_norm(h, g1, be1))
        h = _gcn_conv(h, edge_src, edge_dst, W2, b2, n)
        h = jax.nn.relu(_batch_norm(h, g2, be2))
        h = jax.nn.relu(_gcn_conv(h, edge_src, edge_dst, W3, b3, n))
        h = _gcn_conv(h, edge_src, edge_dst, W3, b3, n)
        return h
    h = jnp.maximum(_layernorm(x, axis=-1), 0.0)
    x = x + _L0_gnn_ref(h, src, dst, L0_gnn_ln1_w, L0_gnn_ln1_b, L0_gnn_W_att, L0_gnn_hr_w, L0_gnn_hr_b, L0_gnn_in_w, L0_gnn_in_b, L0_gnn_w1, L0_gnn_b1, L0_gnn_w2, L0_gnn_b2)
    h = jnp.maximum(_layernorm(x, axis=-1), 0.0)
    x = x + _L1_gnn_ref(h, src, dst, L1_gnn_W1, L1_gnn_b1, L1_gnn_g1, L1_gnn_be1, L1_gnn_W2, L1_gnn_b2, L1_gnn_g2, L1_gnn_be2, L1_gnn_W3, L1_gnn_b3)
    return x

_drawn_inputs = setup_inputs


def setup_inputs(seed=0):
    import zlib

    import numpy as np

    out = dict(_drawn_inputs(seed))
    spreads = {'L0_gnn_ln1_w': (1.0, 0.2),
     'L0_gnn_ln1_b': (0.0, 0.1),
     'L0_gnn_hr_b': (0.0, 0.1),
     'L0_gnn_in_w': (1.0, 0.2),
     'L0_gnn_in_b': (0.0, 0.1),
     'L0_gnn_b1': (0.0, 0.1),
     'L0_gnn_b2': (0.0, 0.1),
     'L1_gnn_b1': (0.0, 0.8),
     'L1_gnn_g1': (1.0, 0.6),
     'L1_gnn_be1': (0.0, 0.8),
     'L1_gnn_b2': (0.0, 0.8),
     'L1_gnn_g2': (1.0, 0.575),
     'L1_gnn_be2': (0.0, 0.648),
     'L1_gnn_b3': (0.0, 0.1)}
    factors = {'L1_gnn_W1': 8.0, 'L1_gnn_W2': 7.198}
    for name, (base, spread) in spreads.items():
        noise = np.random.default_rng([zlib.crc32(name.encode()), seed]).standard_normal(out[name].shape)
        drawn = base * np.exp(spread * noise) if base else spread * noise
        out[name] = jnp.asarray(drawn.astype(out[name].dtype))
    for name, factor in factors.items():
        out[name] = (out[name] * factor).astype(out[name].dtype)
    return out
```

```python
import concourse.bass as bass
from concourse import mybir
from concourse.alu_op_type import AluOpType as ALU
from contextlib import ExitStack

F32 = mybir.dt.float32
BF16 = mybir.dt.bfloat16
FP16 = mybir.dt.float16
I32 = mybir.dt.int32
ACT = mybir.ActivationFunctionType
AX = mybir.AxisListType
ds = bass.ds

P = 128
D = 128
N = 6250
E = 200000
NT = -(-N // P)
NP = NT * P
N_LAST = N - (NT - 1) * P
H, DH = 10, 13
HD = H * DH
BATCH = 7
NB = NT // BATCH
BW = BATCH * D

GC = 8
GE = GC * P
NG = -(-E // GE)
EP = NG * GE
EJ = EP // P

SUB = 32
NS = NP // SUB
SC = 10
SW = SC * P
STRIP = NT * SUB
TC = 35
TW = TC * P
COARSE = 32
FRONT = 16
EX = -(-(E + TW) // (16 * P)) * 16 * P
EXJ = EX // P
KS = 4096.0
NOWHERE = NP
TAB = NP + P
NEG = -1.0e38
EPS = 1e-5
UN = 4
GRP = 512
NGR = NP // GRP
SPG = GRP // SUB
CHUNKS = [(0, 16), (16, 16), (32, 17)]
CMAX = 17


def gnn_program(nc, t):
    out = t["out"]
    dram = lambda name, shape, dt: nc.dram_tensor(name, shape, dt).ap()
    dst_pad = dram("dst_pad", (FRONT + EX + FRONT,), I32)
    src_pad = dram("src_pad", (EX,), I32)
    edge_key = dram("edge_key", (EX, 3), F32)
    ft_tab = dram("ft_tab", (TAB, HD), F32)
    edge_ft = dram("edge_ft", (EX, HD), F32)
    edge_score = dram("edge_score", (EX, H), F32)
    edge_exp = dram("edge_exp", (EX, H), F32)
    adj = dram("adj", (NS, P, STRIP), BF16)
    hn_dram = dram("hn_dram", (NP, D), F32)
    hT_dram = dram("hT_dram", (D, NP), F32)

    top = ExitStack()
    with top:
        def sb(name, shape, dt, on=top):
            return on.enter_context(nc.sbuf_tensor(name, shape, dt))

        def pb(name, shape, dt, on):
            return on.enter_context(nc.psum_tensor(name, shape, dt))

        def sem(name):
            return top.enter_context(nc.semaphore(name))

        x_sb = sb("x_sb", [P, NT, D], F32)
        ident = sb("ident", [P, P], F32)
        ident_bf = sb("ident_bf", [P, P], BF16)
        ones = sb("ones", [P, P], F32)
        eps = sb("eps", [P, 1], F32)
        starts = sb("starts", [1, NS], I32)
        bases = sb("bases", [1, NG], I32)
        base_bc = sb("base_bc", [P, NG], F32)
        strip_no = sb("strip_no", [P, NS], F32)
        dis_col = sb("dis_col", [P, NT], F32)

        def ln_batch(nm, on):
            return dict(st=sb(nm + "_st", [P, BATCH, 6], F32, on), mv=sb(nm + "_mv", [P, BATCH, 2], F32, on),
                        sd=sb(nm + "_sd", [P, BATCH], F32, on), rs=sb(nm + "_rs", [P, BATCH], F32, on),
                        nb=sb(nm + "_nb", [P, BATCH], F32, on))

        prelude(nc, t, sb, pb, sem, locals(), ln_batch)
        with ExitStack() as mid:
            node_features(nc, t, sb, pb, sem, locals(), ln_batch)
            scores_and_strips(nc, t, sb, pb, sem, locals())
            softmax_numerators(nc, t, sb, pb, sem, locals())
            agg_sb = sb("agg_sb", [P, NT, HD], F32, mid)
            aggregate(nc, t, sb, pb, sem, locals())
            node_update(nc, t, sb, pb, sem, locals(), ln_batch)
        convolutions(nc, t, sb, pb, sem, locals())


def settle(engine, steps_taken):
    engine.sem_inc(steps_taken, 1)


def rounds(engine, n, body):
    body(0, True)
    with engine.Fori(1, n) as i:
        body(i, False)


class Chain:

    def __init__(self, engine, semaphore, base=0):
        self.engine, self.sem, self.n, self.base = engine, semaphore, 0, base

    def __call__(self, ins):
        self.n += 1
        ins.then_inc(self.sem, 1)
        self.engine.wait_ge(self.sem, self.base + self.n)


def prelude(nc, t, sb, pb, sem, g, ln_batch):
    dst_pad, src_pad, edge_key, ft_tab, edge_ft, edge_exp = (g[k] for k in (
        "dst_pad", "src_pad", "edge_key", "ft_tab", "edge_ft", "edge_exp"))
    x_sb, ident, ident_bf, ones, eps, starts, bases, base_bc, strip_no = (g[k] for k in (
        "x_sb", "ident", "ident_bf", "ones", "eps", "starts", "bases", "base_bc", "strip_no"))
    with ExitStack() as c:
        fill_no = sb("fill_no", [16, 512], I32, c)
        fill_zero = sb("fill_zero", [16, 512], I32, c)
        fill_neg = sb("fill_neg", [1, FRONT], I32, c)
        zero_f = sb("zero_f", [P, TC * HD], F32, c)
        dst_p = sb("dst_p", [P, EXJ], I32, c)
        src_p = sb("src_p", [P, EXJ], I32, c)
        dst_s = sb("dst_s", [P, EJ], I32, c)
        hi = sb("hi", [P, EXJ], I32, c)
        lo = sb("lo", [P, EXJ], I32, c)
        keys = sb("keys", [P, EXJ, 3], F32, c)
        kf = sb("kf", [P, 2, EXJ], F32, c)
        coarse = sb("coarse", [P, EJ // COARSE], F32, c)
        thr = sb("thr", [P, NS], F32, c)
        below = sb("below", [P, NS, EJ // COARSE], F32, c)
        below_n = sb("below_n", [P, NS], F32, c)
        start_f = sb("start_f", [1, NS], F32, c)
        base_f = sb("base_f", [1, NG], F32, c)
        cnt_ps = pb("cnt_ps", [P, 512], F32, c)
        base_ps = pb("base_ps", [P, 512], F32, c)
        pool_const = sem("pool_const")
        filled = sem("filled")
        pads_out = sem("pads_out")
        lists_in = sem("lists_in")
        x_in = sem("x_in")
        keys_made = sem("keys_made")
        keys_out = sem("keys_out")
        counted = sem("counted")
        counts_summed = sem("counts_summed")
        dve_chain = sem("prelude_dve_chain")
        pool_chain = sem("prelude_pool_chain")
        block = c.enter_context(nc.Block())

        @block.gpsimd
        def _(pool):
            link = Chain(pool, pool_chain)
            nc.gpsimd.iota(strip_no[:], [[1, NS]], base=0, channel_multiplier=0,
                           allow_small_or_imprecise_dtypes=True)
            nc.gpsimd.iota(thr[:], [[SUB, NS]], base=0, channel_multiplier=0,
                           allow_small_or_imprecise_dtypes=True)
            link(nc.gpsimd.memset(ident[:], 0.0))
            link(nc.gpsimd.affine_select(out=ident[:], in_=ident[:], compare_op=ALU.not_equal, fill=1.0,
                                         base=0, pattern=[[-1, P]], channel_multiplier=1))
            nc.gpsimd.tensor_copy(ident_bf[:], ident[:]).then_inc(pool_const, 1)

        @block.sync
        def _(sp):
            sp.wait_ge(filled, 1)
            for k in range(0, NT - 1, 8):
                sp.dma_start(x_sb[:, k:k + 8, :], t["x"][k * P:(k + 8) * P, :].rearrange("(b p) d -> p b d", p=P)
                             ).then_inc(x_in, 16)
            sp.dma_start(x_sb[0:N_LAST, NT - 1, :], t["x"][(NT - 1) * P:N, :]).then_inc(x_in, 16)
            sp.dma_start(dst_pad[FRONT:FRONT + E].rearrange("(a b) -> a b", a=16),
                         t["dst"].rearrange("(a b) -> a b", a=16)).then_inc(pads_out, 16)
            sp.dma_start(src_pad[0:E].rearrange("(a b) -> a b", a=16),
                         t["src"].rearrange("(a b) -> a b", a=16)).then_inc(pads_out, 16)
            tail = EX - E + FRONT
            sp.dma_start(dst_pad[FRONT + E:FRONT + EX + FRONT].rearrange("(a b) -> a b", a=16),
                         fill_no[:, 0:tail // 16]).then_inc(pads_out, 16)
            sp.dma_start(src_pad[E:EX].rearrange("(a b) -> a b", a=16),
                         fill_zero[:, 0:(EX - E) // 16]).then_inc(pads_out, 16)
            sp.dma_start(dst_pad[0:FRONT].rearrange("(a b) -> a b", a=1), fill_neg[:]).then_inc(pads_out, 16)
            sp.dma_start(ft_tab[NP:TAB, :], zero_f[:, 0:HD]).then_inc(pads_out, 16)
            sp.dma_start(edge_ft[EP:EX, :].rearrange("(p c) f -> p (c f)", p=P),
                         zero_f[:, 0:(EX - EP) // P * HD]).then_inc(pads_out, 16)
            sp.dma_start(edge_exp[EP:EX, :].rearrange("(p c) f -> p (c f)", p=P),
                         zero_f[:, 0:(EX - EP) // P * H]).then_inc(pads_out, 16)
            sp.wait_ge(pads_out, 8 * 16)
            sp.dma_start(dst_p[:], dst_pad[FRONT:FRONT + EX].rearrange("(p j) -> p j", p=P)).then_inc(lists_in, 16)
            sp.dma_start(src_p[:], src_pad.rearrange("(p j) -> p j", p=P)).then_inc(lists_in, 16)
            sp.dma_start(dst_s[:], dst_pad[FRONT:FRONT + EP].rearrange("(p j) -> p j", p=P)).then_inc(lists_in, 16)
            with nc.allow_non_contiguous_dma(reason="first destination of every group"):
                sp.dma_start(bases[0:1, :], dst_pad[FRONT:FRONT + EP].rearrange("(g e) -> e g", e=GE)[0:1, :]
                             ).then_inc(lists_in, 16)
            sp.wait_ge(keys_made, 1)
            sp.dma_start(edge_key.rearrange("(p j) k -> p (j k)", p=P),
                         keys[:].rearrange("p j k -> p (j k)")).then_inc(keys_out, 16)
            sp.wait_ge(keys_out, 16)
            sp.wait_ge(x_in, 16 * 7)

        @block.vector
        def _(dve):
            link = Chain(dve, dve_chain)
            nc.vector.memset(x_sb[:, NT - 1, :], 0.0)
            nc.vector.memset(fill_no[:], NOWHERE)
            nc.vector.memset(fill_zero[:], 0)
            nc.vector.memset(fill_neg[:], -1)
            nc.vector.memset(eps[:], EPS)
            nc.vector.memset(zero_f[:], 0.0)
            link(nc.vector.memset(ones[:], 1.0))
            nc.vector.tensor_copy(kf[0:1, 0, 0:1], ones[0:1, 0:1]).then_inc(filled, 1)
            dve.wait_ge(lists_in, 64)
            nc.vector.tensor_single_scalar(hi[:], dst_p[:], 5, ALU.logical_shift_right)
            link(nc.vector.tensor_scalar(lo[:], src_p[:], 127, None, ALU.bitwise_and))
            nc.vector.tensor_copy(keys[:, :, 2], lo[:])
            link(nc.vector.tensor_copy(keys[:, :, 0], hi[:]))
            nc.vector.tensor_scalar(hi[:], src_p[:], 7, 5, ALU.logical_shift_right, ALU.logical_shift_left)
            link(nc.vector.tensor_scalar(lo[:], dst_p[:], 31, None, ALU.bitwise_and))
            nc.vector.tensor_copy(kf[:, 0, :], hi[:])
            link(nc.vector.tensor_copy(kf[:, 1, :], lo[:]))
            link(nc.vector.tensor_tensor(kf[:, 0, :], kf[:, 0, :], kf[:, 1, :], ALU.add))
            nc.vector.tensor_scalar(keys[:, :, 1], kf[:, 0, :], 1.0 / KS, None, ALU.mult).then_inc(keys_made, 1)
            nc.vector.tensor_copy(base_f[:], bases[:])
            link(nc.vector.tensor_copy(coarse[:], dst_s[:].rearrange("p (j c) -> p j c", c=COARSE)[:, :, 0]))
            dve.wait_ge(pool_const, 1)
            J = EJ // COARSE
            link(nc.vector.tensor_tensor(below[:], coarse[:].unsqueeze(1).to_broadcast([P, NS, J]),
                                         thr[:].unsqueeze(2).to_broadcast([P, NS, J]), ALU.is_lt))
            nc.vector.tensor_reduce(below_n[:], below[:], AX.X, ALU.add).then_inc(counted, 1)
            dve.wait_ge(counts_summed, 1)
            link(nc.vector.tensor_scalar(start_f[:], cnt_ps[0:1, 0:NS], -1.0, 0.0, ALU.add, ALU.max))
            link(nc.vector.tensor_scalar(start_f[:], start_f[:], float(COARSE), None, ALU.mult))
            nc.vector.tensor_copy(starts[:], start_f[:])
            nc.vector.tensor_copy(base_bc[:], base_ps[:, 0:NG])

        @block.tensor
        def _(pe):
            pe.wait_ge(counted, 1)
            nc.tensor.matmul(cnt_ps[:, 0:NS], ones[:], below_n[:], start=True, stop=True)
            nc.tensor.matmul(base_ps[:, 0:NG], ones[0:1, :], base_f[:], start=True, stop=True).then_inc(counts_summed, 1)


def layer_norm_stats(nc, dve, link, ln, src, tick):
    for b in range(BATCH):
        last = nc.vector.bn_stats(ln["st"][:, b, :], src[:, b, :])
    link(last)
    settle(dve, tick)
    for b in range(BATCH):
        last = nc.vector.bn_aggr(ln["mv"][:, b, :], ln["st"][:, b, :])
    return last


def row_bc(ap):
    return ap.rearrange("(a d) -> a d", a=1).to_broadcast([P, ap.shape[0]])


def node_features(nc, t, sb, pb, sem, g, ln_batch):
    x_sb, ident, eps, hn_dram, ft_tab = (g[k] for k in ("x_sb", "ident", "eps", "hn_dram", "ft_tab"))
    with ExitStack() as c:
        a, b_ = ln_batch("na", c), ln_batch("nb", c)
        w_att = sb("w_att", [D, HD], F32, c)
        lnw = sb("nf_lnw", [P, D], F32, c)
        lnb = sb("nf_lnb", [P, D], F32, c)
        h = sb("nf_h", [P, BATCH, D], F32, c)
        u = sb("nf_u", [P, BATCH, D], F32, c)
        hn = sb("nf_hn", [P, BATCH, D], F32, c)
        hnT = sb("nf_hnT", [D, BATCH, P], F32, c)
        ft = sb("nf_ft", [P, BATCH, HD], F32, c)
        T_ps = pb("nf_T_ps", [D, 2, 512], F32, c)
        ft_ps = pb("nf_ft_ps", [P, 3, 512], F32, c)
        w_in, var1, sd1, neg1, h_done, var2, sd2, hn_done, hnT_ps, hnT_sb, ft_done, ft_sb, ft_out, vch, hn_out, tick = (
            sem("nf_" + s) for s in ("w_in", "var1", "sd1", "neg1", "h_done", "var2", "sd2", "hn_done", "hnT_ps",
                                     "hnT_sb", "ft_done", "ft_sb", "ft_out", "vch", "hn_out", "tick"))
        block = c.enter_context(nc.Block())

        @block.sync
        def _(sp):
            sp.dma_start(w_att[:], t["L0_gnn_W_att"]).then_inc(w_in, 16)
            sp.dma_start(lnw[:], row_bc(t["L0_gnn_ln1_w"])).then_inc(w_in, 16)
            sp.dma_start(lnb[:], row_bc(t["L0_gnn_ln1_b"])).then_inc(w_in, 16)
            def copy_out(i, first):
                sp.wait_ge(hn_done, i + 1)
                sp.dma_start(hn_dram[ds(i * BW, BW), :].rearrange("(b p) f -> p b f", p=P), hn[:]).then_inc(hn_out, 16)
                sp.wait_ge(ft_sb, i + 1)
                sp.dma_start(ft_tab[ds(i * BW, BW), :].rearrange("(b p) f -> p b f", p=P), ft[:]).then_inc(ft_out, 16)
            rounds(sp, NB, copy_out)
            sp.wait_ge(ft_out, 16 * NB)
            sp.wait_ge(hn_out, 16 * NB)

        @block.vector
        def _(dve):
            PER = 10

            def body(i, first):
                link = Chain(dve, vch, i * PER)
                xb = x_sb[:, ds(i * BATCH, BATCH), :]
                for b in range(BATCH):
                    last = nc.vector.bn_stats(a["st"][:, b, :], x_sb[:, ds(i * BATCH + b, 1), :])
                link(last)
                settle(dve, tick)
                for b in range(BATCH):
                    last = nc.vector.bn_aggr(a["mv"][:, b, :], a["st"][:, b, :])
                last.then_inc(var1, 1)
                dve.wait_ge(sd1, i + 1)
                link(nc.vector.reciprocal(a["rs"][:], a["sd"][:]))
                nc.vector.scalar_tensor_tensor(a["nb"][:], a["mv"][:, :, 0], -1.0, a["rs"][:], ALU.mult, ALU.mult
                                               ).then_inc(neg1, 1)
                dve.wait_ge(h_done, i + 1)
                link(layer_norm_stats(nc, dve, link, b_, h, tick))
                nc.vector.tensor_tensor(u[:], h[:], b_["mv"][:, :, 0:1].to_broadcast([P, BATCH, D]), ALU.subtract
                                        ).then_inc(var2, 1)
                dve.wait_ge(sd2, i + 1)
                dve.wait_ge(var2, i + 1)
                link(nc.vector.reciprocal(b_["rs"][:], b_["sd"][:]))
                link(nc.vector.tensor_tensor(u[:], u[:], b_["rs"][:].unsqueeze(2).to_broadcast([P, BATCH, D]), ALU.mult))
                dve.wait_ge(w_in, 48)
                link(nc.vector.tensor_tensor(u[:], u[:], lnw[:].unsqueeze(1).to_broadcast([P, BATCH, D]), ALU.mult))
                if not first:
                    dve.wait_ge(hn_out, 16 * i)
                nc.vector.tensor_tensor(hn[:], u[:], lnb[:].unsqueeze(1).to_broadcast([P, BATCH, D]), ALU.add
                                        ).then_inc(hn_done, 1)
                dve.wait_ge(hnT_ps, i + 1)
                nc.vector.tensor_copy(hnT[:, 0:4, :].rearrange("f b p -> f (b p)"), T_ps[:, 0, :])
                nc.vector.tensor_copy(hnT[:, 4:7, :].rearrange("f b p -> f (b p)"), T_ps[:, 1, 0:384]).then_inc(hnT_sb, 1)
                dve.wait_ge(hnT_sb, i + 1)
                assert link.n <= PER
                while link.n < PER:
                    link(nc.vector.memset(a["nb"][0:1, 0:1], 0.0))
            rounds(dve, NB, body)

        @block.scalar
        def _(act):
            def body(i, first):
                act.wait_ge(var1, i + 1)
                nc.scalar.activation(a["sd"][:], a["mv"][:, :, 1], ACT.Sqrt, bias=eps[:]).then_inc(sd1, 1)
                act.wait_ge(neg1, i + 1)
                for b in range(BATCH):
                    last = nc.scalar.activation(h[:, b, :], x_sb[:, ds(i * BATCH + b, 1), :], ACT.Relu,
                                                bias=a["nb"][:, b:b + 1], scale=a["rs"][:, b:b + 1])
                last.then_inc(h_done, 1)
                act.wait_ge(var2, i + 1)
                nc.scalar.activation(b_["sd"][:], b_["mv"][:, :, 1], ACT.Sqrt, bias=eps[:]).then_inc(sd2, 1)
                act.wait_ge(ft_done, i + 1)
                if not first:
                    act.wait_ge(ft_out, 16 * i)
                for q, n in ((0, 3), (1, 3), (2, 1)):
                    last = nc.scalar.copy(ft[:, 3 * q:3 * q + n, :].rearrange("p b f -> p (b f)"), ft_ps[:, q, 0:n * HD])
                last.then_inc(ft_sb, 1)
            rounds(act, NB, body)

        @block.tensor
        def _(pe):
            pe.wait_ge(w_in, 48)

            def body(i, first):
                pe.wait_ge(hn_done, i + 1)
                for b in range(BATCH):
                    last = nc.tensor.transpose(T_ps[:, b // 4, (b % 4) * P:(b % 4 + 1) * P], hn[:, b, :], ident[:])
                last.then_inc(hnT_ps, 1)
                pe.wait_ge(hnT_sb, i + 1)
                if not first:
                    pe.wait_ge(ft_sb, i)
                for b in range(BATCH):
                    last = nc.tensor.matmul(ft_ps[:, b // 3, (b % 3) * HD:(b % 3 + 1) * HD], hnT[:, b, :], w_att[:],
                                            start=True, stop=True)
                last.then_inc(ft_done, 1)
            rounds(pe, NB, body)


def scores_and_strips(nc, t, sb, pb, sem, g):
    (dst_pad, src_pad, edge_key, ft_tab, edge_ft, edge_score, adj, starts, bases, base_bc, strip_no, ident_bf) = (
        g[k] for k in ("dst_pad", "src_pad", "edge_key", "ft_tab", "edge_ft", "edge_score", "adj", "starts",
                       "bases", "base_bc", "strip_no", "ident_bf"))
    with ExitStack() as c:
        src_ix = sb("src_ix", [P, UN, GC], I32, c)
        dst_ix = sb("dst_ix", [P, UN, GC], I32, c)
        win = sb("win", [P, UN, HD], F32, c)
        ek = sb("ek", [P, UN, SC, 3], F32, c)
        fts = [sb(f"fts{u}", [P, GC, HD], F32, c) for u in range(UN)]
        rel = sb("rel", [P, 2, GC], BF16, c)
        dist = sb("dist", [P, GE], F32, c)
        ohdT = sb("ohdT", [P, 2, GE], F32, c)
        prod = sb("prod", [P, GC, HD], F32, c)
        score = sb("score", [P, UN, GC * H], F32, c)
        kk = sb("kk", [P, 2, SC], F32, c)
        key_iota = sb("key_iota", [P, STRIP], FP16, c)
        lo_iota = sb("lo_iota", [P, P], FP16, c)
        key_i = sb("key_i", [P, STRIP], F32, c)
        neg_p = sb("neg_p", [P, 1], F32, c)
        ohk = sb("ohk", [P, 2, SC, STRIP], BF16, c)
        ohl = sb("ohl", [P, 2, SC, P], BF16, c)
        strip = sb("strip", [P, 2, STRIP], BF16, c)
        bc_ps = pb("bc_ps", [P, 512], F32, c)
        adj_ps = [pb(f"adj_ps{q}", [P, 512], F32, c) for q in range(4)]
        ftd_ps = [pb(f"ftd_ps{q}", [P, 512], F32, c) for q in range(3)]
        iotas = sem("iotas")
        idx_in = [sem(f"idx_in{u}") for u in range(UN)]
        ek_in = [sem(f"ek_in{u}") for u in range(UN)]
        gathered = [sem(f"gathered{u}") for u in range(UN)]
        fts_out = [sem(f"fts_out{u}") for u in range(UN)]
        score_out = [sem(f"score_out{u}") for u in range(UN)]
        strip_out = [sem(f"strip_out{u}") for u in range(2)]
        rel_made, keys_done, bc_done, dist_done, ohdT_done, ftd_done, prod_done, score_done, adj_done, tail_done, strip_done, kk_done = (
            sem("sc_" + s) for s in ("rel_made", "keys_done", "bc_done", "dist_done", "ohdT_done", "ftd_done",
                                     "prod_done", "score_done", "adj_done", "tail_done", "strip_done", "kk_done"))
        tick_pool, tick_sp = sem("sc_tick_pool"), sem("sc_tick_sp")
        TAILW = STRIP - 3 * 512
        block = c.enter_context(nc.Block())

        def steps(engine, body):
            for u in range(UN):
                body(u, 0, u, True)
            with engine.Fori(1, NG // UN) as j:
                for u in range(UN):
                    body(j * UN + u, j, u, False)

        @block.sync
        def _(sp):
            def body(i, j, u, first):
                start = sp.value_load(starts[0:1, i:i + 1] if first else starts[0:1, ds(i, 1)], min_val=0, max_val=E)
                base = sp.value_load(bases[0:1, i:i + 1] if first else bases[0:1, ds(i, 1)], min_val=0, max_val=NP)
                if not first:
                    sp.wait_ge(gathered[u], 16 * GC * j)
                    settle(sp, tick_sp)
                    sp.wait_ge(ftd_done, i - UN + 1)
                    sp.wait_ge(adj_done, i - UN + 1)
                    settle(sp, tick_sp)
                sp.dma_start(src_ix[:, u, :], src_pad[ds(i * GE, GE)].rearrange("(p c) -> p c", c=GC)
                             ).then_inc(idx_in[u], 16)
                sp.dma_start(dst_ix[:, u, :], dst_pad[ds(i * GE + FRONT, GE)].rearrange("(p c) -> p c", c=GC)
                             ).then_inc(idx_in[u], 16)
                sp.dma_start(win[:, u, :], ft_tab[ds(base, P), :]).then_inc(idx_in[u], 16)
                sp.dma_start(ek[:, u, :, :], edge_key[ds(start, SW), :].rearrange("(p c) k -> p c k", c=SC)
                             ).then_inc(ek_in[u], 16)
            steps(sp, body)
            for u in range(UN):
                sp.wait_ge(fts_out[u], 16 * (NG // UN))
                sp.wait_ge(score_out[u], 16 * (NG // UN))
            for u in range(2):
                sp.wait_ge(strip_out[u], 16 * (NG // 2))

        @block.gpsimd
        def _(pool):
            nc.gpsimd.iota(key_i[:], [[1, STRIP]], base=0, channel_multiplier=0, allow_small_or_imprecise_dtypes=True)
            nc.gpsimd.iota(lo_iota[:], [[1, P]], base=0, channel_multiplier=0, allow_small_or_imprecise_dtypes=True)
            nc.gpsimd.iota(neg_p[:], [[0, 1]], base=0, channel_multiplier=-1, allow_small_or_imprecise_dtypes=True
                           ).then_inc(iotas, 1)

            def body(i, j, u, first):
                if not first:
                    pool.wait_ge(prod_done, i - UN + 1)
                    pool.wait_ge(fts_out[u], 16 * j)
                    pool.wait_ge(idx_in[u], 48 * (j + 1))
                else:
                    pool.wait_ge(idx_in[u], 48)
                settle(pool, tick_pool)
                for k in range(GC):
                    nc.gpsimd.indirect_dma_start(fts[u][:, k, :], None, ft_tab[:, :],
                                                 bass.IndirectOffsetOnAxis(src_ix[:, u, k:k + 1], 0)
                                                 ).then_inc(gathered[u], 16)
            steps(pool, body)

        @block.vector
        def _(dve):
            dve.wait_ge(iotas, 1)
            nc.vector.tensor_scalar(key_iota[:], key_i[:], 1.0 / KS, None, ALU.mult).then_inc(iotas, 1)
            dve.wait_ge(iotas, 2)

            def multiply(i, j, u, first):
                dve.wait_ge(gathered[u], 16 * GC * (j + 1))
                dve.wait_ge(ftd_done, i + 1)
                if not (isinstance(i, int) and i == 0):
                    dve.wait_ge(score_done, i)
                if not first:
                    dve.wait_ge(score_out[u], 16 * j)
                for q, n in ((0, 3), (1, 3), (2, 2)):
                    last = nc.vector.tensor_tensor(prod[:, 3 * q:3 * q + n, :],
                                                   ftd_ps[q][:, 0:n * HD].rearrange("p (b f) -> p b f", f=HD),
                                                   fts[u][:, 3 * q:3 * q + n, :], ALU.mult)
                last.then_inc(prod_done, 1)
                dve.wait_ge(prod_done, i + 1)
                nc.vector.tensor_reduce(score[:, u, :], prod[:].rearrange("p c (h d) -> p (c h) d", d=DH),
                                        AX.X, ALU.add).then_inc(score_done, 1)

            def body(i, j, u, first):
                s = u % 2
                two = first and u < 2
                dve.wait_ge(idx_in[u], 48 * (j + 1))
                if not two:
                    dve.wait_ge(bc_done, 2 * (i - 1))
                nc.vector.tensor_scalar(rel[:, s, :], dst_ix[:, u, :], base_bc[:, i:i + 1] if first else base_bc[:, ds(i, 1)],
                                        None, ALU.subtract).then_inc(rel_made, 1)
                dve.wait_ge(ek_in[u], 16 * (j + 1))
                if not two:
                    dve.wait_ge(adj_done, i - 1)
                nc.vector.scalar_tensor_tensor(kk[:, s, :], ek[:, u, :, 0],
                                               strip_no[:, i:i + 1] if first else strip_no[:, ds(i, 1)],
                                               ek[:, u, :, 1], ALU.not_equal, ALU.add).then_inc(kk_done, 1)
                for k in range(SC):
                    nc.vector.tensor_scalar(ohl[:, s, k, :], lo_iota[:], ek[:, u, k, 2:3], None, ALU.is_equal)
                dve.wait_ge(kk_done, i + 1)
                for k in range(SC):
                    last = nc.vector.tensor_scalar(ohk[:, s, k, :], key_iota[:], kk[:, s, k:k + 1], None, ALU.is_equal)
                last.then_inc(keys_done, 1)
                if first and u == 0:
                    return
                if first:
                    multiply(i - 1, 0, u - 1, True)
                elif u == 0:
                    multiply_prev(i, j)
                else:
                    multiply(i - 1, j, u - 1, False)

            def multiply_prev(i, j):
                dve.wait_ge(gathered[UN - 1], 16 * GC * j)
                dve.wait_ge(ftd_done, i)
                dve.wait_ge(score_done, i - 1)
                dve.wait_ge(score_out[UN - 1], 16 * (j - 1))
                for q, n in ((0, 3), (1, 3), (2, 2)):
                    last = nc.vector.tensor_tensor(prod[:, 3 * q:3 * q + n, :],
                                                   ftd_ps[q][:, 0:n * HD].rearrange("p (b f) -> p b f", f=HD),
                                                   fts[UN - 1][:, 3 * q:3 * q + n, :], ALU.mult)
                last.then_inc(prod_done, 1)
                dve.wait_ge(prod_done, i)
                nc.vector.tensor_reduce(score[:, UN - 1, :], prod[:].rearrange("p c (h d) -> p (c h) d", d=DH),
                                        AX.X, ALU.add).then_inc(score_done, 1)
            steps(dve, body)
            multiply(NG - 1, NG // UN - 1, UN - 1, False)

        @block.scalar
        def _(act):
            act.wait_ge(iotas, 2)

            def copy_scores(i, j, u):
                act.wait_ge(score_done, i + 1)
                act.dma_start(edge_score[ds(i * GE, GE), :].rearrange("(p c) h -> p (c h)", p=P), score[:, u, :]
                              ).then_inc(score_out[u], 16)

            def copy_rows(i, j, u):
                act.wait_ge(gathered[u], 16 * GC * (j + 1))
                act.dma_start(edge_ft[ds(i * GE, GE), :].rearrange("(p c) f -> p (c f)", p=P),
                              fts[u][:].rearrange("p c f -> p (c f)")).then_inc(fts_out[u], 16)

            def body(i, j, u, first):
                s = u % 2
                two = first and u < 2
                if not (first and u == 0):
                    act.wait_ge(ohdT_done, i)
                for a in range(2):
                    act.wait_ge(bc_done, 2 * i + a + 1)
                    nc.scalar.activation(dist[:, a * 512:(a + 1) * 512], bc_ps[:], ACT.Abs, bias=neg_p[:]
                                         ).then_inc(dist_done, 1)
                act.wait_ge(dist_done, 2 * i + 2)
                if not two:
                    act.wait_ge(ftd_done, i - 1)
                nc.scalar.activation(ohdT[:, s, :], dist[:], ACT.Relu, bias=1.0, scale=-1.0).then_inc(ohdT_done, 1)
                if not two:
                    act.wait_ge(strip_out[s], 16 * (j * (UN // 2) + u // 2))
                act.wait_ge(adj_done, i + 1)
                for q in range(3):
                    nc.scalar.copy(strip[:, s, q * 512:(q + 1) * 512], adj_ps[q][:])
                nc.scalar.copy(strip[:, s, 3 * 512:STRIP], adj_ps[3][:, 0:TAILW]).then_inc(strip_done, 1)
                act.wait_ge(strip_done, i + 1)
                act.dma_start(adj[ds(i, 1)].rearrange("a p s -> (a p) s"),
                              strip[:, s, :]).then_inc(strip_out[s], 16)
                copy_rows(i, j, u)
                if first and u == 0:
                    return
                if u == 0:
                    copy_scores(i - 1, j - 1, UN - 1)
                else:
                    copy_scores(i - 1, j, u - 1)
            steps(act, body)
            copy_scores(NG - 1, NG // UN - 1, UN - 1)

        @block.tensor
        def _(pe):
            def body(i, j, u, first):
                s = u % 2
                one = first and u == 0
                pe.wait_ge(rel_made, i + 1)

                def spread(a):
                    if a or not one:
                        pe.wait_ge(dist_done, 2 * i + a)
                    for k in range(4):
                        last = nc.tensor.matmul(bc_ps[:, k * P:(k + 1) * P],
                                                rel[:, s, 4 * a + k:4 * a + k + 1].to_broadcast([P, P]), ident_bf[:],
                                                start=True, stop=True)
                    last.then_inc(bc_done, 1)

                spread(0)
                pe.wait_ge(keys_done, i + 1)
                if not one:
                    pe.wait_ge(strip_done, i)
                for q in range(4):
                    if q == 1:
                        spread(1)
                    for k in range(SC):
                        out_ps = adj_ps[q][:, 0:min(512, STRIP - q * 512)]
                        last = nc.tensor.matmul(out_ps, ohl[:, s, k, :], ohk[:, s, k, q * 512:min(STRIP, (q + 1) * 512)],
                                                start=(k == 0), stop=(k == SC - 1))
                last.then_inc(adj_done, 1)
                pe.wait_ge(ohdT_done, i + 1)
                if not one:
                    pe.wait_ge(prod_done, i)
                pe.wait_ge(idx_in[u], 48 * (j + 1))
                for k in range(GC):
                    last = nc.tensor.matmul(ftd_ps[k // 3][:, (k % 3) * HD:(k % 3 + 1) * HD],
                                            ohdT[:, s, k * P:(k + 1) * P], win[:, u, :], start=True, stop=True)
                last.then_inc(ftd_done, 1)
            steps(pe, body)


def softmax_numerators(nc, t, sb, pb, sem, g):
    dst_pad, edge_score, edge_exp, ident = (g[k] for k in ("dst_pad", "edge_score", "edge_exp", "ident"))
    with ExitStack() as c:
        s_all = sb("sm_s", [P, EJ, H], F32, c)
        f_all = sb("sm_f", [P, EJ, H], F32, c)
        here = sb("sm_here", [P, EJ], I32, c)
        before = sb("sm_before", [P, EJ], I32, c)
        after = sb("sm_after", [P, EJ], I32, c)
        first = sb("sm_first", [P, EJ], F32, c)
        last_ = sb("sm_last", [P, EJ], F32, c)
        ends = sb("sm_ends", [P, 4, H], F32, c)
        flags = sb("sm_flags", [P, 2], F32, c)
        rows = sb("sm_rows", [H, 4, P], F32, c)
        step_ = sb("sm_step", [H, 4, P], F32, c)
        carry = sb("sm_carry", [H, 2, P], F32, c)
        carry_p = sb("sm_carry_p", [P, 2, H], F32, c)
        tr_ps = pb("sm_tr_ps", [H, 512], F32, c)
        back_ps = pb("sm_back_ps", [P, 512], F32, c)
        d_in, s_in, ends_made, rows_ps, carries, back, diff, expd, e_out, vch = (
            sem("sm_" + s) for s in ("d_in", "s_in", "ends_made", "rows_ps", "carries", "back", "diff", "expd",
                                     "e_out", "vch"))
        block = c.enter_context(nc.Block())

        @block.sync
        def _(sp):
            for i, buf in enumerate((here, before, after)):
                off = FRONT + (0, -1, 1)[i]
                sp.dma_start(buf[:], dst_pad[off:off + EP].rearrange("(p j) -> p j", p=P)).then_inc(d_in, 16)
            sp.dma_start(s_all[:].rearrange("p j h -> p (j h)"),
                         edge_score[0:EP, :].rearrange("(p j) h -> p (j h)", p=P)).then_inc(s_in, 16)
            sp.wait_ge(expd, 1)
            sp.dma_start(edge_exp[0:EP, :].rearrange("(p j) h -> p (j h)", p=P),
                         s_all[:].rearrange("p j h -> p (j h)")).then_inc(e_out, 16)
            sp.wait_ge(e_out, 16)

        @block.vector
        def _(dve):
            link = Chain(dve, vch)
            dve.wait_ge(d_in, 48)
            nc.vector.tensor_tensor(first[:], here[:], before[:], ALU.not_equal)
            link(nc.vector.tensor_tensor(last_[:], here[:], after[:], ALU.not_equal))
            link(nc.vector.tensor_tensor(flags[:, 1:2], here[:, 0:1], here[:, EJ - 1:EJ], ALU.not_equal))
            nc.vector.tensor_scalar(flags[:, 0:1], first[:, 0:1], NEG, None, ALU.mult)
            link(nc.vector.tensor_scalar(flags[:, 1:2], flags[:, 1:2], NEG, None, ALU.mult))
            nc.vector.tensor_copy(ends[:, 2, :], flags[:, 0:1].to_broadcast([P, H]))
            nc.vector.tensor_copy(ends[:, 3, :], flags[:, 1:2].to_broadcast([P, H]))
            nc.vector.tensor_scalar(first[:], first[:], NEG, None, ALU.mult)
            link(nc.vector.tensor_scalar(last_[:], last_[:], NEG, None, ALU.mult))
            dve.wait_ge(s_in, 16)

            def scan(out, data, fresh, initial, back):
                if back:
                    out, data, fresh = out[:, ::-1], data[:, ::-1], fresh[:, ::-1]
                return nc.vector.tensor_tensor_scan(out, fresh, data, initial, ALU.add, ALU.max)

            for h in range(H):
                ins = scan(f_all[:, :, h], s_all[:, :, h], first[:], NEG, False)
            link(ins)
            link(nc.vector.tensor_copy(ends[:, 0, :], f_all[:, EJ - 1, :]))
            for h in range(H):
                ins = scan(f_all[:, :, h], s_all[:, :, h], last_[:], NEG, True)
            link(ins)
            nc.vector.tensor_copy(ends[:, 1, :], f_all[:, 0, :]).then_inc(ends_made, 1)
            dve.wait_ge(rows_ps, 1)
            link(nc.vector.tensor_copy(rows[:], tr_ps[:].rearrange("h (k p) -> h k p", k=4)))
            nc.vector.memset(step_[:], NEG)
            link(nc.vector.memset(carry[:], NEG))
            nc.vector.tensor_tensor(step_[:, 0, 1:P], rows[:, 2, 1:P], rows[:, 3, 0:P - 1], ALU.add)
            nc.vector.tensor_tensor(step_[:, 1, 1:P], rows[:, 2, 1:P], rows[:, 0, 0:P - 1], ALU.add)
            nc.vector.tensor_tensor(step_[:, 2, 0:P - 1], rows[:, 2, 1:P], rows[:, 3, 1:P], ALU.add)
            link(nc.vector.tensor_tensor(step_[:, 3, 0:P - 1], rows[:, 2, 1:P], rows[:, 1, 1:P], ALU.add))
            scan(carry[:, 0, :], step_[:, 1, :], step_[:, 0, :], NEG, False)
            scan(carry[:, 1, :], step_[:, 3, :], step_[:, 2, :], NEG, True).then_inc(carries, 1)
            dve.wait_ge(back, 1)
            link(nc.vector.tensor_copy(carry_p[:], back_ps[:, 0:2 * H].rearrange("p (k h) -> p k h", k=2)))
            for h in range(H):
                ins = scan(f_all[:, :, h], s_all[:, :, h], first[:], carry_p[:, 0, h:h + 1], False)
            link(ins)
            for h in range(H):
                ins = scan(f_all[:, :, h], f_all[:, :, h], last_[:], carry_p[:, 1, h:h + 1], True)
            link(ins)
            nc.vector.tensor_tensor(s_all[:], s_all[:], f_all[:], ALU.subtract).then_inc(diff, 1)

        @block.tensor
        def _(pe):
            pe.wait_ge(ends_made, 1)
            for k in range(4):
                ins = nc.tensor.transpose(tr_ps[:, k * P:(k + 1) * P], ends[:, k, :], ident[:])
            ins.then_inc(rows_ps, 1)
            pe.wait_ge(carries, 1)
            for k in range(2):
                ins = nc.tensor.transpose(back_ps[:, k * H:(k + 1) * H], carry[:, k, :], ident[0:H, 0:H])
            ins.then_inc(back, 1)

        @block.scalar
        def _(act):
            act.wait_ge(diff, 1)
            nc.scalar.activation(s_all[:], s_all[:], ACT.Exp, scale=float(DH) ** -0.5).then_inc(expd, 1)


def aggregate(nc, t, sb, pb, sem, g):
    dst_pad, edge_ft, edge_exp, starts, agg_sb, dis_col = (g[k] for k in (
        "dst_pad", "edge_ft", "edge_exp", "starts", "agg_sb", "dis_col"))
    W = HD + H + 1
    with ExitStack() as c:
        rows = sb("ag_rows", [P, 2, TC, HD], F32, c)
        ex = sb("ag_ex", [P, 2, TC, H], F32, c)
        dst = sb("ag_dst", [P, 2, TC], I32, c)
        rel = sb("ag_rel", [P, 2, TC], F32, c)
        terms = sb("ag_terms", [P, 2, TC, W], F32, c)
        oh = sb("ag_oh", [P, TC, P], F32, c)
        iota = sb("ag_iota", [P, P], F32, c)
        tile_no = sb("ag_tile_no", [P, NT], F32, c)
        z = sb("ag_z", [P, H], F32, c)
        sums = sb("ag_sums", [P, W], F32, c)
        deg = sb("ag_deg", [P, NT], F32, c)
        sum_ps = [pb(f"ag_ps{s}", [P, 512], F32, c) for s in range(2)]
        in_ = [sem(f"ag_in{s}") for s in range(2)]
        const, rel_made, terms_dve, terms_pool, oh_done, summed, taken, sq, vch = (
            sem("ag_" + s) for s in ("const", "rel_made", "terms_dve", "terms_pool", "oh_done", "summed", "taken",
                                     "sq", "vch"))
        CP = 10
        block = c.enter_context(nc.Block())

        def steps(engine, body):
            body(0, 0, 0, True)
            body(1, 0, 1, True)
            with engine.Fori(1, NT // 2) as j:
                body(j * 2, j, 0, False)
                body(j * 2 + 1, j, 1, False)
            body(NT - 1, NT // 2, 0, False)

        @block.sync
        def _(sp):
            def body(i, j, s, first):
                at = i * (P // SUB)
                start = sp.value_load(starts[0:1, at:at + 1] if isinstance(at, int) else starts[0:1, ds(at, 1)],
                                      min_val=0, max_val=E)
                if not first:
                    sp.wait_ge(summed, i - 1)
                    sp.wait_ge(terms_pool, i - 1)
                sp.dma_start(dst[:, s, :], dst_pad[ds(start + FRONT, TW)].rearrange("(p c) -> p c", c=TC)
                             ).then_inc(in_[s], 16)
                sp.dma_start(ex[:, s, :, :].rearrange("p c h -> p (c h)"),
                             edge_exp[ds(start, TW), :].rearrange("(p c) h -> p (c h)", c=TC)).then_inc(in_[s], 16)
                sp.dma_start(rows[:, s, :, :].rearrange("p c f -> p (c f)"),
                             edge_ft[ds(start, TW), :].rearrange("(p c) f -> p (c f)", c=TC)).then_inc(in_[s], 16)
            steps(sp, body)

        @block.gpsimd
        def _(pool):
            nc.gpsimd.iota(iota[:], [[1, P]], base=0, channel_multiplier=0, allow_small_or_imprecise_dtypes=True)
            nc.gpsimd.iota(tile_no[:], [[P, NT]], base=0, channel_multiplier=0, allow_small_or_imprecise_dtypes=True)
            nc.gpsimd.memset(terms[:, 0, :, W - 1:W], 1.0)
            nc.gpsimd.memset(terms[:, 1, :, W - 1:W], 1.0).then_inc(const, 1)

            def body(i, j, s, first):
                if not first:
                    pool.wait_ge(summed, i - 1)
                pool.wait_ge(in_[s], 48 * (j + 1))
                nc.gpsimd.tensor_tensor(terms[:, s, 0:CP, 0:HD].rearrange("p c (h d) -> p c h d", d=DH),
                                        rows[:, s, 0:CP, :].rearrange("p c (h d) -> p c h d", d=DH),
                                        ex[:, s, 0:CP, :].unsqueeze(3).to_broadcast([P, CP, H, DH]), ALU.mult
                                        ).then_inc(terms_pool, 1)
            steps(pool, body)

        @block.vector
        def _(dve):
            dve.wait_ge(const, 1)

            def body(i, j, s, first):
                dve.wait_ge(in_[s], 48 * (j + 1))
                if not first:
                    dve.wait_ge(summed, i - 1)
                nc.vector.tensor_scalar(rel[:, s, :], dst[:, s, :],
                                        tile_no[:, i:i + 1] if isinstance(i, int) else tile_no[:, ds(i, 1)],
                                        None, ALU.subtract).then_inc(rel_made, 1)
                nc.vector.tensor_copy(terms[:, s, :, HD:HD + H], ex[:, s, :, :])
                nc.vector.tensor_tensor(terms[:, s, CP:TC, 0:HD].rearrange("p c (h d) -> p c h d", d=DH),
                                        rows[:, s, CP:TC, :].rearrange("p c (h d) -> p c h d", d=DH),
                                        ex[:, s, CP:TC, :].unsqueeze(3).to_broadcast([P, TC - CP, H, DH]), ALU.mult
                                        ).then_inc(terms_dve, 1)
                dve.wait_ge(rel_made, i + 1)
                if not (isinstance(i, int) and i == 0):
                    dve.wait_ge(summed, i)
                nc.vector.tensor_tensor(oh[:], iota[:].unsqueeze(1).to_broadcast([P, TC, P]),
                                        rel[:, s, :].unsqueeze(2).to_broadcast([P, TC, P]), ALU.is_equal
                                        ).then_inc(oh_done, 1)
                dve.wait_ge(summed, i + 1)
                link = Chain(dve, vch, i * 3)
                link(nc.vector.tensor_scalar(z[:], sum_ps[s][:, HD:HD + H], 1e-30, None, ALU.max))
                link(nc.vector.reciprocal(z[:], z[:]))
                nc.vector.tensor_copy(deg[:, i:i + 1] if isinstance(i, int) else deg[:, ds(i, 1)],
                                      sum_ps[s][:, W - 1:W])
                o = agg_sb[:, i:i + 1, :] if isinstance(i, int) else agg_sb[:, ds(i, 1), :]
                link(nc.vector.tensor_tensor(o.rearrange("p a (h d) -> p (a h) d", d=DH),
                                             sum_ps[s][:, 0:HD].rearrange("p (h d) -> p h d", d=DH),
                                             z[:].unsqueeze(2).to_broadcast([P, H, DH]), ALU.mult))
            steps(dve, body)
            dve.wait_ge(sq, 1)
            nc.vector.reciprocal(dis_col[:], deg[:]).then_inc(sq, 1)
            dve.wait_ge(sq, 2)

        @block.scalar
        def _(act):
            act.wait_ge(vch, 3 * NT)
            nc.scalar.activation(deg[:], deg[:], ACT.Sqrt, bias=1.0).then_inc(sq, 1)

        @block.tensor
        def _(pe):
            def body(i, j, s, first):
                pe.wait_ge(terms_dve, i + 1)
                pe.wait_ge(terms_pool, i + 1)
                pe.wait_ge(oh_done, i + 1)
                for k in range(TC):
                    last = nc.tensor.matmul(sum_ps[s][:, 0:W], oh[:, k, :], terms[:, s, k, :],
                                            start=(k == 0), stop=(k == TC - 1))
                last.then_inc(summed, 1)
            steps(pe, body)


def node_update(nc, t, sb, pb, sem, g, ln_batch):
    agg_sb, hn_dram, x_sb, ident, ones, eps, hT_dram = (g[k] for k in (
        "agg_sb", "hn_dram", "x_sb", "ident", "ones", "eps", "hT_dram"))
    F = 4 * D
    BH = BW // 2
    with ExitStack() as c:
        la, lb = ln_batch("ua", c), ln_batch("ub", c)
        hr_w = sb("hr_w", [P, D], F32, c)
        hr_3 = sb("hr_3", [HD - P + 1, D], F32, c)
        in_w = sb("nu_in_w", [P, D], F32, c)
        in_b = sb("nu_in_b", [P, D], F32, c)
        w1 = sb("nu_w1", [D, F], F32, c)
        b1 = sb("nu_b1", [P, 4], F32, c)
        w2 = sb("nu_w2", [P, 4, D], F32, c)
        b2 = sb("nu_b2", [1, D], F32, c)
        low = sb("nu_low", [P, BATCH, HD], F32, c)
        ex = sb("nu_ex", [P, BATCH, HD], F32, c)
        el = sb("nu_el", [P, BATCH, HD + 1], F32, c)
        elT = sb("nu_elT", [P, BATCH, P], F32, c)
        el3T = sb("nu_el3T", [HD - P + 1, BATCH, P], F32, c)
        hn = sb("nu_hn", [P, BATCH, D], F32, c)
        o = sb("nu_o", [P, BATCH, D], F32, c)
        s2 = sb("nu_s2", [P, BATCH, D], F32, c)
        s2T = sb("nu_s2T", [D, BATCH, P], F32, c)
        lowF = sb("nu_lowF", [P, BW], F32, c)
        exF = sb("nu_exF", [P, BW], F32, c)
        reF = sb("nu_reF", [P, BW], F32, c)
        uT = sb("nu_uT", [P, 4, BW], F32, c)
        h = sb("nu_h", [P, BATCH, D], F32, c)
        hT = sb("nu_hT", [D, BATCH, P], F32, c)
        T_ps = pb("nu_T_ps", [P, 2, 512], F32, c)
        T3_ps = pb("nu_T3_ps", [HD - P + 1, 2, 512], F32, c)
        o_ps = pb("nu_o_ps", [P, 2, 512], F32, c)
        up_ps = pb("nu_up_ps", [P, 2, 512], F32, c)
        names = ("w_in", "low", "ex", "el", "elT_ps", "elT", "el3T", "o_ps", "var", "sd", "s2", "s2T_ps", "s2T", "up_ps",
                 "lowF", "exF", "uT", "v_ps", "lowV", "exV", "var2", "sd2", "nb2", "h", "hT_ps", "hT", "hT_out", "vch", "one", "hn_in", "tick", "tick_sp")
        s = {n: sem("nu_" + n) for n in names}
        block = c.enter_context(nc.Block())

        @block.sync
        def _(sp):
            loads = [(hr_w[:], t["L0_gnn_hr_w"][0:P, :]), (hr_3[0:HD - P, :], t["L0_gnn_hr_w"][P:HD, :]),
                     (hr_3[HD - P:HD - P + 1, :], t["L0_gnn_hr_b"].rearrange("(a d) -> a d", a=1)),
                     (in_w[:], row_bc(t["L0_gnn_in_w"])), (in_b[:], row_bc(t["L0_gnn_in_b"])),
                     (w1[:], t["L0_gnn_w1"]), (w2[:], t["L0_gnn_w2"].rearrange("(f p) d -> p f d", p=P)),
                     (b2[:], t["L0_gnn_b2"].rearrange("(a d) -> a d", a=1))]
            for dst, src in loads:
                sp.dma_start(dst, src).then_inc(s["w_in"], 16)
            with nc.allow_non_contiguous_dma(reason="a bias, one value per partition"):
                sp.dma_start(b1[:], t["L0_gnn_b1"].rearrange("(f p) -> p f", p=P)).then_inc(s["w_in"], 16)
            def body(i, first):
                if not first:
                    sp.wait_ge(s["var"], i)
                    settle(sp, s["tick_sp"])
                sp.dma_start(hn[:], hn_dram[ds(i * BW, BW), :].rearrange("(b p) f -> p b f", p=P)).then_inc(s["hn_in"], 16)
                sp.wait_ge(s["hT"], i + 1)
                settle(sp, s["tick_sp"])
                sp.dma_start(hT_dram[:, ds(i * BW, BW)], hT[:].rearrange("f b p -> f (b p)")).then_inc(s["hT_out"], 16)
            rounds(sp, NB, body)
            sp.wait_ge(s["hT_out"], 16 * NB)

        W_ALL = 9 * 16

        @block.vector
        def _(dve):
            nc.vector.memset(el[:, :, HD:HD + 1], 1.0).then_inc(s["one"], 1)
            dve.wait_ge(s["one"], 1)
            dve.wait_ge(s["w_in"], W_ALL)
            PER = 19

            def norm(link, ln, src, dst, w, b):
                wide = [P, BATCH, D]
                link(nc.vector.reciprocal(ln["rs"][:], ln["sd"][:]))
                link(nc.vector.tensor_tensor(src[:], src[:], ln["rs"][:].unsqueeze(2).to_broadcast(wide), ALU.mult))
                link(nc.vector.tensor_tensor(src[:], src[:], w[:].unsqueeze(1).to_broadcast(wide), ALU.mult))
                return nc.vector.tensor_tensor(dst[:], src[:], b[:].unsqueeze(1).to_broadcast(wide), ALU.add)

            def body(i, first):
                link = Chain(dve, s["vch"], i * PER)
                agg = agg_sb[:, ds(i * BATCH, BATCH), :]
                xb = x_sb[:, ds(i * BATCH, BATCH), :]
                nc.vector.tensor_scalar(low[:], agg, 0.0, None, ALU.min).then_inc(s["low"], 1)
                dve.wait_ge(s["ex"], i + 1)
                nc.vector.scalar_tensor_tensor(el[:, :, 0:HD], ex[:], -1.0, agg, ALU.add, ALU.max).then_inc(s["el"], 1)
                dve.wait_ge(s["elT_ps"], i + 1)
                nc.vector.tensor_copy(el3T[:, 0:4, :].rearrange("f b p -> f (b p)"), T3_ps[:, 0, :])
                nc.vector.tensor_copy(el3T[:, 4:7, :].rearrange("f b p -> f (b p)"), T3_ps[:, 1, 0:384]
                                      ).then_inc(s["el3T"], 1)
                dve.wait_ge(s["hn_in"], 16 * (i + 1))
                dve.wait_ge(s["o_ps"], 2 * i + 1)
                nc.vector.tensor_tensor(o[:, 0:4, :], o_ps[:, 0, :].rearrange("p (b d) -> p b d", d=D),
                                        hn[:, 0:4, :], ALU.add)
                link(nc.vector.tensor_tensor(o[:, 4:7, :], o_ps[:, 1, 0:384].rearrange("p (b d) -> p b d", d=D),
                                             hn[:, 4:7, :], ALU.add))
                link(layer_norm_stats(nc, dve, link, la, o, s["tick"]))
                nc.vector.tensor_tensor(o[:], o[:], la["mv"][:, :, 0:1].to_broadcast([P, BATCH, D]), ALU.subtract
                                        ).then_inc(s["var"], 1)
                dve.wait_ge(s["var"], i + 1)
                dve.wait_ge(s["sd"], i + 1)
                norm(link, la, o, s2, in_w, in_b).then_inc(s["s2"], 1)
                for f in range(4):
                    dve.wait_ge(s["up_ps"], 4 * i + f + 1)
                    nc.vector.tensor_scalar(lowF[:].rearrange("p (a b) -> p a b", a=2), up_ps[:, :, 0:BH],
                                            b1[:, f:f + 1], 0.0, ALU.add, ALU.min).then_inc(s["lowF"], 1)
                    dve.wait_ge(s["exF"], 4 * i + f + 1)
                    nc.vector.scalar_tensor_tensor(uT[:, f, :], exF[:], -1.0, reF[:], ALU.add, ALU.add
                                                   ).then_inc(s["uT"], 1)
                dve.wait_ge(s["v_ps"], i + 1)
                dve.wait_ge(s["uT"], 4 * i + 4)
                nc.vector.tensor_scalar(lowF[:, 0:512], o_ps[:, 0, :], 0.0, None, ALU.min)
                nc.vector.tensor_scalar(lowF[:, 512:BW], o_ps[:, 1, 0:384], 0.0, None, ALU.min).then_inc(s["lowV"], 1)
                dve.wait_ge(s["exV"], i + 1)
                flat = lambda a: a[:].rearrange("p b d -> p (b d)")
                link(nc.vector.scalar_tensor_tensor(flat(o), exF[:], -1.0, reF[:], ALU.add, ALU.add))
                link(nc.vector.tensor_tensor(o[:], o[:], s2[:], ALU.add))
                link(nc.vector.tensor_tensor(o[:], o[:], xb, ALU.add))
                settle(dve, s["tick"])
                nc.vector.tensor_copy(xb, o[:])
                link(layer_norm_stats(nc, dve, link, lb, o, s["tick"]))
                nc.vector.tensor_copy(lb["nb"][:], lb["mv"][:, :, 0]).then_inc(s["var2"], 1)
                dve.wait_ge(s["sd2"], i + 1)
                dve.wait_ge(s["var2"], i + 1)
                link(nc.vector.reciprocal(lb["rs"][:], lb["sd"][:]))
                nc.vector.scalar_tensor_tensor(lb["nb"][:], lb["nb"][:], -1.0, lb["rs"][:], ALU.mult, ALU.mult
                                               ).then_inc(s["nb2"], 1)
                dve.wait_ge(s["h"], i + 1)
                assert link.n <= PER, link.n
                while link.n < PER:
                    link(nc.vector.memset(lb["st"][0:1, 0, 0:1], 0.0))
            rounds(dve, NB, body)

        @block.scalar
        def _(act):
            act.wait_ge(s["w_in"], W_ALL)
            def body(i, first):
                act.wait_ge(s["low"], i + 1)
                nc.scalar.activation(ex[:], low[:], ACT.Exp).then_inc(s["ex"], 1)
                act.wait_ge(s["elT_ps"], i + 1)
                nc.scalar.copy(elT[:, 0:4, :].rearrange("f b p -> f (b p)"), T_ps[:, 0, :])
                nc.scalar.copy(elT[:, 4:7, :].rearrange("f b p -> f (b p)"), T_ps[:, 1, 0:384]).then_inc(s["elT"], 1)
                act.wait_ge(s["var"], i + 1)
                nc.scalar.activation(la["sd"][:], la["mv"][:, :, 1], ACT.Sqrt, bias=eps[:]).then_inc(s["sd"], 1)
                act.wait_ge(s["s2T_ps"], i + 1)
                nc.scalar.copy(s2T[:, 0:4, :].rearrange("f b p -> f (b p)"), T_ps[:, 0, :])
                nc.scalar.copy(s2T[:, 4:7, :].rearrange("f b p -> f (b p)"), T_ps[:, 1, 0:384]).then_inc(s["s2T"], 1)
                for f in range(4):
                    act.wait_ge(s["lowF"], 4 * i + f + 1)
                    if f:
                        act.wait_ge(s["uT"], 4 * i + f)
                    nc.scalar.activation(reF[:].rearrange("p (a b) -> p a b", a=2), up_ps[:, :, 0:BH], ACT.Relu,
                                         bias=b1[:, f:f + 1])
                    nc.scalar.activation(exF[:], lowF[:], ACT.Exp).then_inc(s["exF"], 1)
                act.wait_ge(s["uT"], 4 * i + 4)
                act.wait_ge(s["lowV"], i + 1)
                nc.scalar.activation(reF[:, 0:512], o_ps[:, 0, :], ACT.Relu)
                nc.scalar.activation(reF[:, 512:BW], o_ps[:, 1, 0:384], ACT.Relu)
                nc.scalar.activation(exF[:], lowF[:], ACT.Exp).then_inc(s["exV"], 1)
                act.wait_ge(s["var2"], i + 1)
                nc.scalar.activation(lb["sd"][:], lb["mv"][:, :, 1], ACT.Sqrt, bias=eps[:]).then_inc(s["sd2"], 1)
                act.wait_ge(s["nb2"], i + 1)
                for b in range(BATCH):
                    last = nc.scalar.activation(h[:, b, :], o[:, b, :], ACT.Relu, bias=lb["nb"][:, b:b + 1],
                                                scale=lb["rs"][:, b:b + 1])
                last.then_inc(s["h"], 1)
                act.wait_ge(s["hT_ps"], i + 1)
                if not first:
                    act.wait_ge(s["hT_out"], 16 * i)
                nc.scalar.copy(hT[:, 0:4, :].rearrange("f b p -> f (b p)"), T_ps[:, 0, :])
                nc.scalar.copy(hT[:, 4:7, :].rearrange("f b p -> f (b p)"), T_ps[:, 1, 0:384]).then_inc(s["hT"], 1)
            rounds(act, NB, body)

        @block.tensor
        def _(pe):
            def turn(src):
                for b in range(BATCH):
                    last = nc.tensor.transpose(T_ps[:, b // 4, (b % 4) * P:(b % 4 + 1) * P], src[:, b, 0:P], ident[:])
                return last

            pe.wait_ge(s["w_in"], W_ALL)
            def body(i, first):
                pe.wait_ge(s["el"], i + 1)
                if not first:
                    pe.wait_ge(s["hT"], i)
                turn(el)
                for b in range(BATCH):
                    last = nc.tensor.transpose(T3_ps[:, b // 4, (b % 4) * P:(b % 4 + 1) * P], el[:, b, P:HD + 1],
                                               ident[:])
                last.then_inc(s["elT_ps"], 1)
                pe.wait_ge(s["elT"], i + 1)
                pe.wait_ge(s["el3T"], i + 1)
                for b in range(BATCH):
                    at = o_ps[:, b // 4, (b % 4) * P:(b % 4 + 1) * P]
                    nc.tensor.matmul(at, elT[:, b, :], hr_w[:], start=True, stop=False)
                    last = nc.tensor.matmul(at, el3T[:, b, :], hr_3[:], start=False, stop=True)
                last.then_inc(s["o_ps"], 1)
                pe.wait_ge(s["s2"], i + 1)
                turn(s2).then_inc(s["s2T_ps"], 1)
                pe.wait_ge(s["s2T"], i + 1)
                for f in range(4):
                    if f or not first:
                        pe.wait_ge(s["exF"], 4 * i + f)
                    for a in range(2):
                        last = nc.tensor.matmul(up_ps[:, a, 0:BH], w1[:, f * P:(f + 1) * P],
                                                s2T[:].rearrange("f b p -> f (b p)")[:, a * BH:(a + 1) * BH],
                                                start=True, stop=True)
                    last.then_inc(s["up_ps"], 1)
                pe.wait_ge(s["uT"], 4 * i + 4)
                for b in range(BATCH):
                    at = o_ps[:, b // 4, (b % 4) * P:(b % 4 + 1) * P]
                    for f in range(4):
                        nc.tensor.matmul(at, uT[:, f, b * P:(b + 1) * P], w2[:, f, :], start=(f == 0), stop=False)
                    last = nc.tensor.matmul(at, ones[0:1, :], b2[:], start=False, stop=True)
                last.then_inc(s["v_ps"], 1)
                nc.tensor.nop().then_inc(s["o_ps"], 1)
                pe.wait_ge(s["h"], i + 1)
                turn(h).then_inc(s["hT_ps"], 1)
            rounds(pe, NB, body)


def convolutions(nc, t, sb, pb, sem, g):
    adj, x_sb, ident, ident_bf, dis_col, eps, hT_dram, out = (g[k] for k in (
        "adj", "x_sb", "ident", "ident_bf", "dis_col", "eps", "hT_dram", "out"))
    L = 4
    BIG = 3.0e38
    with ExitStack() as c:
        hT = sb("cv_hT", [D, NP], F32, c)
        parts = sb("cv_parts", [P, NT, 3, D], BF16, c)
        cnt = [sb(f"cv_cnt{q}", [P, SPG, CMAX * SUB], BF16, c) for q in range(3)]
        dis_row = sb("cv_dis_row", [P, NP], F32, c)
        W = sb("cv_W", [D, L, D], F32, c)
        bias = sb("cv_bias", [D, L], F32, c)
        gam = sb("cv_gam", [D, L], F32, c)
        bet = sb("cv_bet", [D, L], F32, c)
        isbn = sb("cv_isbn", [D, L], F32, c)
        notbn = sb("cv_notbn", [D, L], F32, c)
        floor = sb("cv_floor", [D, L], F32, c)
        stage = sb("cv_stage", [D, BATCH, P], F32, c)
        dis7 = sb("cv_dis7", [P, BATCH], F32, c)
        hs = sb("cv_hs", [P, BATCH, D], F32, c)
        res = sb("cv_res", [P, BATCH, D], F32, c)
        y = sb("cv_y", [D, GRP], F32, c)
        stats = sb("cv_stats", [D, NGR + 1, 6], F32, c)
        mv = sb("cv_mv", [D, 2], F32, c)
        sd = sb("cv_sd", [D, 1], F32, c)
        scale = sb("cv_scale", [D, 1], F32, c)
        shift = sb("cv_shift", [D, 1], F32, c)
        tmp = sb("cv_tmp", [D, 1], F32, c)
        w_ps = pb("cv_w_ps", [P, 2, 512], F32, c)
        acc = [pb(f"cv_acc{s}", [D, GRP], F32, c) for s in range(2)]
        names = ("w_in", "par_in", "const", "dis7", "row_ps", "row", "staged", "floored", "w_ps", "hs", "split", "acc",
                 "y", "vch", "dch", "var", "sd", "ready", "out_ps", "sum", "out", "tick", "tick_pe")
        s = {n: sem("cv_" + n) for n in names}
        cnt_in = [sem(f"cv_cnt_in{q}") for q in range(3)]
        acc_read = [sem(f"cv_acc_read{u}") for u in range(2)]
        uses = (NGR // 2 + 1, NGR // 2)
        cnt_used = [sem(f"cv_cnt_used{q}") for q in range(3)]
        PAR = 13
        NGA = NGR + 1
        LW = NP - NGR * GRP
        block = c.enter_context(nc.Block())


        @block.sync
        def _(sp):
            sp.dma_start(hT[:], hT_dram).then_inc(s["w_in"], 16)
            for l, name in enumerate(("W1", "W2", "W3", "W3")):
                sp.dma_start(W[:, l, :], t["L1_gnn_" + name]).then_inc(s["par_in"], 16)
            with nc.allow_non_contiguous_dma(reason="vectors, one value per partition"):
                col = lambda n: t["L1_gnn_" + n].rearrange("(d a) -> d a", a=1)
                for l, name in enumerate(("b1", "b2", "b3", "b3")):
                    sp.dma_start(bias[:, l:l + 1], col(name)).then_inc(s["par_in"], 16)
                for l in range(2):
                    sp.dma_start(gam[:, l:l + 1], col(f"g{l + 1}")).then_inc(s["par_in"], 16)
                    sp.dma_start(bet[:, l:l + 1], col(f"be{l + 1}")).then_inc(s["par_in"], 16)
            with sp.Fori(0, L) as l:
                with sp.Fori(0, NGR) as i:
                    for q, (b0, n) in enumerate(CHUNKS):
                        sp.wait_ge(cnt_used[q], l * NGA + i + 1)
                        sp.dma_start(cnt[q][:, :, 0:n * SUB], adj[ds(i * SPG, SPG), :, b0 * SUB:(b0 + n) * SUB]
                                     .rearrange("t p s -> p t s")).then_inc(cnt_in[q], 16)
                for q, (b0, n) in enumerate(CHUNKS):
                    sp.wait_ge(cnt_used[q], l * NGA + NGR + 1)
                    sp.dma_start(cnt[q][:, 0:LW // SUB, 0:n * SUB], adj[NGR * SPG:NS, :, b0 * SUB:(b0 + n) * SUB]
                                 .rearrange("t p s -> p t s")).then_inc(cnt_in[q], 16)
            with sp.Fori(0, NB - 1) as k:
                sp.wait_ge(s["sum"], k + 1)
                sp.dma_start(out[ds(k * BW, BW), :].rearrange("(b p) d -> p b d", p=P), res[:]).then_inc(s["out"], 16)
            sp.wait_ge(s["sum"], NB)
            sp.dma_start(out[(NB - 1) * BW:(NT - 1) * P, :].rearrange("(b p) d -> p b d", p=P), res[:, 0:BATCH - 1, :]
                         ).then_inc(s["out"], 16)
            sp.dma_start(out[(NT - 1) * P:N, :], res[0:N_LAST, BATCH - 1, :]).then_inc(s["out"], 16)
            sp.wait_ge(s["out"], 16 * (NB + 1))

        @block.vector
        def _(dve):
            for u in range(2):
                dve.sem_inc(acc_read[u], 1)
            for n in ("ready", "split"):
                dve.sem_inc(s[n], 1)
            link = Chain(dve, s["const"])
            nc.vector.memset(isbn[:, 0:2], 1.0)
            nc.vector.memset(isbn[:, 2:L], 0.0)
            nc.vector.memset(notbn[:, 0:2], 0.0)
            nc.vector.memset(notbn[:, 2:L], 1.0)
            nc.vector.memset(gam[:, 2:L], 0.0)
            nc.vector.memset(bet[:, 2:L], 0.0)
            nc.vector.memset(floor[:, 0:1], -BIG)
            nc.vector.memset(floor[:, 1:L], 0.0)
            nc.vector.memset(shift[:], 0.0)
            link(nc.vector.memset(scale[:], 1.0))
            def columns(k, first):
                if not first:
                    dve.wait_ge(s["row_ps"], k)
                    settle(dve, s["tick"])
                nc.vector.tensor_copy(dis7[:], dis_col[:, ds(k * BATCH, BATCH)]).then_inc(s["dis7"], 1)
            rounds(dve, NB, columns)
            dve.wait_ge(s["par_in"], 16 * 12)
            dve.wait_ge(s["row"], NB)
            PER = 4
            with dve.Fori(0, L) as l:
                with dve.Fori(0, NB) as k:
                    n = l * NB + k
                    ch = Chain(dve, s["vch"], n * PER)
                    dve.wait_ge(s["staged"], n + 1)
                    nc.vector.tensor_scalar(stage[:], stage[:], floor[:, ds(l, 1)], None, ALU.max
                                            ).then_inc(s["floored"], 1)
                    dve.wait_ge(s["hs"], n + 2)
                    part = lambda q: parts[:, ds(k * BATCH, BATCH), q, :]
                    ch(nc.vector.tensor_copy(part(0), hs[:]))
                    ch(nc.vector.tensor_tensor(res[:], hs[:], part(0), ALU.subtract))
                    ch(nc.vector.tensor_copy(part(1), res[:]))
                    ch(nc.vector.tensor_tensor(res[:], res[:], part(1), ALU.subtract))
                    nc.vector.tensor_copy(part(2), res[:]).then_inc(s["split"], 1)
                    dve.wait_ge(s["split"], n + 2)

                def finish_group(n, u, use, at, width, real, stat):
                    dve.wait_ge(s["acc"], n + 1)
                    nc.vector.tensor_tensor(y[:, 0:width], acc[u][:, 0:width], dis_row[:, at], ALU.mult
                                            ).then_inc(acc_read[u], 1)
                    dve.wait_ge(acc_read[u], use + 2)
                    ch = Chain(dve, s["dch"], n)
                    ch(nc.vector.tensor_scalar(hT[:, at], y[:, 0:width], bias[:, ds(l, 1)], None, ALU.add))
                    return nc.vector.bn_stats(stat, hT[:, real])

                with dve.Fori(0, NGR // 2) as j:
                    for u in range(2):
                        i = j * 2 + u
                        at = ds(i * GRP, GRP)
                        finish_group(l * NGA + i, u, l * uses[u] + j, at, GRP, at, stats[:, ds(i, 1), :])
                finish_group(l * NGA + NGR, 0, l * uses[0] + NGR // 2, slice(NGR * GRP, NP), LW, slice(NGR * GRP, N),
                             stats[:, NGR:NGR + 1, :]).then_inc(s["y"], 1)
                dve.wait_ge(s["y"], l * 7 + 1)
                ch = Chain(dve, s["y"], l * 7 + 1)
                settle(dve, s["tick"])
                ch(nc.vector.bn_aggr(mv[:], stats[:].rearrange("d a b -> d (a b)")))
                nc.vector.tensor_copy(tmp[:], mv[:, 0:1]).then_inc(s["var"], 1)
                dve.wait_ge(s["var"], l + 1)
                dve.wait_ge(s["sd"], l + 1)
                ch(nc.vector.reciprocal(sd[:], sd[:]))
                ch(nc.vector.tensor_tensor(sd[:], sd[:], gam[:, ds(l, 1)], ALU.mult))
                ch(nc.vector.scalar_tensor_tensor(tmp[:], tmp[:], -1.0, sd[:], ALU.mult, ALU.mult))
                ch(nc.vector.tensor_tensor(tmp[:], tmp[:], bet[:, ds(l, 1)], ALU.add))
                ch(nc.vector.tensor_tensor(shift[:], tmp[:], isbn[:, ds(l, 1)], ALU.mult))
                nc.vector.scalar_tensor_tensor(scale[:], sd[:], isbn[:, ds(l, 1)], notbn[:, ds(l, 1)],
                                               ALU.mult, ALU.add).then_inc(s["ready"], 1)
            def add(k, first):
                dve.wait_ge(s["out_ps"], k + 2)
                if not first:
                    dve.wait_ge(s["out"], 16 * k)
                nc.vector.tensor_tensor(res[:, 0:4, :], x_sb[:, ds(k * BATCH, 4), :],
                                        w_ps[:, 0, :].rearrange("p (b d) -> p b d", d=D), ALU.add)
                nc.vector.tensor_tensor(res[:, 4:7, :], x_sb[:, ds(k * BATCH + 4, 3), :],
                                        w_ps[:, 1, 0:384].rearrange("p (b d) -> p b d", d=D), ALU.add
                                        ).then_inc(s["sum"], 1)
            rounds(dve, NB, add)

        @block.scalar
        def _(act):
            with act.Fori(0, NB) as k:
                act.wait_ge(s["row_ps"], k + 1)
                nc.scalar.copy(dis_row[:, ds(k * BW, 512)], w_ps[:, 0, :])
                nc.scalar.copy(dis_row[:, ds(k * BW + 512, BW - 512)], w_ps[:, 1, 0:384]).then_inc(s["row"], 1)
            act.wait_ge(s["w_in"], 16)
            act.wait_ge(s["const"], 1)
            with act.Fori(0, L) as l:
                act.wait_ge(s["ready"], l + 1)
                with act.Fori(0, NB) as k:
                    n = l * NB + k
                    act.wait_ge(s["w_ps"], n + 1)
                    nc.scalar.activation(stage[:].rearrange("f b p -> f (b p)"), hT[:, ds(k * BW, BW)], ACT.Identity,
                                         bias=shift[:], scale=scale[:]).then_inc(s["staged"], 1)
                    act.wait_ge(s["w_ps"], n + 2)
                    act.wait_ge(s["split"], n + 1)
                    for b in range(BATCH):
                        last = nc.scalar.activation(hs[:, b, :], w_ps[:, b // 4, (b % 4) * D:(b % 4 + 1) * D],
                                                    ACT.Copy, scale=dis_col[:, ds(k * BATCH + b, 1)])
                    last.then_inc(s["hs"], 1)
                act.wait_ge(s["y"], l * 7 + 2)
                act.wait_ge(s["var"], l + 1)
                nc.scalar.activation(sd[:], mv[:, 1:2], ACT.Sqrt, bias=eps[:]).then_inc(s["sd"], 1)
            act.wait_ge(s["ready"], L + 1)
            act.sem_inc(s["out_ps"], 1)
            with act.Fori(0, NB) as k:
                act.wait_ge(s["out_ps"], k + 1)
                nc.scalar.copy(stage[:].rearrange("f b p -> f (b p)"), hT[:, ds(k * BW, BW)]).then_inc(s["staged"], 1)

        @block.tensor
        def _(pe):
            for q in range(3):
                pe.sem_inc(cnt_used[q], 1)
            pe.sem_inc(s["w_ps"], 1)

            def row(k, first):
                pe.wait_ge(s["dis7"], k + 1)
                if not first:
                    pe.wait_ge(s["row"], k)
                for b in range(BATCH):
                    last = nc.tensor.matmul(w_ps[:, b // 4, (b % 4) * P:(b % 4 + 1) * P],
                                            dis7[:, b:b + 1].to_broadcast([P, P]), ident[:], start=True, stop=True)
                last.then_inc(s["row_ps"], 1)
            rounds(pe, NB, row)
            pe.wait_ge(s["row"], NB)
            pe.wait_ge(s["par_in"], 16 * 12)

            def group(l, n, a, tile0, width):
                for q, (b0, m) in enumerate(CHUNKS):
                    pe.wait_ge(cnt_in[q], (n + 1) * 16)
                    for b in range(b0, b0 + m):
                        for r in range(3):
                            last = nc.tensor.matmul(a[:, 0:width], parts[:, b, r, :],
                                                    cnt[q][:, 0:width // SUB, (b - b0) * SUB:(b - b0 + 1) * SUB],
                                                    start=(b == 0 and r == 0), stop=False)
                    last.then_inc(cnt_used[q], 1)
                for b in range(width // P):
                    for r in range(3):
                        w = parts[:, ds(tile0 + b, 1), r, :].rearrange("p a d -> p (a d)")
                        last = nc.tensor.matmul(a[:, b * P:(b + 1) * P], w, ident_bf[:], start=False,
                                                stop=(b == width // P - 1 and r == 2))
                last.then_inc(s["acc"], 1)

            pe.sem_inc(s["hs"], 1)
            with pe.Fori(0, L) as l:
                with pe.Fori(0, NB) as k:
                    n = l * NB + k
                    pe.wait_ge(s["floored"], n + 1)
                    pe.wait_ge(s["hs"], n + 1)
                    for b in range(BATCH):
                        last = nc.tensor.matmul(w_ps[:, b // 4, (b % 4) * D:(b % 4 + 1) * D], stage[:, b, :],
                                                W[:, ds(l, 1), :].rearrange("f a d -> f (a d)"), start=True, stop=True)
                    last.then_inc(s["w_ps"], 1)
                pe.wait_ge(s["split"], (l + 1) * NB + 1)
                settle(pe, s["tick_pe"])
                with pe.Fori(0, NGR // 2) as j:
                    for u in range(2):
                        i = j * 2 + u
                        n = l * NGA + i
                        pe.wait_ge(acc_read[u], l * uses[u] + j + 1)
                        group(l, n, acc[u], i * (GRP // P), GRP)
                pe.wait_ge(acc_read[0], l * uses[0] + NGR // 2 + 1)
                group(l, l * NGA + NGR, acc[0], NGR * (GRP // P), LW)

            def turn(k, first):
                pe.wait_ge(s["staged"], L * NB + k + 1)
                if not first:
                    pe.wait_ge(s["sum"], k)
                for b in range(BATCH):
                    last = nc.tensor.transpose(w_ps[:, b // 4, (b % 4) * P:(b % 4 + 1) * P], stage[:, b, :], ident[:])
                last.then_inc(s["out_ps"], 1)
            rounds(pe, NB, turn)


_INS = ['x', 'src', 'dst', 'L0_gnn_ln1_w', 'L0_gnn_ln1_b', 'L0_gnn_W_att', 'L0_gnn_hr_w', 'L0_gnn_hr_b',
        'L0_gnn_in_w', 'L0_gnn_in_b', 'L0_gnn_w1', 'L0_gnn_b1', 'L0_gnn_w2', 'L0_gnn_b2', 'L1_gnn_W1', 'L1_gnn_b1',
        'L1_gnn_g1', 'L1_gnn_be1', 'L1_gnn_W2', 'L1_gnn_b2', 'L1_gnn_g2', 'L1_gnn_be2', 'L1_gnn_W3', 'L1_gnn_b3']


def kernel(**inputs):
    import numpy as _np
    import concourse.bacc as _bacc
    from concourse import mybir as _mybir
    from concourse.bass_utils import run_bass_kernel_spmd as _run

    nc = _bacc.Bacc("TRN2", target_bir_lowering=False, num_devices=1)
    arrays, aps = {}, {}
    for name in _INS:
        a = _np.ascontiguousarray(inputs[name])
        arrays[f"in_{name}"] = a
        aps[name] = nc.dram_tensor(f"in_{name}", a.shape, _mybir.dt.from_np(a.dtype), kind="ExternalInput").ap()
    aps["out"] = nc.dram_tensor("out_0", (6250, 128), _mybir.dt.float32, kind="ExternalOutput").ap()
    gnn_program(nc, aps)
    r = _run(nc, [arrays], core_ids=[0])
    return r.results[0]["out_0"]
```

```python
import concourse.bass as bass
from concourse import mybir
from concourse.alu_op_type import AluOpType as ALU
from contextlib import ExitStack

F32 = mybir.dt.float32
BF16 = mybir.dt.bfloat16
FP16 = mybir.dt.float16
I32 = mybir.dt.int32
ACT = mybir.ActivationFunctionType
AX = mybir.AxisListType
ds = bass.ds

P = 128
D = 128
N = 6250
E = 200000
NT = -(-N // P)
NP = NT * P
N_LAST = N - (NT - 1) * P
H, DH = 10, 13
HD = H * DH
BATCH = 7
NB = NT // BATCH
BW = BATCH * D

GC = 8
GE = GC * P
NG = -(-E // GE)
EP = NG * GE
EJ = EP // P

SUB = 32
NS = NP // SUB
HALF = SUB // 2
NH = NP // HALF
SC = 6
SW = SC * P
STRIP = NT * SUB
KEYS = NT * HALF
TC = 35
TW = TC * P
COARSE = 56
FRONT = 16
EX = -(-(E + TW) // (16 * P)) * 16 * P
EXJ = EX // P
KS = 1024.0
NOWHERE = NP
TAB = NP + P
NEG = -1.0e38
EPS = 1e-5
FORCE_GENERAL = 0.5
UN = 4
GRP = 512
NGR = NP // GRP
SPG = GRP // SUB
CHUNKS = [(0, 16), (16, 16), (32, 17)]
CMAX = 17


def gnn_program(nc, t):
    out = t["out"]
    dram = lambda name, shape, dt: nc.dram_tensor(name, shape, dt).ap()
    dst_pad = dram("dst_pad", (FRONT + EX + FRONT,), I32)
    src_pad = dram("src_pad", (EX,), I32)
    edge_key = dram("edge_key", (EX, 3), F32)
    ft_tab = dram("ft_tab", (TAB, HD), F32)
    edge_ft = dram("edge_ft", (EX, HD), F32)
    edge_score = dram("edge_score", (EX, H), F32)
    edge_exp = dram("edge_exp", (EX, H), F32)
    adj = dram("adj", (NS, P, STRIP), BF16)
    max_tab = dram("max_tab", (TAB, H), F32)
    parts_tab = dram("parts_tab", (NP, 3 * D), BF16)
    hn_dram = dram("hn_dram", (NP, D), F32)

    top = ExitStack()
    with top:
        def sb(name, shape, dt, on=top):
            return on.enter_context(nc.sbuf_tensor(name, shape, dt))

        def pb(name, shape, dt, on):
            return on.enter_context(nc.psum_tensor(name, shape, dt))

        held = []

        def sem(name):
            held.append(nc.alloc_semaphore(name))
            return held[-1]

        def stage_over():
            nc.clear_and_free_semaphores(list(held))
            nc.all_engine_barrier()
            held.clear()

        x_sb = sb("x_sb", [P, NT, D], F32)
        ident = sb("ident", [P, P], F32)
        ident_bf = sb("ident_bf", [P, P], BF16)
        ones = sb("ones", [P, P], F32)
        eps = sb("eps", [P, 1], F32)
        starts = sb("starts", [1, NH], I32)
        bases = sb("bases", [1, NG], I32)
        base_bc = sb("base_bc", [P, NG], F32)
        strip_no = sb("strip_no", [P, NH], F32)
        dis_col = sb("dis_col", [P, NT], F32)

        def ln_batch(nm, on):
            return dict(st=sb(nm + "_st", [P, BATCH, 6], F32, on), mv=sb(nm + "_mv", [P, BATCH, 2], F32, on),
                        sd=sb(nm + "_sd", [P, BATCH], F32, on), rs=sb(nm + "_rs", [P, BATCH], F32, on),
                        nb=sb(nm + "_nb", [P, BATCH], F32, on))

        irr_part = sb("irr_part", [1, 1], F32)
        irregular = sb("irregular", [1, 1], I32)
        g = dict(dst_pad=dst_pad, src_pad=src_pad, edge_key=edge_key, ft_tab=ft_tab, edge_ft=edge_ft,
                 edge_score=edge_score, edge_exp=edge_exp, adj=adj, hn_dram=hn_dram,
                 max_tab=max_tab, parts_tab=parts_tab, out=out, x_sb=x_sb, ident=ident, ident_bf=ident_bf, ones=ones,
                 eps=eps, starts=starts, bases=bases, base_bc=base_bc, strip_no=strip_no, dis_col=dis_col,
                 irr_part=irr_part, irregular=irregular)

        prelude(nc, t, sb, pb, sem, g)
        stage_over()
        node_features(nc, t, sb, pb, sem, g, ln_batch)
        stage_over()
        scores_and_strips(nc, t, sb, pb, sem, g)
        stage_over()
        softmax_numerators(nc, t, sb, pb, sem, g)
        stage_over()
        g["hT"] = sb("hT", [D, NP], F32)
        with ExitStack() as mid:
            g["agg_sb"] = sb("agg_sb", [P, NT, HD], F32, mid)
            aggregate(nc, t, sb, pb, sem, g)
            stage_over()
            general_attention(nc, t, sb, pb, sem, g)
            stage_over()
            node_update(nc, t, sb, pb, sem, g, ln_batch)
            stage_over()
        convolutions(nc, t, sb, pb, sem, g)


def settle(engine, steps_taken):
    engine.sem_inc(steps_taken, 1)


def rounds(engine, n, body):
    body(0, True)
    with engine.Fori(1, n) as i:
        body(i, False)


class Chain:

    def __init__(self, engine, semaphore, base=0):
        self.engine, self.sem, self.n, self.base = engine, semaphore, 0, base

    def __call__(self, ins):
        self.n += 1
        ins.then_inc(self.sem, 1)
        self.engine.wait_ge(self.sem, self.base + self.n)


def prelude(nc, t, sb, pb, sem, g):
    dst_pad, src_pad, edge_key, ft_tab, edge_ft, edge_exp = (g[k] for k in (
        "dst_pad", "src_pad", "edge_key", "ft_tab", "edge_ft", "edge_exp"))
    x_sb, ident, ident_bf, ones, eps, starts, bases, base_bc, strip_no, irr_part = (g[k] for k in (
        "x_sb", "ident", "ident_bf", "ones", "eps", "starts", "bases", "base_bc", "strip_no", "irr_part"))
    with ExitStack() as c:
        fill_no = sb("fill_no", [16, 512], I32, c)
        fill_zero = sb("fill_zero", [16, 512], I32, c)
        fill_neg = sb("fill_neg", [1, FRONT], I32, c)
        zero_f = sb("zero_f", [P, TC * HD], F32, c)
        dst_p = sb("dst_p", [P, EXJ], I32, c)
        src_p = sb("src_p", [P, EXJ], I32, c)
        dst_s = sb("dst_s", [P, EJ], I32, c)
        hi = sb("hi", [P, EXJ], I32, c)
        lo = sb("lo", [P, EXJ], I32, c)
        keys = sb("keys", [P, EXJ, 3], F32, c)
        kf = sb("kf", [P, 2, EXJ], F32, c)
        coarse = sb("coarse", [P, EJ // COARSE], F32, c)
        nxt_s = sb("nxt_s", [P, EJ], I32, c)
        falls = sb("falls", [P, EJ], F32, c)
        thr = sb("thr", [P, NH + 1], F32, c)
        below = sb("below", [P, NH + 1, EJ // COARSE], F32, c)
        below_n = sb("below_n", [P, NH + 2], F32, c)
        start_f = sb("start_f", [1, NH + 1], F32, c)
        lasts = sb("lasts", [1, NG], I32, c)
        last_f = sb("last_f", [1, NG], F32, c)
        odd = sb("odd", [1, NG + NH + NT], F32, c)
        base_f = sb("base_f", [1, NG], F32, c)
        cnt_ps = pb("cnt_ps", [P, 512], F32, c)
        base_ps = pb("base_ps", [P, 512], F32, c)
        pool_const = sem("pool_const")
        filled = sem("filled")
        pads_out = sem("pads_out")
        lists_in = sem("lists_in")
        x_in = sem("x_in")
        keys_made = sem("keys_made")
        keys_out = sem("keys_out")
        counted = sem("counted")
        counts_summed = sem("counts_summed")
        dve_chain = sem("prelude_dve_chain")
        pool_chain = sem("prelude_pool_chain")
        block = c.enter_context(nc.Block())

        @block.gpsimd
        def _(pool):
            link = Chain(pool, pool_chain)
            nc.gpsimd.iota(strip_no[:], [[1, NH]], base=0, channel_multiplier=0,
                           allow_small_or_imprecise_dtypes=True)
            nc.gpsimd.iota(thr[:], [[HALF, NH + 1]], base=0, channel_multiplier=0,
                           allow_small_or_imprecise_dtypes=True)
            link(nc.gpsimd.memset(ident[:], 0.0))
            link(nc.gpsimd.affine_select(out=ident[:], in_=ident[:], compare_op=ALU.not_equal, fill=1.0,
                                         base=0, pattern=[[-1, P]], channel_multiplier=1))
            nc.gpsimd.tensor_copy(ident_bf[:], ident[:]).then_inc(pool_const, 1)

        @block.sync
        def _(sp):
            sp.wait_ge(filled, 1)
            for k in range(0, NT - 1, 8):
                sp.dma_start(x_sb[:, k:k + 8, :], t["x"][k * P:(k + 8) * P, :].rearrange("(b p) d -> p b d", p=P)
                             ).then_inc(x_in, 16)
            sp.dma_start(x_sb[0:N_LAST, NT - 1, :], t["x"][(NT - 1) * P:N, :]).then_inc(x_in, 16)
            sp.dma_start(dst_pad[FRONT:FRONT + E].rearrange("(a b) -> a b", a=16),
                         t["dst"].rearrange("(a b) -> a b", a=16)).then_inc(pads_out, 16)
            sp.dma_start(src_pad[0:E].rearrange("(a b) -> a b", a=16),
                         t["src"].rearrange("(a b) -> a b", a=16)).then_inc(pads_out, 16)
            tail = EX - E + FRONT
            sp.dma_start(dst_pad[FRONT + E:FRONT + EX + FRONT].rearrange("(a b) -> a b", a=16),
                         fill_no[:, 0:tail // 16]).then_inc(pads_out, 16)
            sp.dma_start(src_pad[E:EX].rearrange("(a b) -> a b", a=16),
                         fill_zero[:, 0:(EX - E) // 16]).then_inc(pads_out, 16)
            sp.dma_start(dst_pad[0:FRONT].rearrange("(a b) -> a b", a=1), fill_neg[:]).then_inc(pads_out, 16)
            sp.dma_start(ft_tab[NP:TAB, :], zero_f[:, 0:HD]).then_inc(pads_out, 16)
            sp.dma_start(edge_ft[EP:EX, :].rearrange("(p c) f -> p (c f)", p=P),
                         zero_f[:, 0:(EX - EP) // P * HD]).then_inc(pads_out, 16)
            sp.dma_start(edge_exp[EP:EX, :].rearrange("(p c) f -> p (c f)", p=P),
                         zero_f[:, 0:(EX - EP) // P * H]).then_inc(pads_out, 16)
            sp.wait_ge(pads_out, 8 * 16)
            sp.dma_start(dst_p[:], dst_pad[FRONT:FRONT + EX].rearrange("(p j) -> p j", p=P)).then_inc(lists_in, 16)
            sp.dma_start(src_p[:], src_pad.rearrange("(p j) -> p j", p=P)).then_inc(lists_in, 16)
            sp.dma_start(dst_s[:], dst_pad[FRONT:FRONT + EP].rearrange("(p j) -> p j", p=P)).then_inc(lists_in, 16)
            sp.dma_start(nxt_s[:], dst_pad[FRONT + 1:FRONT + 1 + EP].rearrange("(p j) -> p j", p=P)).then_inc(lists_in, 16)
            sp.dma_start(lasts[0:1, NG - 1:NG], dst_pad[FRONT + E - 1:FRONT + E].rearrange("(a b) -> a b", a=1)
                         ).then_inc(lists_in, 16)
            with nc.allow_non_contiguous_dma(reason="first and last destination of every group"):
                sp.dma_start(lasts[0:1, 0:NG - 1], dst_pad[FRONT:FRONT + EP].rearrange("(g e) -> e g", e=GE)[GE - 1:GE, 0:NG - 1]
                             ).then_inc(lists_in, 16)
                sp.dma_start(bases[0:1, :], dst_pad[FRONT:FRONT + EP].rearrange("(g e) -> e g", e=GE)[0:1, :]
                             ).then_inc(lists_in, 16)
            sp.wait_ge(keys_made, 1)
            sp.dma_start(edge_key.rearrange("(p j) k -> p (j k)", p=P),
                         keys[:].rearrange("p j k -> p (j k)")).then_inc(keys_out, 16)
            sp.wait_ge(keys_out, 16)
            sp.wait_ge(x_in, 16 * 7)

        @block.vector
        def _(dve):
            link = Chain(dve, dve_chain)
            nc.vector.memset(x_sb[:, NT - 1, :], 0.0)
            nc.vector.memset(fill_no[:], NOWHERE)
            nc.vector.memset(fill_zero[:], 0)
            nc.vector.memset(fill_neg[:], -1)
            nc.vector.memset(eps[:], EPS)
            nc.vector.memset(zero_f[:], 0.0)
            link(nc.vector.memset(ones[:], 1.0))
            nc.vector.tensor_copy(kf[0:1, 0, 0:1], ones[0:1, 0:1]).then_inc(filled, 1)
            dve.wait_ge(lists_in, 16 * 7)
            nc.vector.tensor_single_scalar(hi[:], dst_p[:], 4, ALU.logical_shift_right)
            link(nc.vector.tensor_scalar(lo[:], src_p[:], 127, None, ALU.bitwise_and))
            nc.vector.tensor_copy(keys[:, :, 2], lo[:])
            link(nc.vector.tensor_copy(keys[:, :, 0], hi[:]))
            nc.vector.tensor_scalar(hi[:], src_p[:], 7, 4, ALU.logical_shift_right, ALU.logical_shift_left)
            link(nc.vector.tensor_scalar(lo[:], dst_p[:], HALF - 1, None, ALU.bitwise_and))
            nc.vector.tensor_copy(kf[:, 0, :], hi[:])
            link(nc.vector.tensor_copy(kf[:, 1, :], lo[:]))
            link(nc.vector.tensor_tensor(kf[:, 0, :], kf[:, 0, :], kf[:, 1, :], ALU.add))
            nc.vector.tensor_scalar(keys[:, :, 1], kf[:, 0, :], 1.0 / KS, None, ALU.mult).then_inc(keys_made, 1)
            nc.vector.tensor_copy(base_f[:], bases[:])
            link(nc.vector.tensor_copy(coarse[:], dst_s[:].rearrange("p (j c) -> p j c", c=COARSE)[:, :, 0]))
            dve.wait_ge(pool_const, 1)
            J = EJ // COARSE
            link(nc.vector.tensor_tensor(below[:], coarse[:].unsqueeze(1).to_broadcast([P, NH + 1, J]),
                                         thr[:].unsqueeze(2).to_broadcast([P, NH + 1, J]), ALU.is_lt))
            nc.vector.tensor_reduce(below_n[:, 0:NH + 1], below[:], AX.X, ALU.add)
            link(nc.vector.tensor_tensor(falls[:], dst_s[:], nxt_s[:], ALU.is_gt))
            nc.vector.tensor_reduce(below_n[:, NH + 1:NH + 2], falls[:], AX.X, ALU.add).then_inc(counted, 1)
            dve.wait_ge(counts_summed, 1)
            link(nc.vector.tensor_scalar(start_f[:], cnt_ps[0:1, 0:NH + 1], -1.0, 0.0, ALU.add, ALU.max))
            link(nc.vector.tensor_scalar(start_f[:], start_f[:], float(COARSE), None, ALU.mult))
            nc.vector.tensor_copy(starts[:], start_f[:, 0:NH])
            nc.vector.tensor_copy(base_bc[:], base_ps[:, 0:NG])
            sp_ = lambda a, b: odd[:, a:b]
            PT = P // HALF
            nc.vector.tensor_copy(last_f[:], lasts[:])
            nc.vector.tensor_tensor(sp_(NG, NG + NH), start_f[:, 1:NH + 1], start_f[:, 0:NH], ALU.subtract)
            link(nc.vector.tensor_tensor(sp_(NG + NH, NG + NH + NT), start_f[:, PT:NH + 1:PT], start_f[:, 0:NH:PT], ALU.subtract))
            link(nc.vector.tensor_tensor(sp_(0, NG), last_f[:], base_f[:], ALU.subtract))
            link(nc.vector.tensor_scalar(sp_(0, NG), sp_(0, NG), float(P - 1), None, ALU.is_gt))
            nc.vector.tensor_scalar(sp_(NG, NG + NH), sp_(NG, NG + NH), float(SW - COARSE), None, ALU.is_gt)
            link(nc.vector.tensor_scalar(sp_(NG + NH, NG + NH + NT), sp_(NG + NH, NG + NH + NT), float(TW - COARSE), None, ALU.is_gt))
            link(nc.vector.tensor_reduce(irr_part[:], odd[:], AX.X, ALU.add))
            nc.vector.tensor_tensor(irr_part[:], irr_part[:], cnt_ps[0:1, NH + 1:NH + 2], ALU.add)

        @block.tensor
        def _(pe):
            pe.wait_ge(counted, 1)
            nc.tensor.matmul(cnt_ps[:, 0:NH + 2], ones[:], below_n[:], start=True, stop=True)
            nc.tensor.matmul(base_ps[:, 0:NG], ones[0:1, :], base_f[:], start=True, stop=True).then_inc(counts_summed, 1)


def layer_norm_stats(nc, dve, link, ln, rows, tick):
    for b in range(BATCH):
        last = nc.vector.bn_stats(ln["st"][:, b, :], rows(b))
    link(last)
    settle(dve, tick)
    for b in range(BATCH):
        last = nc.vector.bn_aggr(ln["mv"][:, b, :], ln["st"][:, b, :])
    return last


def row_bc(ap):
    return ap.rearrange("(a d) -> a d", a=1).to_broadcast([P, ap.shape[0]])


def node_features(nc, t, sb, pb, sem, g, ln_batch):
    x_sb, ident, eps, hn_dram, ft_tab = (g[k] for k in ("x_sb", "ident", "eps", "hn_dram", "ft_tab"))
    with ExitStack() as c:
        a, b_ = ln_batch("na", c), ln_batch("nb", c)
        w_att = sb("w_att", [D, HD], F32, c)
        lnw = sb("nf_lnw", [P, D], F32, c)
        lnb = sb("nf_lnb", [P, D], F32, c)
        h = sb("nf_h", [P, BATCH, D], F32, c)
        u = sb("nf_u", [P, BATCH, D], F32, c)
        hn = sb("nf_hn", [P, BATCH, D], F32, c)
        hnT = sb("nf_hnT", [D, BATCH, P], F32, c)
        ft = sb("nf_ft", [P, BATCH, HD], F32, c)
        T_ps = pb("nf_T_ps", [D, 2, 512], F32, c)
        ft_ps = pb("nf_ft_ps", [P, 3, 512], F32, c)
        w_in, var1, sd1, neg1, h_done, var2, sd2, hn_done, hnT_ps, hnT_sb, ft_done, ft_sb, ft_out, vch, hn_out, tick = (
            sem("nf_" + s) for s in ("w_in", "var1", "sd1", "neg1", "h_done", "var2", "sd2", "hn_done", "hnT_ps",
                                     "hnT_sb", "ft_done", "ft_sb", "ft_out", "vch", "hn_out", "tick"))
        block = c.enter_context(nc.Block())

        @block.sync
        def _(sp):
            sp.dma_start(w_att[:], t["L0_gnn_W_att"]).then_inc(w_in, 16)
            sp.dma_start(lnw[:], row_bc(t["L0_gnn_ln1_w"])).then_inc(w_in, 16)
            sp.dma_start(lnb[:], row_bc(t["L0_gnn_ln1_b"])).then_inc(w_in, 16)
            def copy_out(i, first):
                sp.wait_ge(hn_done, i + 1)
                sp.dma_start(hn_dram[ds(i * BW, BW), :].rearrange("(b p) f -> p b f", p=P), hn[:]).then_inc(hn_out, 16)
                sp.wait_ge(ft_sb, i + 1)
                sp.dma_start(ft_tab[ds(i * BW, BW), :].rearrange("(b p) f -> p b f", p=P), ft[:]).then_inc(ft_out, 16)
            rounds(sp, NB, copy_out)
            sp.wait_ge(ft_out, 16 * NB)
            sp.wait_ge(hn_out, 16 * NB)

        @block.vector
        def _(dve):
            PER = 10

            def body(i, first):
                link = Chain(dve, vch, i * PER)
                xb = x_sb[:, ds(i * BATCH, BATCH), :]
                for b in range(BATCH):
                    last = nc.vector.bn_stats(a["st"][:, b, :], x_sb[:, ds(i * BATCH + b, 1), :])
                link(last)
                settle(dve, tick)
                for b in range(BATCH):
                    last = nc.vector.bn_aggr(a["mv"][:, b, :], a["st"][:, b, :])
                last.then_inc(var1, 1)
                dve.wait_ge(sd1, i + 1)
                link(nc.vector.reciprocal(a["rs"][:], a["sd"][:]))
                nc.vector.scalar_tensor_tensor(a["nb"][:], a["mv"][:, :, 0], -1.0, a["rs"][:], ALU.mult, ALU.mult
                                               ).then_inc(neg1, 1)
                dve.wait_ge(h_done, i + 1)
                link(layer_norm_stats(nc, dve, link, b_, lambda b: h[:, b, :], tick))
                nc.vector.tensor_tensor(u[:], h[:], b_["mv"][:, :, 0:1].to_broadcast([P, BATCH, D]), ALU.subtract
                                        ).then_inc(var2, 1)
                dve.wait_ge(sd2, i + 1)
                dve.wait_ge(var2, i + 1)
                link(nc.vector.reciprocal(b_["rs"][:], b_["sd"][:]))
                link(nc.vector.tensor_tensor(u[:], u[:], b_["rs"][:].unsqueeze(2).to_broadcast([P, BATCH, D]), ALU.mult))
                dve.wait_ge(w_in, 48)
                link(nc.vector.tensor_tensor(u[:], u[:], lnw[:].unsqueeze(1).to_broadcast([P, BATCH, D]), ALU.mult))
                if not first:
                    dve.wait_ge(hn_out, 16 * i)
                nc.vector.tensor_tensor(hn[:], u[:], lnb[:].unsqueeze(1).to_broadcast([P, BATCH, D]), ALU.add
                                        ).then_inc(hn_done, 1)
                dve.wait_ge(hnT_ps, i + 1)
                nc.vector.tensor_copy(hnT[:, 0:4, :].rearrange("f b p -> f (b p)"), T_ps[:, 0, :])
                nc.vector.tensor_copy(hnT[:, 4:7, :].rearrange("f b p -> f (b p)"), T_ps[:, 1, 0:384]).then_inc(hnT_sb, 1)
                dve.wait_ge(hnT_sb, i + 1)
                assert link.n <= PER
                while link.n < PER:
                    link(nc.vector.memset(a["nb"][0:1, 0:1], 0.0))
            rounds(dve, NB, body)

        @block.scalar
        def _(act):
            def body(i, first):
                act.wait_ge(var1, i + 1)
                nc.scalar.activation(a["sd"][:], a["mv"][:, :, 1], ACT.Sqrt, bias=eps[:]).then_inc(sd1, 1)
                act.wait_ge(neg1, i + 1)
                for b in range(BATCH):
                    last = nc.scalar.activation(h[:, b, :], x_sb[:, ds(i * BATCH + b, 1), :], ACT.Relu,
                                                bias=a["nb"][:, b:b + 1], scale=a["rs"][:, b:b + 1])
                last.then_inc(h_done, 1)
                act.wait_ge(var2, i + 1)
                nc.scalar.activation(b_["sd"][:], b_["mv"][:, :, 1], ACT.Sqrt, bias=eps[:]).then_inc(sd2, 1)
                act.wait_ge(ft_done, i + 1)
                if not first:
                    act.wait_ge(ft_out, 16 * i)
                for q, n in ((0, 3), (1, 3), (2, 1)):
                    last = nc.scalar.copy(ft[:, 3 * q:3 * q + n, :].rearrange("p b f -> p (b f)"), ft_ps[:, q, 0:n * HD])
                last.then_inc(ft_sb, 1)
            rounds(act, NB, body)

        @block.tensor
        def _(pe):
            pe.wait_ge(w_in, 48)

            def body(i, first):
                pe.wait_ge(hn_done, i + 1)
                for b in range(BATCH):
                    last = nc.tensor.transpose(T_ps[:, b // 4, (b % 4) * P:(b % 4 + 1) * P], hn[:, b, :], ident[:])
                last.then_inc(hnT_ps, 1)
                pe.wait_ge(hnT_sb, i + 1)
                if not first:
                    pe.wait_ge(ft_sb, i)
                for b in range(BATCH):
                    last = nc.tensor.matmul(ft_ps[:, b // 3, (b % 3) * HD:(b % 3 + 1) * HD], hnT[:, b, :], w_att[:],
                                            start=True, stop=True)
                last.then_inc(ft_done, 1)
            rounds(pe, NB, body)


def scores_and_strips(nc, t, sb, pb, sem, g):
    (dst_pad, src_pad, edge_key, ft_tab, edge_ft, edge_score, adj, starts, bases, base_bc, strip_no, ident_bf) = (
        g[k] for k in ("dst_pad", "src_pad", "edge_key", "ft_tab", "edge_ft", "edge_score", "adj", "starts",
                       "bases", "base_bc", "strip_no", "ident_bf"))
    with ExitStack() as c:
        src_ix = sb("src_ix", [P, UN, GC], I32, c)
        dst_ix = sb("dst_ix", [P, UN, GC], I32, c)
        win = sb("win", [P, UN, HD], F32, c)
        ek = sb("ek", [P, UN, 2, SC, 3], F32, c)
        fts = [sb(f"fts{u}", [P, GC, HD], F32, c) for u in range(UN)]
        rel = sb("rel", [P, 2, GC], BF16, c)
        dist = sb("dist", [P, GE], F32, c)
        ohdT = sb("ohdT", [P, 2, GE], F32, c)
        prod = sb("prod", [P, GC, HD], F32, c)
        score = sb("score", [P, UN, GC * H], F32, c)
        kk = sb("kk", [P, 2, 2, SC], F32, c)
        key_iota = sb("key_iota", [P, KEYS], FP16, c)
        lo_iota = sb("lo_iota", [P, P], FP16, c)
        key_i = sb("key_i", [P, KEYS], F32, c)
        neg_p = sb("neg_p", [P, 1], F32, c)
        ohk = sb("ohk", [P, 2, 2, SC, KEYS], BF16, c)
        ohl = sb("ohl", [P, 2, 2, SC, P], BF16, c)
        dist_l = sb("dist_l", [P, SC, P], BF16, c)
        strip = sb("strip", [P, 2, NT, 2, HALF], BF16, c)
        bc_ps = pb("bc_ps", [P, 512], F32, c)
        adj_ps = [pb(f"adj_ps{q}", [P, 512], F32, c) for q in range(4)]
        ftd_ps = [pb(f"ftd_ps{q}", [P, 512], F32, c) for q in range(3)]
        iotas = sem("iotas")
        idx_in = [sem(f"idx_in{u}") for u in range(UN)]
        ek_in = [sem(f"ek_in{u}") for u in range(UN)]
        gathered = [sem(f"gathered{u}") for u in range(UN)]
        fts_out = [sem(f"fts_out{u}") for u in range(UN)]
        score_out = [sem(f"score_out{u}") for u in range(UN)]
        strip_out = [sem(f"strip_out{u}") for u in range(2)]
        rel_made, keys_done, bc_done, dist_done, ohdT_done, ftd_done, prod_done, score_done, adj_done, strip_done, kk_done, dist_l_done, ohl_done = (
            sem("sc_" + s) for s in ("rel_made", "keys_done", "bc_done", "dist_done", "ohdT_done", "ftd_done",
                                     "prod_done", "score_done", "adj_done", "strip_done", "kk_done", "dist_l_done", "ohl_done"))
        tick_pool, tick_sp = sem("sc_tick_pool"), sem("sc_tick_sp")
        QT = ((0, 25), (25, 24))
        block = c.enter_context(nc.Block())

        def steps(engine, body):
            for u in range(UN):
                body(u, 0, u, True, True)
            with engine.Fori(1, NG // UN - 1) as j:
                for u in range(UN):
                    body(j * UN + u, j, u, False, True)
            for u in range(UN):
                body(NG - UN + u, NG // UN - 1, u, False, u < UN - 1)

        def after(i, j, u, first):
            return i + 1, j + (u == UN - 1), (u + 1) % UN, first and u < UN - 1

        def column(a, n):
            return a[:, n:n + 1] if isinstance(n, int) else a[:, ds(n, 1)]

        @block.sync
        def _(sp):
            def store_rows(i, j, u):
                sp.wait_ge(gathered[u], 16 * GC * (j + 1))
                sp.dma_start(edge_ft[ds(i * GE, GE), :].rearrange("(p c) f -> p (c f)", p=P),
                             fts[u][:].rearrange("p c f -> p (c f)")).then_inc(fts_out[u], 16)

            def store_scores(i, u):
                sp.wait_ge(score_done, i + 1)
                sp.dma_start(edge_score[ds(i * GE, GE), :].rearrange("(p c) h -> p (c h)", p=P), score[:, u, :]
                             ).then_inc(score_out[u], 16)

            def body(i, j, u, first, more):
                start = [sp.value_load(column(starts, n), min_val=0, max_val=E) for n in (2 * i, 2 * i + 1)]
                base = sp.value_load(column(bases, i), min_val=0, max_val=NP)
                if not first:
                    settle(sp, tick_sp)
                    store_rows(i - UN, j - 1, u)
                    sp.wait_ge(ftd_done, i - UN + 1)
                    settle(sp, tick_sp)
                    sp.wait_ge(adj_done, 2 * (i - UN + 1))
                    settle(sp, tick_sp)
                sp.dma_start(src_ix[:, u, :], src_pad[ds(i * GE, GE)].rearrange("(p c) -> p c", c=GC)
                             ).then_inc(idx_in[u], 16)
                sp.dma_start(dst_ix[:, u, :], dst_pad[ds(i * GE + FRONT, GE)].rearrange("(p c) -> p c", c=GC)
                             ).then_inc(idx_in[u], 16)
                sp.dma_start(win[:, u, :], ft_tab[ds(base, P), :]).then_inc(idx_in[u], 16)
                for a in range(2):
                    sp.dma_start(ek[:, u, a, :, :], edge_key[ds(start[a], SW), :].rearrange("(p c) k -> p c k", c=SC)
                                 ).then_inc(ek_in[u], 16)
                if not first:
                    store_scores(i - UN, u)
            steps(sp, body)
            for u in range(UN):
                store_rows(NG - UN + u, NG // UN - 1, u)
                store_scores(NG - UN + u, u)
            for u in range(UN):
                sp.wait_ge(fts_out[u], 16 * (NG // UN))
                sp.wait_ge(score_out[u], 16 * (NG // UN))
            for u in range(2):
                sp.wait_ge(strip_out[u], 16 * (NG // 2))

        @block.gpsimd
        def _(pool):
            nc.gpsimd.iota(key_i[:], [[1, KEYS]], base=0, channel_multiplier=0, allow_small_or_imprecise_dtypes=True)
            nc.gpsimd.iota(lo_iota[:], [[1, P]], base=0, channel_multiplier=0, allow_small_or_imprecise_dtypes=True)
            nc.gpsimd.iota(neg_p[:], [[0, 1]], base=0, channel_multiplier=-1, allow_small_or_imprecise_dtypes=True
                           ).then_inc(iotas, 1)

            def body(i, j, u, first, more):
                if not first:
                    pool.wait_ge(prod_done, i - UN + 1)
                    pool.wait_ge(fts_out[u], 16 * j)
                pool.wait_ge(idx_in[u], 48 * (j + 1))
                settle(pool, tick_pool)
                for k in range(GC):
                    nc.gpsimd.indirect_dma_start(fts[u][:, k, :], None, ft_tab[:, :],
                                                 bass.IndirectOffsetOnAxis(src_ix[:, u, k:k + 1], 0)
                                                 ).then_inc(gathered[u], 16)
            steps(pool, body)

        @block.vector
        def _(dve):
            dve.wait_ge(iotas, 1)
            nc.vector.tensor_scalar(key_iota[:], key_i[:], 1.0 / KS, None, ALU.mult).then_inc(iotas, 1)
            dve.wait_ge(iotas, 2)

            def relative(i, j, u, first):
                dve.wait_ge(idx_in[u], 48 * (j + 1))
                if not (first and u < 2):
                    dve.wait_ge(bc_done, 2 * (i - 1))
                nc.vector.tensor_scalar(rel[:, u % 2, :], dst_ix[:, u, :], column(base_bc, i), None, ALU.subtract
                                        ).then_inc(rel_made, 1)

            def one_hots(i, j, u, first):
                s = u % 2
                dve.wait_ge(ek_in[u], 32 * (j + 1))
                if not (first and u < 2):
                    dve.wait_ge(adj_done, 2 * (i - 1))
                for a in range(2):
                    nc.vector.scalar_tensor_tensor(kk[:, s, a, :], ek[:, u, a, :, 0], column(strip_no, 2 * i + a),
                                                   ek[:, u, a, :, 1], ALU.not_equal, ALU.add).then_inc(kk_done, 1)
                for k in range(SC):
                    nc.vector.tensor_scalar(ohl[:, s, 0, k, :], lo_iota[:], ek[:, u, 0, k, 2:3], None, ALU.is_equal)
                dve.wait_ge(kk_done, 2 * i + 2)
                for a in range(2):
                    for k in range(SC):
                        last = nc.vector.tensor_scalar(ohk[:, s, a, k, :], key_iota[:], kk[:, s, a, k:k + 1], None,
                                                       ALU.is_equal)
                    last.then_inc(keys_done, 1)

            def multiply(i, j, u, one, first):
                dve.wait_ge(gathered[u], 16 * GC * (j + 1))
                dve.wait_ge(ftd_done, i + 1)
                if not one:
                    dve.wait_ge(score_done, i)
                if not first:
                    dve.wait_ge(score_out[u], 16 * j)
                for q, n in ((0, 3), (1, 3), (2, 2)):
                    last = nc.vector.tensor_tensor(prod[:, 3 * q:3 * q + n, :],
                                                   ftd_ps[q][:, 0:n * HD].rearrange("p (b f) -> p b f", f=HD),
                                                   fts[u][:, 3 * q:3 * q + n, :], ALU.mult)
                last.then_inc(prod_done, 1)
                dve.wait_ge(prod_done, i + 1)
                nc.vector.tensor_reduce(score[:, u, :], prod[:].rearrange("p c (h d) -> p (c h) d", d=DH),
                                        AX.X, ALU.add).then_inc(score_done, 1)

            def body(i, j, u, first, more):
                if more:
                    relative(*after(i, j, u, first))
                one_hots(i, j, u, first)
                if first and u:
                    multiply(i - 1, j, u - 1, u == 1, True)
                elif not first:
                    multiply(i - 1, j - (u == 0), (u - 1) % UN, False, False)
            relative(0, 0, 0, True)
            for u in range(UN):
                body(u, 0, u, True, True)
            relative(*after(UN, 1, 0, False))
            one_hots(UN, 1, 0, False)
            multiply(UN - 1, 0, UN - 1, False, True)
            for u in range(1, UN):
                body(UN + u, 1, u, False, True)
            with dve.Fori(2, NG // UN - 1) as j:
                for u in range(UN):
                    body(j * UN + u, j, u, False, True)
            for u in range(UN):
                body(NG - UN + u, NG // UN - 1, u, False, u < UN - 1)
            multiply(NG - 1, NG // UN - 1, UN - 1, False, False)

        @block.scalar
        def _(act):
            act.wait_ge(iotas, 2)

            def distances(i, a):
                act.wait_ge(bc_done, 2 * i + a + 1)
                nc.scalar.activation(dist[:, a * 512:(a + 1) * 512], bc_ps[:], ACT.Abs, bias=neg_p[:]
                                     ).then_inc(dist_done, 1)

            def destination_one_hot(i, u, first):
                act.wait_ge(dist_done, 2 * i + 2)
                if not (first and u < 2):
                    act.wait_ge(ftd_done, i - 1)
                nc.scalar.activation(ohdT[:, u % 2, :], dist[:], ACT.Relu, bias=1.0, scale=-1.0).then_inc(ohdT_done, 1)

            def source_one_hot(i, j, u, first):
                act.wait_ge(ek_in[u], 32 * (j + 1))
                if not (first and u == 0):
                    act.wait_ge(ohl_done, i)
                for k in range(SC):
                    last = nc.scalar.activation(dist_l[:, k, :], lo_iota[:], ACT.Abs, bias=ek[:, u, 1, k, 2:3], scale=-1.0)
                last.then_inc(dist_l_done, 1)
                if not (first and u < 2):
                    act.wait_ge(adj_done, 2 * (i - 1))
                act.wait_ge(dist_l_done, i + 1)
                nc.scalar.activation(ohl[:, u % 2, 1, :, :], dist_l[:], ACT.Relu, bias=1.0, scale=-1.0
                                     ).then_inc(ohl_done, 1)

            def copy_half(i, a, u):
                act.wait_ge(adj_done, 2 * i + a + 1)
                for q, (t0, m) in enumerate(QT):
                    last = nc.scalar.copy(strip[:, u % 2, t0:t0 + m, a, :],
                                          adj_ps[2 * a + q][:, 0:m * HALF].rearrange("p (t d) -> p t d", d=HALF))
                last.then_inc(strip_done, 1)

            def body(i, j, u, first, more):
                s = u % 2
                nxt = after(i, j, u, first)
                if more:
                    act.wait_ge(ohdT_done, i + 1)
                    distances(i + 1, 0)
                if not (first and u < 2):
                    act.wait_ge(strip_out[s], 16 * (j * (UN // 2) + u // 2))
                copy_half(i, 0, u)
                if more:
                    distances(i + 1, 1)
                    destination_one_hot(nxt[0], nxt[2], nxt[3])
                    source_one_hot(*nxt)
                copy_half(i, 1, u)
                act.wait_ge(strip_done, 2 * i + 2)
                act.dma_start(adj[ds(i, 1)].rearrange("a p s -> (a p) s"),
                              strip[:, s].rearrange("p t a d -> p (t a d)")).then_inc(strip_out[s], 16)
            distances(0, 0)
            distances(0, 1)
            destination_one_hot(0, 0, True)
            source_one_hot(0, 0, 0, True)
            steps(act, body)

        @block.tensor
        def _(pe):
            def spread(i, a, s):
                if a == 0:
                    pe.wait_ge(rel_made, i + 1)
                if a or not (isinstance(i, int) and i == 0):
                    pe.wait_ge(dist_done, 2 * i + a)
                for k in range(4):
                    last = nc.tensor.matmul(bc_ps[:, k * P:(k + 1) * P],
                                            rel[:, s, 4 * a + k:4 * a + k + 1].to_broadcast([P, P]), ident_bf[:],
                                            start=True, stop=True)
                last.then_inc(bc_done, 1)

            def count(i, a, q, s):
                t0, m = QT[q]
                for k in range(SC):
                    last = nc.tensor.matmul(adj_ps[2 * a + q][:, 0:m * HALF], ohl[:, s, a, k, :],
                                            ohk[:, s, a, k, t0 * HALF:(t0 + m) * HALF],
                                            start=(k == 0), stop=(k == SC - 1))
                return last

            def body(i, j, u, first, more):
                s = u % 2
                one = first and u == 0
                for a in range(2):
                    pe.wait_ge(keys_done, 2 * i + a + 1)
                    if a:
                        pe.wait_ge(ohl_done, i + 1)
                    if not one:
                        pe.wait_ge(strip_done, 2 * i + a - 1)
                    count(i, a, 0, s)
                    if more:
                        spread(i + 1, a, 1 - s)
                    count(i, a, 1, s).then_inc(adj_done, 1)
                pe.wait_ge(ohdT_done, i + 1)
                if not one:
                    pe.wait_ge(prod_done, i)
                pe.wait_ge(idx_in[u], 48 * (j + 1))
                for k in range(GC):
                    last = nc.tensor.matmul(ftd_ps[k // 3][:, (k % 3) * HD:(k % 3 + 1) * HD],
                                            ohdT[:, s, k * P:(k + 1) * P], win[:, u, :], start=True, stop=True)
                last.then_inc(ftd_done, 1)
            spread(0, 0, 0)
            spread(0, 1, 0)
            steps(pe, body)


def softmax_numerators(nc, t, sb, pb, sem, g):
    dst_pad, edge_score, edge_exp, ident = (g[k] for k in ("dst_pad", "edge_score", "edge_exp", "ident"))
    with ExitStack() as c:
        s_all = sb("sm_s", [P, EJ, H], F32, c)
        f_all = sb("sm_f", [P, EJ, H], F32, c)
        here = sb("sm_here", [P, EJ], I32, c)
        before = sb("sm_before", [P, EJ], I32, c)
        after = sb("sm_after", [P, EJ], I32, c)
        first = sb("sm_first", [P, EJ], F32, c)
        last_ = sb("sm_last", [P, EJ], F32, c)
        ends = sb("sm_ends", [P, 4, H], F32, c)
        flags = sb("sm_flags", [P, 2], F32, c)
        rows = sb("sm_rows", [H, 4, P], F32, c)
        step_ = sb("sm_step", [H, 4, P], F32, c)
        carry = sb("sm_carry", [H, 2, P], F32, c)
        carry_p = sb("sm_carry_p", [P, 2, H], F32, c)
        tr_ps = pb("sm_tr_ps", [H, 512], F32, c)
        back_ps = pb("sm_back_ps", [P, 512], F32, c)
        d_in, s_in, ends_made, rows_ps, carries, back, diff, expd, e_out, vch = (
            sem("sm_" + s) for s in ("d_in", "s_in", "ends_made", "rows_ps", "carries", "back", "diff", "expd",
                                     "e_out", "vch"))
        block = c.enter_context(nc.Block())

        @block.sync
        def _(sp):
            for i, buf in enumerate((here, before, after)):
                off = FRONT + (0, -1, 1)[i]
                sp.dma_start(buf[:], dst_pad[off:off + EP].rearrange("(p j) -> p j", p=P)).then_inc(d_in, 16)
            sp.dma_start(s_all[:].rearrange("p j h -> p (j h)"),
                         edge_score[0:EP, :].rearrange("(p j) h -> p (j h)", p=P)).then_inc(s_in, 16)
            sp.wait_ge(expd, 1)
            sp.dma_start(edge_exp[0:EP, :].rearrange("(p j) h -> p (j h)", p=P),
                         s_all[:].rearrange("p j h -> p (j h)")).then_inc(e_out, 16)
            sp.wait_ge(e_out, 16)

        @block.vector
        def _(dve):
            link = Chain(dve, vch)
            dve.wait_ge(d_in, 48)
            nc.vector.tensor_tensor(first[:], here[:], before[:], ALU.not_equal)
            link(nc.vector.tensor_tensor(last_[:], here[:], after[:], ALU.not_equal))
            link(nc.vector.tensor_tensor(flags[:, 1:2], here[:, 0:1], here[:, EJ - 1:EJ], ALU.not_equal))
            nc.vector.tensor_scalar(flags[:, 0:1], first[:, 0:1], NEG, None, ALU.mult)
            link(nc.vector.tensor_scalar(flags[:, 1:2], flags[:, 1:2], NEG, None, ALU.mult))
            nc.vector.tensor_copy(ends[:, 2, :], flags[:, 0:1].to_broadcast([P, H]))
            nc.vector.tensor_copy(ends[:, 3, :], flags[:, 1:2].to_broadcast([P, H]))
            nc.vector.tensor_scalar(first[:], first[:], NEG, None, ALU.mult)
            link(nc.vector.tensor_scalar(last_[:], last_[:], NEG, None, ALU.mult))
            dve.wait_ge(s_in, 16)

            def scan(out, data, fresh, initial, back):
                if back:
                    out, data, fresh = out[:, ::-1], data[:, ::-1], fresh[:, ::-1]
                return nc.vector.tensor_tensor_scan(out, fresh, data, initial, ALU.add, ALU.max)

            for h in range(H):
                ins = scan(f_all[:, :, h], s_all[:, :, h], first[:], NEG, False)
            link(ins)
            link(nc.vector.tensor_copy(ends[:, 0, :], f_all[:, EJ - 1, :]))
            for h in range(H):
                ins = scan(f_all[:, :, h], s_all[:, :, h], last_[:], NEG, True)
            link(ins)
            nc.vector.tensor_copy(ends[:, 1, :], f_all[:, 0, :]).then_inc(ends_made, 1)
            dve.wait_ge(rows_ps, 1)
            link(nc.vector.tensor_copy(rows[:], tr_ps[:].rearrange("h (k p) -> h k p", k=4)))
            nc.vector.memset(step_[:], NEG)
            link(nc.vector.memset(carry[:], NEG))
            nc.vector.tensor_tensor(step_[:, 0, 1:P], rows[:, 2, 1:P], rows[:, 3, 0:P - 1], ALU.add)
            nc.vector.tensor_tensor(step_[:, 1, 1:P], rows[:, 2, 1:P], rows[:, 0, 0:P - 1], ALU.add)
            nc.vector.tensor_tensor(step_[:, 2, 0:P - 1], rows[:, 2, 1:P], rows[:, 3, 1:P], ALU.add)
            link(nc.vector.tensor_tensor(step_[:, 3, 0:P - 1], rows[:, 2, 1:P], rows[:, 1, 1:P], ALU.add))
            scan(carry[:, 0, :], step_[:, 1, :], step_[:, 0, :], NEG, False)
            scan(carry[:, 1, :], step_[:, 3, :], step_[:, 2, :], NEG, True).then_inc(carries, 1)
            dve.wait_ge(back, 1)
            link(nc.vector.tensor_copy(carry_p[:], back_ps[:, 0:2 * H].rearrange("p (k h) -> p k h", k=2)))
            for h in range(H):
                ins = scan(f_all[:, :, h], s_all[:, :, h], first[:], carry_p[:, 0, h:h + 1], False)
            link(ins)
            for h in range(H):
                ins = scan(f_all[:, :, h], f_all[:, :, h], last_[:], carry_p[:, 1, h:h + 1], True)
            link(ins)
            nc.vector.tensor_tensor(s_all[:], s_all[:], f_all[:], ALU.subtract).then_inc(diff, 1)

        @block.tensor
        def _(pe):
            pe.wait_ge(ends_made, 1)
            for k in range(4):
                ins = nc.tensor.transpose(tr_ps[:, k * P:(k + 1) * P], ends[:, k, :], ident[:])
            ins.then_inc(rows_ps, 1)
            pe.wait_ge(carries, 1)
            for k in range(2):
                ins = nc.tensor.transpose(back_ps[:, k * H:(k + 1) * H], carry[:, k, :], ident[0:H, 0:H])
            ins.then_inc(back, 1)

        @block.scalar
        def _(act):
            act.wait_ge(diff, 1)
            nc.scalar.activation(s_all[:], s_all[:], ACT.Exp, scale=float(DH) ** -0.5).then_inc(expd, 1)


def aggregate(nc, t, sb, pb, sem, g):
    dst_pad, edge_ft, edge_exp, starts, agg_sb, dis_col, ones, irr_part, irregular = (g[k] for k in (
        "dst_pad", "edge_ft", "edge_exp", "starts", "agg_sb", "dis_col", "ones", "irr_part", "irregular"))
    W = HD + H + 1
    CP = 10
    CA = 10
    with ExitStack() as c:
        rows = sb("ag_rows", [P, 2, TC, HD], F32, c)
        ex = sb("ag_ex", [P, 2, TC, H], F32, c)
        dst = sb("ag_dst", [P, 2, TC], I32, c)
        rel = sb("ag_rel", [P, 2, TC], F32, c)
        terms = sb("ag_terms", [P, 2, TC, W], F32, c)
        oh = sb("ag_oh", [P, 2, TC, P], F32, c)
        dist = sb("ag_dist", [P, CA, P], F32, c)
        iota = sb("ag_iota", [P, P], F32, c)
        neg_iota = sb("ag_neg_iota", [P, P], F32, c)
        tile_no = sb("ag_tile_no", [P, NT], F32, c)
        z = sb("ag_z", [P, H], F32, c)
        deg = sb("ag_deg", [P, NT], F32, c)
        high = sb("ag_high", [P, NT], F32, c)
        high_n = sb("ag_high_n", [P, 1], F32, c)
        sum_ps = [pb(f"ag_ps{s}", [P, 512], F32, c) for s in range(2)]
        in_ = [sem(f"ag_in{s}") for s in range(2)]
        const, rel_made, terms_dve, terms_pool, oh_dve, oh_act, dist_made, summed, sq, vch, high_made, high_ps = (
            sem("ag_" + s) for s in ("const", "rel_made", "terms_dve", "terms_pool", "oh_dve", "oh_act",
                                     "dist_made", "summed", "sq", "vch", "high_made", "high_ps"))
        LINKS = 3
        block = c.enter_context(nc.Block())

        def steps(engine, body):
            body(0, 0, 0, True)
            body(1, 0, 1, True)
            with engine.Fori(1, NT // 2) as j:
                body(j * 2, j, 0, False)
                body(j * 2 + 1, j, 1, False)
            body(NT - 1, NT // 2, 0, False)

        @block.sync
        def _(sp):
            def body(i, j, s, first):
                at = i * (P // HALF)
                start = sp.value_load(starts[0:1, at:at + 1] if isinstance(at, int) else starts[0:1, ds(at, 1)],
                                      min_val=0, max_val=E)
                if not first:
                    sp.wait_ge(terms_dve, i - 1)
                    sp.wait_ge(terms_pool, i - 1)
                sp.dma_start(dst[:, s, :], dst_pad[ds(start + FRONT, TW)].rearrange("(p c) -> p c", c=TC)
                             ).then_inc(in_[s], 16)
                sp.dma_start(ex[:, s, :, :].rearrange("p c h -> p (c h)"),
                             edge_exp[ds(start, TW), :].rearrange("(p c) h -> p (c h)", c=TC)).then_inc(in_[s], 16)
                sp.dma_start(rows[:, s, :, :].rearrange("p c f -> p (c f)"),
                             edge_ft[ds(start, TW), :].rearrange("(p c) f -> p (c f)", c=TC)).then_inc(in_[s], 16)
            steps(sp, body)

        @block.gpsimd
        def _(pool):
            nc.gpsimd.iota(iota[:], [[1, P]], base=0, channel_multiplier=0, allow_small_or_imprecise_dtypes=True)
            nc.gpsimd.iota(tile_no[:], [[P, NT]], base=0, channel_multiplier=0, allow_small_or_imprecise_dtypes=True)
            nc.gpsimd.iota(neg_iota[:], [[-1, P]], base=0, channel_multiplier=0, allow_small_or_imprecise_dtypes=True)
            nc.gpsimd.memset(terms[:, 0, :, W - 1:W], 1.0)
            nc.gpsimd.memset(terms[:, 1, :, W - 1:W], 1.0).then_inc(const, 1)

            def body(i, j, s, first):
                if not first:
                    pool.wait_ge(summed, i - 1)
                pool.wait_ge(in_[s], 48 * (j + 1))
                nc.gpsimd.tensor_tensor(terms[:, s, 0:CP, 0:HD].rearrange("p c (h d) -> p c h d", d=DH),
                                        rows[:, s, 0:CP, :].rearrange("p c (h d) -> p c h d", d=DH),
                                        ex[:, s, 0:CP, :].unsqueeze(3).to_broadcast([P, CP, H, DH]), ALU.mult
                                        ).then_inc(terms_pool, 1)
            steps(pool, body)

        @block.vector
        def _(dve):
            dve.wait_ge(const, 1)

            def body(i, j, s, first):
                dve.wait_ge(in_[s], 48 * (j + 1))
                if not first:
                    dve.wait_ge(summed, i - 1)
                nc.vector.tensor_scalar(rel[:, s, :], dst[:, s, :],
                                        tile_no[:, i:i + 1] if isinstance(i, int) else tile_no[:, ds(i, 1)],
                                        -1.0, ALU.subtract, ALU.mult).then_inc(rel_made, 1)
                nc.vector.tensor_copy(terms[:, s, :, HD:HD + H], ex[:, s, :, :])
                nc.vector.tensor_tensor(terms[:, s, CP:TC, 0:HD].rearrange("p c (h d) -> p c h d", d=DH),
                                        rows[:, s, CP:TC, :].rearrange("p c (h d) -> p c h d", d=DH),
                                        ex[:, s, CP:TC, :].unsqueeze(3).to_broadcast([P, TC - CP, H, DH]), ALU.mult
                                        ).then_inc(terms_dve, 1)
                dve.wait_ge(rel_made, i + 1)
                nc.vector.tensor_tensor(oh[:, s, CA:TC, :], neg_iota[:].unsqueeze(1).to_broadcast([P, TC - CA, P]),
                                        rel[:, s, CA:TC].unsqueeze(2).to_broadcast([P, TC - CA, P]), ALU.is_equal
                                        ).then_inc(oh_dve, 1)

            def quotient(i, s):
                dve.wait_ge(summed, i + 1)
                link = Chain(dve, vch, i * LINKS)
                link(nc.vector.tensor_scalar(z[:], sum_ps[s][:, HD:HD + H], 1e-30, None, ALU.max))
                link(nc.vector.reciprocal(z[:], z[:]))
                nc.vector.tensor_copy(deg[:, i:i + 1] if isinstance(i, int) else deg[:, ds(i, 1)],
                                      sum_ps[s][:, W - 1:W])
                o = agg_sb[:, i:i + 1, :] if isinstance(i, int) else agg_sb[:, ds(i, 1), :]
                link(nc.vector.tensor_tensor(o.rearrange("p a (h d) -> p (a h) d", d=DH),
                                             sum_ps[s][:, 0:HD].rearrange("p (h d) -> p h d", d=DH),
                                             z[:].unsqueeze(2).to_broadcast([P, H, DH]), ALU.mult))

            def step(i, j, s, first):
                body(i, j, s, first)
                if not (first and s == 0):
                    quotient(i - 1, 1 - s)
            steps(dve, step)
            quotient(NT - 1, 0)
            link = Chain(dve, vch, LINKS * NT)
            link(nc.vector.tensor_scalar(high[:], deg[:], 256.0, None, ALU.is_gt))
            nc.vector.tensor_reduce(high_n[:], high[:], AX.X, ALU.add).then_inc(high_made, 1)
            dve.wait_ge(high_ps, 1)
            link(nc.vector.tensor_tensor(irr_part[:], irr_part[:], sum_ps[0][0:1, 0:1], ALU.add))
            nc.vector.tensor_scalar(irregular[:], irr_part[:], FORCE_GENERAL, None, ALU.is_gt)
            dve.wait_ge(sq, 1)
            nc.vector.reciprocal(dis_col[:], deg[:]).then_inc(sq, 1)
            dve.wait_ge(sq, 2)

        @block.scalar
        def _(act):
            act.wait_ge(const, 1)

            def body(i, j, s, first):
                if not (isinstance(i, int) and i == 0):
                    act.wait_ge(oh_act, i)
                act.wait_ge(rel_made, i + 1)
                for k in range(CA):
                    last = nc.scalar.activation(dist[:, k, :], iota[:], ACT.Abs, bias=rel[:, s, k:k + 1])
                last.then_inc(dist_made, 1)
                act.wait_ge(dist_made, i + 1)
                if not first:
                    act.wait_ge(summed, i - 1)
                nc.scalar.activation(oh[:, s, 0:CA, :], dist[:], ACT.Relu, bias=1.0, scale=-1.0).then_inc(oh_act, 1)
            steps(act, body)
            act.wait_ge(high_made, 1)
            nc.scalar.activation(deg[:], deg[:], ACT.Sqrt, bias=1.0).then_inc(sq, 1)

        @block.tensor
        def _(pe):
            def body(i, j, s, first):
                pe.wait_ge(terms_dve, i + 1)
                pe.wait_ge(terms_pool, i + 1)
                pe.wait_ge(oh_dve, i + 1)
                pe.wait_ge(oh_act, i + 1)
                if not first:
                    pe.wait_ge(vch, (i - 1) * LINKS)
                for k in range(TC):
                    last = nc.tensor.matmul(sum_ps[s][:, 0:W], oh[:, s, k, :], terms[:, s, k, :],
                                            start=(k == 0), stop=(k == TC - 1))
                last.then_inc(summed, 1)
            steps(pe, body)
            pe.wait_ge(high_made, 1)
            nc.tensor.matmul(sum_ps[0][:, 0:1], ones[:], high_n[:], start=True, stop=True).then_inc(high_ps, 1)


def general_attention(nc, t, sb, pb, sem, g):
    src_pad, dst_pad, ft_tab, edge_score, max_tab, agg_sb, dis_col, ident, irregular = (g[k] for k in (
        "src_pad", "dst_pad", "ft_tab", "edge_score", "max_tab", "agg_sb", "dis_col", "ident", "irregular"))
    W = HD + H + 1
    NCH = EP // P
    with ExitStack() as c:
        six = sb("ga_six", [P, 1], I32, c)
        dix = sb("ga_dix", [P, 1], I32, c)
        a_rows = sb("ga_a", [P, HD], F32, c)
        b_rows = sb("ga_b", [P, HD], F32, c)
        m_rows = sb("ga_m", [P, H], F32, c)
        prod = sb("ga_prod", [P, HD], F32, c)
        score = sb("ga_score", [P, H], F32, c)
        dstf = sb("ga_dstf", [P, 1], F32, c)
        rel = sb("ga_rel", [P, 1], F32, c)
        spread = sb("ga_spread", [P, 3, 4, P], F32, c)
        mask = sb("ga_mask", [P, P], F32, c)
        masked = sb("ga_masked", [P, H, P], F32, c)
        top = sb("ga_top", [P, H], F32, c)
        most = sb("ga_most", [P, NT, H], F32, c)
        node_no = sb("ga_node_no", [P, NT], F32, c)
        tile_no = sb("ga_tile_no", [P, NT], F32, c)
        iota = sb("ga_iota", [P, P], F32, c)
        zero = sb("ga_zero", [P, H], F32, c)
        terms = sb("ga_terms", [P, W], F32, c)
        oh = sb("ga_oh", [P, P], F32, c)
        acc = sb("ga_acc", [P, NT, W], F32, c)
        z = sb("ga_z", [P, NT, H], F32, c)
        root = sb("ga_root", [P, NT], F32, c)
        spread_ps = pb("ga_spread_ps", [P, 3, 4, P], F32, c)
        sum_ps = pb("ga_sum_ps", [P, 512], F32, c)
        names = ("const", "first", "idx_in", "rows_in", "score_made", "spread_ps", "chunk_over", "score_out", "max_out",
                 "score_in", "diff", "exp", "oh", "sum_ps", "vch", "wch", "deg", "root", "tick_dve", "tick_pe",
                 "tick_sp", "tick_pool", "tick_act")
        s = {n: sem("ga_" + n) for n in names}
        block = c.enter_context(nc.Block())

        def wait(engine, tick, semaphore, value):
            engine.wait_ge(semaphore, value)
            settle(engine, s[tick])

        def index_loads(sp, i, done):
            sp.wait_ge(s["chunk_over"], done)
            settle(sp, s["tick_sp"])
            col = lambda a, o: a[ds(i * P + o, P)].rearrange("(p c) -> p c", c=1)
            sp.dma_start(six[:], col(src_pad, 0)).then_inc(s["idx_in"], 16)
            sp.dma_start(dix[:], col(dst_pad, FRONT)).then_inc(s["idx_in"], 16)

        def gather(pool, out, table, idx):
            nc.gpsimd.indirect_dma_start(out[:], None, table, bass.IndirectOffsetOnAxis(idx[:, 0:1], 0)
                                         ).then_inc(s["rows_in"], 16)

        @block.sync
        def _(sp):
            flag = sp.value_load(irregular[0:1, 0:1], min_val=0, max_val=1)
            with sp.If(flag):
                with sp.Fori(0, NCH) as i:
                    index_loads(sp, i, i + 1)
                    wait(sp, "tick_sp", s["score_made"], i + 1)
                    sp.dma_start(edge_score[ds(i * P, P), :], score[:]).then_inc(s["score_out"], 16)
                    wait(sp, "tick_sp", s["score_out"], 16 * (i + 1))
                sp.wait_ge(s["chunk_over"], NCH + 1)
                sp.dma_start(max_tab[0:NP, :].rearrange("(t p) h -> p t h", p=P), most[:]).then_inc(s["max_out"], 16)
                sp.dma_start(max_tab[NP:TAB, :], zero[:]).then_inc(s["max_out"], 16)
                sp.wait_ge(s["max_out"], 32)
                with sp.Fori(0, NCH) as i:
                    index_loads(sp, i, i + NCH + 1)
                    sp.dma_start(score[:], edge_score[ds(i * P, P), :]).then_inc(s["score_in"], 16)

        @block.gpsimd
        def _(pool):
            flag = pool.value_load(irregular[0:1, 0:1], min_val=0, max_val=1)
            with pool.If(flag):
                nc.gpsimd.iota(node_no[:], [[P, NT]], base=0, channel_multiplier=1, allow_small_or_imprecise_dtypes=True)
                nc.gpsimd.iota(tile_no[:], [[P, NT]], base=0, channel_multiplier=0, allow_small_or_imprecise_dtypes=True)
                nc.gpsimd.iota(iota[:], [[1, P]], base=0, channel_multiplier=0, allow_small_or_imprecise_dtypes=True
                               ).then_inc(s["const"], 1)
                with pool.Fori(0, NCH) as i:
                    wait(pool, "tick_pool", s["idx_in"], 32 * (i + 1))
                    gather(pool, a_rows, ft_tab, six)
                    gather(pool, b_rows, ft_tab, dix)
                pool.wait_ge(s["max_out"], 32)
                settle(pool, s["tick_pool"])
                with pool.Fori(0, NCH) as i:
                    wait(pool, "tick_pool", s["idx_in"], 32 * (i + NCH + 1))
                    gather(pool, a_rows, ft_tab, six)
                    gather(pool, m_rows, max_tab, dix)

        @block.vector
        def _(dve):
            flag = dve.value_load(irregular[0:1, 0:1], min_val=0, max_val=1)
            with dve.If(flag):
                dve.wait_ge(s["const"], 1)
                nc.vector.memset(zero[:], 0.0)
                nc.vector.memset(terms[:, W - 1:W], 1.0)
                nc.vector.memset(acc[:], 0.0)
                nc.vector.memset(most[:], NEG).then_inc(s["first"], 1)
                dve.wait_ge(s["first"], 1)
                dve.sem_inc(s["chunk_over"], 1)
                PER = 3
                with dve.Fori(0, NCH) as i:
                    ch = Chain(dve, s["wch"], i * PER)
                    wait(dve, "tick_dve", s["rows_in"], 32 * (i + 1))
                    ch(nc.vector.tensor_tensor(prod[:], a_rows[:], b_rows[:], ALU.mult))
                    ch(nc.vector.tensor_reduce(score[:], prod[:].rearrange("p (h d) -> p h d", d=DH), AX.X, ALU.add))
                    nc.vector.tensor_copy(dstf[:], dix[:]).then_inc(s["score_made"], 1)
                    wait(dve, "tick_dve", s["spread_ps"], i + 1)
                    flat = lambda v: v[:].rearrange("p a b e -> p (a b) e")[:, 0:H + 1, :]
                    ch(nc.vector.tensor_copy(flat(spread), flat(spread_ps)))
                    settle(dve, s["tick_dve"])
                    with dve.Fori(0, NT) as k:
                        link = Chain(dve, s["vch"], (i * NT + k) * 4)
                        col = spread[:].rearrange("p a b e -> p (a b) e")
                        link(nc.vector.tensor_scalar(mask[:], col[:, H, :], node_no[:, ds(k, 1)], NEG, ALU.not_equal, ALU.mult))
                        link(nc.vector.tensor_tensor(masked[:], col[:, 0:H, :], mask[:].unsqueeze(1).to_broadcast([P, H, P]), ALU.add))
                        link(nc.vector.tensor_reduce(top[:], masked[:], AX.X, ALU.max))
                        now = most[:, ds(k, 1), :].rearrange("p a h -> p (a h)")
                        link(nc.vector.tensor_tensor(now, now, top[:], ALU.max))
                    dve.wait_ge(s["score_out"], 16 * (i + 1))
                    dve.sem_inc(s["chunk_over"], 1)
                with dve.Fori(0, NCH) as i:
                    wait(dve, "tick_dve", s["rows_in"], 32 * (i + NCH + 1))
                    wait(dve, "tick_dve", s["score_in"], 16 * (i + 1))
                    nc.vector.tensor_copy(dstf[:], dix[:])
                    nc.vector.tensor_tensor(score[:], score[:], m_rows[:], ALU.subtract).then_inc(s["diff"], 1)
                    wait(dve, "tick_dve", s["exp"], i + 1)
                    ch = Chain(dve, s["wch"], NCH * PER + i)
                    ch(nc.vector.tensor_tensor(terms[:, 0:HD].rearrange("p (h d) -> p h d", d=DH),
                                               a_rows[:].rearrange("p (h d) -> p h d", d=DH),
                                               terms[:, HD:HD + H].unsqueeze(2).to_broadcast([P, H, DH]), ALU.mult))
                    settle(dve, s["tick_dve"])
                    with dve.Fori(0, NT) as k:
                        n = i * NT + k
                        link = Chain(dve, s["vch"], NCH * NT * 4 + n * 2)
                        link(nc.vector.tensor_scalar(rel[:], dstf[:], tile_no[:, ds(k, 1)], None, ALU.subtract))
                        nc.vector.tensor_scalar(oh[:], iota[:], rel[:], None, ALU.is_equal).then_inc(s["oh"], 1)
                        wait(dve, "tick_dve", s["sum_ps"], n + 1)
                        now = acc[:, ds(k, 1), :].rearrange("p a w -> p (a w)")
                        link(nc.vector.tensor_tensor(now, now, sum_ps[:, 0:W], ALU.add))
                    dve.sem_inc(s["chunk_over"], 1)
                ch = Chain(dve, s["wch"], NCH * PER + NCH)
                nc.vector.tensor_copy(dis_col[:], acc[:, :, W - 1]).then_inc(s["deg"], 1)
                ch(nc.vector.tensor_scalar(z[:], acc[:, :, HD:HD + H], 1e-30, None, ALU.max))
                ch(nc.vector.reciprocal(z[:], z[:]))
                for k in range(NT // BATCH):
                    b = slice(k * BATCH, (k + 1) * BATCH)
                    nc.vector.tensor_tensor(agg_sb[:, b, :].rearrange("p t (h d) -> p t h d", d=DH),
                                            acc[:, b, 0:HD].rearrange("p t (h d) -> p t h d", d=DH),
                                            z[:, b, :].unsqueeze(3).to_broadcast([P, BATCH, H, DH]), ALU.mult)
                dve.wait_ge(s["root"], 1)
                nc.vector.reciprocal(dis_col[:], root[:])

        @block.scalar
        def _(act):
            flag = act.value_load(irregular[0:1, 0:1], min_val=0, max_val=1)
            with act.If(flag):
                with act.Fori(0, NCH) as i:
                    act.wait_ge(s["diff"], i + 1)
                    nc.scalar.activation(terms[:, HD:HD + H], score[:], ACT.Exp, scale=float(DH) ** -0.5
                                         ).then_inc(s["exp"], 1)
                act.wait_ge(s["deg"], 1)
                nc.scalar.activation(root[:], dis_col[:], ACT.Sqrt, bias=1.0).then_inc(s["root"], 1)

        @block.tensor
        def _(pe):
            flag = pe.value_load(irregular[0:1, 0:1], min_val=0, max_val=1)
            with pe.If(flag):
                with pe.Fori(0, NCH) as i:
                    wait(pe, "tick_pe", s["score_made"], i + 1)
                    for h in range(H + 1):
                        src = score[:, h:h + 1] if h < H else dstf[:]
                        last = nc.tensor.matmul(spread_ps[:, h // 4, h % 4, :], src.to_broadcast([P, P]), ident[:],
                                                start=True, stop=True)
                    last.then_inc(s["spread_ps"], 1)
                with pe.Fori(0, NCH) as i:
                    with pe.Fori(0, NT) as k:
                        wait(pe, "tick_pe", s["oh"], i * NT + k + 1)
                        nc.tensor.matmul(sum_ps[:, 0:W], oh[:], terms[:], start=True, stop=True).then_inc(s["sum_ps"], 1)


def node_update(nc, t, sb, pb, sem, g, ln_batch):
    agg_sb, hn_dram, x_sb, ident, ones, eps, hT = (g[k] for k in (
        "agg_sb", "hn_dram", "x_sb", "ident", "ones", "eps", "hT"))
    F = 4 * D
    BH = BW // 2
    R3 = HD + 1 - P
    with ExitStack() as c:
        la, lb = ln_batch("ua", c), ln_batch("ub", c)
        hr_w = sb("hr_w", [P, D], F32, c)
        hr_3 = sb("hr_3", [R3, D], F32, c)
        in_w = sb("nu_in_w", [P, D], F32, c)
        in_b = sb("nu_in_b", [P, D], F32, c)
        w1 = sb("nu_w1", [D, F], F32, c)
        b1 = sb("nu_b1", [P, 4], F32, c)
        w2 = sb("nu_w2", [P, 4, D], F32, c)
        b2 = sb("nu_b2", [1, D], F32, c)
        ex = sb("nu_ex", [P, BATCH, HD], F32, c)
        el = sb("nu_el", [P, BATCH, HD + 1], F32, c)
        elT = sb("nu_elT", [P, BATCH, P], F32, c)
        el3T = sb("nu_el3T", [R3, BATCH, P], F32, c)
        hn = sb("nu_hn", [P, BATCH, D], F32, c)
        o = sb("nu_o", [P, BATCH, D], F32, c)
        s2 = sb("nu_s2", [P, BATCH, D], F32, c)
        skip = sb("nu_skip", [P, BATCH, D], F32, c)
        s2T = sb("nu_s2T", [D, BATCH, P], F32, c)
        exF = [sb(f"nu_exF{u}", [P, BW], F32, c) for u in range(2)]
        uT = sb("nu_uT", [P, 4, BW], F32, c)
        v = sb("nu_v", [P, BATCH, D], F32, c)
        h = sb("nu_h", [P, BATCH, D], F32, c)
        el_ps = pb("nu_el_ps", [P, 2, 512], F32, c)
        el3_ps = pb("nu_el3_ps", [P, 2, 512], F32, c)
        even_ps = pb("nu_even_ps", [P, 2, 512], F32, c)
        odd_ps = pb("nu_odd_ps", [P, 2, 512], F32, c)
        names = ("w_in", "ex", "el", "el_turned", "elT", "el3T", "projected", "var", "sd", "s2", "s2_turned", "s2T",
                 "up_ps", "exF", "uT", "v_ps", "exV", "v", "var2", "sd2", "nb2", "h", "h_turned", "hT", "first_chain",
                 "second_chain", "one", "hn_in", "tick", "tick_sp")
        s = {n: sem("nu_" + n) for n in names}
        block = c.enter_context(nc.Block())

        @block.sync
        def _(sp):
            loads = [(hr_w[:], t["L0_gnn_hr_w"][0:P, :]), (hr_3[0:R3 - 1, :], t["L0_gnn_hr_w"][P:HD, :]),
                     (hr_3[R3 - 1:R3, :], t["L0_gnn_hr_b"].rearrange("(a d) -> a d", a=1)),
                     (in_w[:], row_bc(t["L0_gnn_in_w"])), (in_b[:], row_bc(t["L0_gnn_in_b"])),
                     (w1[:], t["L0_gnn_w1"]), (w2[:], t["L0_gnn_w2"].rearrange("(f p) d -> p f d", p=P)),
                     (b2[:], t["L0_gnn_b2"].rearrange("(a d) -> a d", a=1))]
            for dst, src in loads:
                sp.dma_start(dst, src).then_inc(s["w_in"], 16)
            with nc.allow_non_contiguous_dma(reason="a bias, one value per partition"):
                sp.dma_start(b1[:], t["L0_gnn_b1"].rearrange("(f p) -> p f", p=P)).then_inc(s["w_in"], 16)

            def body(i, first):
                if not first:
                    sp.wait_ge(s["var"], i)
                    settle(sp, s["tick_sp"])
                sp.dma_start(hn[:], hn_dram[ds(i * BW, BW), :].rearrange("(b p) f -> p b f", p=P)).then_inc(s["hn_in"], 16)
            rounds(sp, NB, body)

        def schedule(engine, first, turn_before, second):
            first(0)
            second(0, False, True)
            with engine.Fori(1, NB - 1) as i:
                second(i, True, True)
            second(NB - 1, True, False)
            turn_before(NB)

        flat = lambda a: a[:].rearrange("p b d -> p (b d)")
        halves = lambda a: a.rearrange("p (a b) -> p a b", a=2)

        @block.vector
        def _(dve):
            nc.vector.memset(el[:, :, HD:HD + 1], 1.0).then_inc(s["one"], 1)
            dve.wait_ge(s["one"], 1)
            dve.wait_ge(s["w_in"], 9 * 16)
            FIRST, SECOND = 7, 10
            wide = [P, BATCH, D]
            agg = lambda i: agg_sb[:, ds(i * BATCH, BATCH), :]

            def elu_attention(i, link):
                dve.wait_ge(s["ex"], i + 1)
                link(nc.vector.tensor_scalar(ex[:], ex[:], 1.0, -1.0, ALU.min, ALU.add))
                nc.vector.tensor_tensor(el[:, :, 0:HD], ex[:], agg(i), ALU.max).then_inc(s["el"], 1)

            def last_rows(i):
                dve.wait_ge(s["el_turned"], i + 1)
                nc.vector.tensor_copy(el3T[:, 0:4, :].rearrange("f b p -> f (b p)"), el3_ps[0:R3, 0, :])
                nc.vector.tensor_copy(el3T[:, 4:7, :].rearrange("f b p -> f (b p)"), el3_ps[0:R3, 1, 0:384]
                                      ).then_inc(s["el3T"], 1)

            def add_skip(i, link):
                dve.wait_ge(s["hn_in"], 16 * (i + 1))
                dve.wait_ge(s["projected"], i + 1)
                nc.vector.tensor_tensor(o[:, 0:4, :], el_ps[:, 0, :].rearrange("p (b d) -> p b d", d=D),
                                        hn[:, 0:4, :], ALU.add)
                link(nc.vector.tensor_tensor(o[:, 4:7, :], el_ps[:, 1, 0:384].rearrange("p (b d) -> p b d", d=D),
                                             hn[:, 4:7, :], ALU.add))
                link(layer_norm_stats(nc, dve, link, la, lambda b: o[:, b, :], s["tick"]))
                nc.vector.tensor_tensor(o[:], o[:], la["mv"][:, :, 0:1].to_broadcast(wide), ALU.subtract
                                        ).then_inc(s["var"], 1)

            def norm(i, link):
                dve.wait_ge(s["sd"], i + 1)
                dve.wait_ge(s["var"], i + 1)
                link(nc.vector.reciprocal(la["rs"][:], la["sd"][:]))
                link(nc.vector.tensor_tensor(o[:], o[:], la["rs"][:].unsqueeze(2).to_broadcast(wide), ALU.mult))
                link(nc.vector.tensor_tensor(o[:], o[:], in_w[:].unsqueeze(1).to_broadcast(wide), ALU.mult))
                nc.vector.tensor_tensor(s2[:], o[:], in_b[:].unsqueeze(1).to_broadcast(wide), ALU.add
                                        ).then_inc(s["s2"], 1)

            def elu_quarter(i, f, link):
                ps = (even_ps, odd_ps)[f % 2]
                dve.wait_ge(s["exF"], 4 * i + f + 1)
                link(nc.vector.tensor_scalar(exF[f % 2][:], exF[f % 2][:], 1.0, -1.0, ALU.min, ALU.add))
                nc.vector.scalar_tensor_tensor(halves(uT[:, f, :]), ps[:, :, 0:BH], b1[:, f:f + 1],
                                               halves(exF[f % 2][:]), ALU.add, ALU.max).then_inc(s["uT"], 1)

            def add_feed_forward(i, link):
                dve.wait_ge(s["exV"], i + 1)
                link(nc.vector.tensor_scalar(exF[0][:], exF[0][:], 1.0, -1.0, ALU.min, ALU.add))
                nc.vector.tensor_tensor(flat(v)[:, 0:512], even_ps[:, 0, :], exF[0][:, 0:512], ALU.max)
                nc.vector.tensor_tensor(flat(v)[:, 512:BW], even_ps[:, 1, 0:384], exF[0][:, 512:BW], ALU.max
                                        ).then_inc(s["v"], 1)
                dve.wait_ge(s["v"], i + 1)
                link(nc.vector.tensor_tensor(v[:], v[:], skip[:], ALU.add))
                xb = x_sb[:, ds(i * BATCH, BATCH), :]
                link(nc.vector.tensor_tensor(xb, xb, v[:], ALU.add))
                settle(dve, s["tick"])
                layer_norm_stats(nc, dve, link, lb, lambda b: x_sb[:, ds(i * BATCH + b, 1), :], s["tick"]
                                 ).then_inc(s["var2"], 1)

            def first(i):
                link = Chain(dve, s["first_chain"], 0)
                elu_attention(i, link)
                last_rows(i)
                add_skip(i, link)
                norm(i, link)
                assert link.n == FIRST

            def second(i, turn, more):
                a, b = Chain(dve, s["first_chain"], (i + 1) * FIRST), Chain(dve, s["second_chain"], i * SECOND)
                dve.wait_ge(s["s2"], i + 1)
                b(nc.vector.tensor_copy(skip[:], s2[:]))
                if more:
                    elu_attention(i + 1, a)
                elu_quarter(i, 0, b)
                elu_quarter(i, 1, b)
                if more:
                    last_rows(i + 1)
                elu_quarter(i, 2, b)
                elu_quarter(i, 3, b)
                if more:
                    add_skip(i + 1, a)
                add_feed_forward(i, b)
                if more:
                    dve.wait_ge(s["s2_turned"], i + 1)
                    norm(i + 1, a)
                dve.wait_ge(s["sd2"], i + 1)
                dve.wait_ge(s["var2"], i + 1)
                b(nc.vector.reciprocal(lb["rs"][:], lb["sd"][:]))
                nc.vector.scalar_tensor_tensor(lb["nb"][:], lb["mv"][:, :, 0], -1.0, lb["rs"][:], ALU.mult, ALU.mult
                                               ).then_inc(s["nb2"], 1)
                dve.wait_ge(s["h"], i + 1)
                assert b.n == SECOND, b.n
            schedule(dve, first, lambda i: None, second)

        @block.scalar
        def _(act):
            act.wait_ge(s["w_in"], 9 * 16)

            def exp_attention(i, later):
                if later:
                    act.wait_ge(s["el"], i)
                nc.scalar.activation(ex[:], agg_sb[:, ds(i * BATCH, BATCH), :], ACT.Exp).then_inc(s["ex"], 1)

            def copy_turned(out, ps, turned, done, i):
                act.wait_ge(turned, i + 1)
                nc.scalar.copy(out[:, 0:4, :].rearrange("f b p -> f (b p)"), ps[:, 0, :])
                nc.scalar.copy(out[:, 4:7, :].rearrange("f b p -> f (b p)"), ps[:, 1, 0:384]).then_inc(done, 1)

            def deviation(i, ln, var, sd):
                act.wait_ge(var, i + 1)
                nc.scalar.activation(ln["sd"][:], ln["mv"][:, :, 1], ACT.Sqrt, bias=eps[:]).then_inc(sd, 1)

            def exp_quarter(i, f):
                act.wait_ge(s["up_ps"], 4 * i + f + 1)
                if f >= 2:
                    act.wait_ge(s["uT"], 4 * i + f - 1)
                nc.scalar.activation(halves(exF[f % 2][:]), (even_ps, odd_ps)[f % 2][:, :, 0:BH], ACT.Exp,
                                     bias=b1[:, f:f + 1]).then_inc(s["exF"], 1)

            def hT_out(i):
                act.wait_ge(s["h_turned"], i)
                nc.scalar.copy(hT[:, ds((i - 1) * BW, 512)], el3_ps[:, 0, :])
                nc.scalar.copy(hT[:, ds((i - 1) * BW + 512, BW - 512)], el3_ps[:, 1, 0:384]).then_inc(s["hT"], 1)

            def first(i):
                exp_attention(i, False)
                copy_turned(elT, el_ps, s["el_turned"], s["elT"], i)
                deviation(i, la, s["var"], s["sd"])

            def second(i, turn, more):
                if more:
                    exp_attention(i + 1, True)
                copy_turned(s2T, odd_ps, s["s2_turned"], s["s2T"], i)
                exp_quarter(i, 0)
                exp_quarter(i, 1)
                if turn:
                    hT_out(i)
                if more:
                    copy_turned(elT, el_ps, s["el_turned"], s["elT"], i + 1)
                exp_quarter(i, 2)
                exp_quarter(i, 3)
                act.wait_ge(s["v_ps"], i + 1)
                nc.scalar.activation(exF[0][:, 0:512], even_ps[:, 0, :], ACT.Exp)
                nc.scalar.activation(exF[0][:, 512:BW], even_ps[:, 1, 0:384], ACT.Exp).then_inc(s["exV"], 1)
                if more:
                    deviation(i + 1, la, s["var"], s["sd"])
                deviation(i, lb, s["var2"], s["sd2"])
                act.wait_ge(s["nb2"], i + 1)
                if turn:
                    act.wait_ge(s["h_turned"], i)
                for b in range(BATCH):
                    last = nc.scalar.activation(h[:, b, :], x_sb[:, ds(i * BATCH + b, 1), :], ACT.Relu,
                                                bias=lb["nb"][:, b:b + 1], scale=lb["rs"][:, b:b + 1])
                last.then_inc(s["h"], 1)
            schedule(act, first, hT_out, second)

        @block.tensor
        def _(pe):
            pe.wait_ge(s["w_in"], 9 * 16)

            def turn(ps, src):
                for b in range(BATCH):
                    last = nc.tensor.transpose(ps[:, b // 4, (b % 4) * P:(b % 4 + 1) * P], src[:, b, 0:P], ident[:])
                return last

            def turn_attention(i, later, h_before):
                pe.wait_ge(s["el"], i + 1)
                if later:
                    pe.wait_ge(s["var"], i)
                if h_before:
                    pe.wait_ge(s["hT"], i - 1)
                elif later:
                    pe.wait_ge(s["el3T"], i)
                turn(el_ps, el)
                for b in range(BATCH):
                    last = nc.tensor.transpose(el3_ps[0:R3, b // 4, (b % 4) * P:(b % 4 + 1) * P], el[:, b, P:HD + 1],
                                               ident[:])
                last.then_inc(s["el_turned"], 1)

            def project(i):
                pe.wait_ge(s["elT"], i + 1)
                pe.wait_ge(s["el3T"], i + 1)
                for b in range(BATCH):
                    at = el_ps[:, b // 4, (b % 4) * P:(b % 4 + 1) * P]
                    nc.tensor.matmul(at, elT[:, b, :], hr_w[:], start=True, stop=False)
                    last = nc.tensor.matmul(at, el3T[:, b, :], hr_3[:], start=False, stop=True)
                last.then_inc(s["projected"], 1)

            def quarter(i, f, later):
                ps = (even_ps, odd_ps)[f % 2]
                if f == 0:
                    pe.wait_ge(s["s2T"], i + 1)
                    if later:
                        pe.wait_ge(s["v"], i)
                if f >= 2:
                    pe.wait_ge(s["uT"], 4 * i + f - 1)
                for a in range(2):
                    last = nc.tensor.matmul(ps[:, a, 0:BH], w1[:, f * P:(f + 1) * P],
                                            s2T[:].rearrange("f b p -> f (b p)")[:, a * BH:(a + 1) * BH],
                                            start=True, stop=True)
                last.then_inc(s["up_ps"], 1)

            def turn_h(i):
                pe.wait_ge(s["h"], i)
                turn(el3_ps, h).then_inc(s["h_turned"], 1)

            def first(i):
                turn_attention(i, False, False)
                project(i)

            def second(i, turn_, more):
                pe.wait_ge(s["s2"], i + 1)
                if turn_:
                    pe.wait_ge(s["uT"], 4 * i)
                turn(odd_ps, s2).then_inc(s["s2_turned"], 1)
                quarter(i, 0, turn_)
                quarter(i, 1, turn_)
                if turn_:
                    turn_h(i)
                if more:
                    turn_attention(i + 1, True, turn_)
                quarter(i, 2, turn_)
                quarter(i, 3, turn_)
                if more:
                    project(i + 1)
                pe.wait_ge(s["uT"], 4 * i + 4)
                for b in range(BATCH):
                    at = even_ps[:, b // 4, (b % 4) * P:(b % 4 + 1) * P]
                    for f in range(4):
                        nc.tensor.matmul(at, uT[:, f, b * P:(b + 1) * P], w2[:, f, :], start=(f == 0), stop=False)
                    last = nc.tensor.matmul(at, ones[0:1, :], b2[:], start=False, stop=True)
                last.then_inc(s["v_ps"], 1)
            schedule(pe, first, turn_h, second)


def convolutions(nc, t, sb, pb, sem, g):
    (adj, x_sb, ident, ident_bf, dis_col, eps, hT, out, src_pad, dst_pad, parts_tab, irregular) = (g[k] for k in (
        "adj", "x_sb", "ident", "ident_bf", "dis_col", "eps", "hT", "out", "src_pad", "dst_pad", "parts_tab",
        "irregular"))
    NCH = EP // P
    L = 4
    with ExitStack() as c:
        parts = sb("cv_parts", [P, NT, 3, D], BF16, c)
        cnt = [sb(f"cv_cnt{q}", [P, SPG, CMAX * SUB], BF16, c) for q in range(3)]
        dis_row = sb("cv_dis_row", [P, NP], F32, c)
        W = sb("cv_W", [D, L, D], F32, c)
        bias = sb("cv_bias", [D, L], F32, c)
        gam = sb("cv_gam", [D, L], F32, c)
        bet = sb("cv_bet", [D, L], F32, c)
        isbn = sb("cv_isbn", [D, L], F32, c)
        notbn = sb("cv_notbn", [D, L], F32, c)
        stage = [sb(f"cv_stage{u}", [D, BATCH, P], F32, c) for u in range(2)]
        dis7 = sb("cv_dis7", [P, BATCH], F32, c)
        hs = [sb(f"cv_hs{u}", [P, BATCH, D], F32, c) for u in range(2)]
        res = sb("cv_res", [P, BATCH, D], F32, c)
        y = sb("cv_y", [D, GRP], F32, c)
        stats = sb("cv_stats", [D, NGR + 1, 6], F32, c)
        mv = sb("cv_mv", [D, 2], F32, c)
        sd = sb("cv_sd", [D, 1], F32, c)
        scale = sb("cv_scale", [D, 1], F32, c)
        shift = sb("cv_shift", [D, 1], F32, c)
        tmp = sb("cv_tmp", [D, 1], F32, c)
        six = sb("cv_six", [P, 1], I32, c)
        dix = sb("cv_dix", [P, 1], I32, c)
        rows = sb("cv_rows", [P, 3, D], BF16, c)
        dstf = sb("cv_dstf", [P, 1], F32, c)
        rel = sb("cv_rel", [P, 1], F32, c)
        oh = sb("cv_oh", [P, P], BF16, c)
        iota = sb("cv_iota", [P, P], F32, c)
        tile_no = sb("cv_tile_no", [P, NT], F32, c)
        w_ps = [pb(f"cv_w_ps{u}", [P, 2, 512], F32, c) for u in range(2)]
        acc = [pb(f"cv_acc{s}", [D, GRP], F32, c) for s in range(2)]
        names = ("par_in", "const", "dis7", "row_ps", "row", "staged", "w_ps", "hs", "split", "acc",
                 "y", "vch", "dch", "var", "sd", "ready", "out_ps", "sum", "tick", "tick_pe", "tick_sp",
                 "tick_pool", "iotas", "table_out", "idx_in", "rows_in", "chunk_over", "oh", "part_ps", "gch", "fch", "loop_free")
        s = {n: sem("cv_" + n) for n in names}
        cnt_in = [sem(f"cv_cnt_in{q}") for q in range(3)]
        acc_read = [sem(f"cv_acc_read{u}") for u in range(2)]
        uses = (NGR // 2 + 1, NGR // 2)
        cnt_used = [sem(f"cv_cnt_used{q}") for q in range(3)]
        out_done = [sem(f"cv_out{u}") for u in range(2)]
        NGA = NGR + 1
        LW = NP - NGR * GRP
        block = c.enter_context(nc.Block())


        def in_pairs(engine, ahead, step):
            ahead(0, 0)
            with engine.Fori(0, NB // 2) as m:
                for u in range(2):
                    ahead(2 * m + u + 1, 1 - u)
                    step(2 * m + u, u)
            step(NB - 1, 0)

        @block.sync
        def _(sp):
            for l, name in enumerate(("W1", "W2", "W3", "W3")):
                sp.dma_start(W[:, l, :], t["L1_gnn_" + name]).then_inc(s["par_in"], 16)
            with nc.allow_non_contiguous_dma(reason="vectors, one value per partition"):
                col = lambda n: t["L1_gnn_" + n].rearrange("(d a) -> d a", a=1)
                for l, name in enumerate(("b1", "b2", "b3", "b3")):
                    sp.dma_start(bias[:, l:l + 1], col(name)).then_inc(s["par_in"], 16)
                for l in range(2):
                    sp.dma_start(gam[:, l:l + 1], col(f"g{l + 1}")).then_inc(s["par_in"], 16)
                    sp.dma_start(bet[:, l:l + 1], col(f"be{l + 1}")).then_inc(s["par_in"], 16)
            flag = sp.value_load(irregular[0:1, 0:1], min_val=0, max_val=1)
            with sp.Fori(0, L) as l:
              with sp.If(flag):
                sp.wait_ge(s["split"], (l + 1) * NB + 2)
                settle(sp, s["tick_sp"])
                sp.dma_start(parts_tab.rearrange("(t p) k -> p t k", p=P), parts[:].rearrange("p t r d -> p t (r d)")
                             ).then_inc(s["table_out"], 16)
                sp.wait_ge(s["table_out"], 16 * (l + 1))
                settle(sp, s["tick_sp"])
                with sp.Fori(0, NCH) as i:
                    sp.wait_ge(s["chunk_over"], l * NCH + i + 1)
                    settle(sp, s["tick_sp"])
                    sp.dma_start(six[:], src_pad[ds(i * P, P)].rearrange("(p c) -> p c", c=1)).then_inc(s["idx_in"], 16)
                    sp.dma_start(dix[:], dst_pad[ds(i * P + FRONT, P)].rearrange("(p c) -> p c", c=1)
                                 ).then_inc(s["idx_in"], 16)
              with sp.Else():
                with sp.Fori(0, NGR) as i:
                    for q, (b0, n) in enumerate(CHUNKS):
                        sp.wait_ge(cnt_used[q], l * NGA + i + 1)
                        sp.dma_start(cnt[q][:, :, 0:n * SUB], adj[ds(i * SPG, SPG), :, b0 * SUB:(b0 + n) * SUB]
                                     .rearrange("t p s -> p t s")).then_inc(cnt_in[q], 16)
                for q, (b0, n) in enumerate(CHUNKS):
                    sp.wait_ge(cnt_used[q], l * NGA + NGR + 1)
                    sp.dma_start(cnt[q][:, 0:LW // SUB, 0:n * SUB], adj[NGR * SPG:NS, :, b0 * SUB:(b0 + n) * SUB]
                                 .rearrange("t p s -> p t s")).then_inc(cnt_in[q], 16)
            with sp.Fori(0, NB // 2) as m:
                for u in range(2):
                    sp.wait_ge(s["sum"], 2 * m + u + 3)
                    sp.dma_start(out[ds((2 * m + u) * BW, BW), :].rearrange("(b p) d -> p b d", p=P), hs[u][:]
                                 ).then_inc(out_done[u], 16)
            sp.wait_ge(s["sum"], NB + 2)
            sp.dma_start(out[(NB - 1) * BW:(NT - 1) * P, :].rearrange("(b p) d -> p b d", p=P), hs[0][:, 0:BATCH - 1, :]
                         ).then_inc(out_done[0], 16)
            sp.dma_start(out[(NT - 1) * P:N, :], hs[0][0:N_LAST, BATCH - 1, :]).then_inc(out_done[0], 16)
            sp.wait_ge(out_done[0], 16 * (NB // 2 + 2))
            sp.wait_ge(out_done[1], 16 * (NB // 2))

        @block.gpsimd
        def _(pool):
            nc.gpsimd.iota(iota[:], [[1, P]], base=0, channel_multiplier=0, allow_small_or_imprecise_dtypes=True)
            nc.gpsimd.iota(tile_no[:], [[P, NT]], base=0, channel_multiplier=0, allow_small_or_imprecise_dtypes=True
                           ).then_inc(s["iotas"], 1)
            flag = pool.value_load(irregular[0:1, 0:1], min_val=0, max_val=1)
            with pool.If(flag):
                with pool.Fori(0, L * NCH) as i:
                    pool.wait_ge(s["idx_in"], 32 * (i + 1))
                    settle(pool, s["tick_pool"])
                    nc.gpsimd.indirect_dma_start(rows[:].rearrange("p r d -> p (r d)"), None, parts_tab,
                                                 bass.IndirectOffsetOnAxis(six[:, 0:1], 0)).then_inc(s["rows_in"], 16)

        @block.vector
        def _(dve):
            flag = dve.value_load(irregular[0:1, 0:1], min_val=0, max_val=1)
            dve.wait_ge(s["iotas"], 1)
            for u in range(2):
                dve.sem_inc(acc_read[u], 1)
            for n in ("ready", "chunk_over", "loop_free"):
                dve.sem_inc(s[n], 1)
            dve.sem_inc(s["split"], 2)
            link = Chain(dve, s["const"])
            nc.vector.memset(isbn[:, 0:2], 1.0)
            nc.vector.memset(isbn[:, 2:L], 0.0)
            nc.vector.memset(notbn[:, 0:2], 0.0)
            nc.vector.memset(notbn[:, 2:L], 1.0)
            nc.vector.memset(gam[:, 2:L], 0.0)
            nc.vector.memset(bet[:, 2:L], 0.0)
            nc.vector.memset(shift[:], 0.0)
            link(nc.vector.memset(scale[:], 1.0))
            def columns(k, first):
                if not first:
                    dve.wait_ge(s["row_ps"], k)
                    settle(dve, s["tick"])
                nc.vector.tensor_copy(dis7[:], dis_col[:, ds(k * BATCH, BATCH)]).then_inc(s["dis7"], 1)
            rounds(dve, NB, columns)
            dve.wait_ge(s["par_in"], 16 * 12)
            dve.wait_ge(s["row"], NB)
            PER = 4
            with dve.Fori(0, L) as l:
                def split(k, u):
                    n = l * NB + k
                    ch = Chain(dve, s["vch"], n * PER)
                    dve.wait_ge(s["hs"], n + 3)
                    part = lambda q: parts[:, ds(k * BATCH, BATCH), q, :]
                    ch(nc.vector.tensor_copy(part(0), hs[u][:]))
                    ch(nc.vector.tensor_tensor(res[:], hs[u][:], part(0), ALU.subtract))
                    ch(nc.vector.tensor_copy(part(1), res[:]))
                    ch(nc.vector.tensor_tensor(res[:], res[:], part(1), ALU.subtract))
                    nc.vector.tensor_copy(part(2), res[:]).then_inc(s["split"], 1)
                    dve.wait_ge(s["split"], n + 3)
                in_pairs(dve, lambda k, u: None, split)
                settle(dve, s["tick"])

                def finish_group(n, u, use, at, width, real, stat):
                    dve.wait_ge(s["acc"], n + 1)
                    nc.vector.tensor_tensor(y[:, 0:width], acc[u][:, 0:width], dis_row[:, at], ALU.mult
                                            ).then_inc(acc_read[u], 1)
                    dve.wait_ge(acc_read[u], use + 2)
                    ch = Chain(dve, s["dch"], n)
                    ch(nc.vector.tensor_scalar(hT[:, at], y[:, 0:width], bias[:, ds(l, 1)], None, ALU.add))
                    return nc.vector.bn_stats(stat, hT[:, real])

                with dve.If(flag):
                    with dve.Fori(0, NT) as k:
                        dve.wait_ge(s["part_ps"], l * (NT + NCH * NT) + k + 1)
                        settle(dve, s["tick"])
                        nc.vector.tensor_copy(hT[:, ds(k * P, P)], acc[0][:, 0:P]).then_inc(s["gch"], 1)
                        dve.wait_ge(s["gch"], l * (NT + NCH * (1 + 2 * NT)) + k + 1)
                        dve.sem_inc(s["loop_free"], 1)
                    with dve.Fori(0, NCH) as i:
                        before = l * (NT + NCH * (1 + 2 * NT)) + NT + i * (1 + 2 * NT)
                        dve.wait_ge(s["rows_in"], 16 * (l * NCH + i + 1))
                        settle(dve, s["tick"])
                        Chain(dve, s["gch"], before)(nc.vector.tensor_copy(dstf[:], dix[:]))
                        settle(dve, s["tick"])
                        with dve.Fori(0, NT) as k:
                            ch = Chain(dve, s["gch"], before + 1 + 2 * k)
                            ch(nc.vector.tensor_scalar(rel[:], dstf[:], tile_no[:, ds(k, 1)], None, ALU.subtract))
                            nc.vector.tensor_scalar(oh[:], iota[:], rel[:], None, ALU.is_equal).then_inc(s["oh"], 1)
                            dve.wait_ge(s["part_ps"], l * (NT + NCH * NT) + NT + i * NT + k + 1)
                            settle(dve, s["tick"])
                            ch(nc.vector.tensor_tensor(hT[:, ds(k * P, P)], hT[:, ds(k * P, P)], acc[0][:, 0:P], ALU.add))
                        dve.sem_inc(s["chunk_over"], 1)

                    def finish_part(n, at, width, real, stat):
                        ch = Chain(dve, s["fch"], n * 2)
                        ch(nc.vector.tensor_tensor(y[:, 0:width], hT[:, at], dis_row[:, at], ALU.mult))
                        ch(nc.vector.tensor_scalar(hT[:, at], y[:, 0:width], bias[:, ds(l, 1)], None, ALU.add))
                        return nc.vector.bn_stats(stat, hT[:, real])

                    with dve.Fori(0, NGR) as i:
                        finish_part(l * NGA + i, ds(i * GRP, GRP), GRP, ds(i * GRP, GRP), stats[:, ds(i, 1), :])
                    finish_part(l * NGA + NGR, slice(NGR * GRP, NP), LW, slice(NGR * GRP, N),
                                stats[:, NGR:NGR + 1, :]).then_inc(s["y"], 1)
                with dve.Else():
                    with dve.Fori(0, NGR // 2) as j:
                        for u in range(2):
                            i = j * 2 + u
                            at = ds(i * GRP, GRP)
                            finish_group(l * NGA + i, u, l * uses[u] + j, at, GRP, at, stats[:, ds(i, 1), :])
                    finish_group(l * NGA + NGR, 0, l * uses[0] + NGR // 2, slice(NGR * GRP, NP), LW,
                                 slice(NGR * GRP, N), stats[:, NGR:NGR + 1, :]).then_inc(s["y"], 1)
                dve.wait_ge(s["y"], l * 7 + 1)
                ch = Chain(dve, s["y"], l * 7 + 1)
                settle(dve, s["tick"])
                ch(nc.vector.bn_aggr(mv[:], stats[:].rearrange("d a b -> d (a b)")))
                nc.vector.tensor_copy(tmp[:], mv[:, 0:1]).then_inc(s["var"], 1)
                dve.wait_ge(s["var"], l + 1)
                dve.wait_ge(s["sd"], l + 1)
                ch(nc.vector.reciprocal(sd[:], sd[:]))
                ch(nc.vector.tensor_tensor(sd[:], sd[:], gam[:, ds(l, 1)], ALU.mult))
                ch(nc.vector.scalar_tensor_tensor(tmp[:], tmp[:], -1.0, sd[:], ALU.mult, ALU.mult))
                ch(nc.vector.tensor_tensor(tmp[:], tmp[:], bet[:, ds(l, 1)], ALU.add))
                ch(nc.vector.tensor_tensor(shift[:], tmp[:], isbn[:, ds(l, 1)], ALU.mult))
                nc.vector.scalar_tensor_tensor(scale[:], sd[:], isbn[:, ds(l, 1)], notbn[:, ds(l, 1)],
                                               ALU.mult, ALU.add).then_inc(s["ready"], 1)

            def add(k, u, j, first):
                dve.wait_ge(s["out_ps"], k + 3)
                if not first:
                    dve.wait_ge(out_done[u], 16 * j)
                nc.vector.tensor_tensor(hs[u][:, 0:4, :], x_sb[:, ds(k * BATCH, 4), :],
                                        w_ps[u][:, 0, :].rearrange("p (b d) -> p b d", d=D), ALU.add)
                nc.vector.tensor_tensor(hs[u][:, 4:7, :], x_sb[:, ds(k * BATCH + 4, 3), :],
                                        w_ps[u][:, 1, 0:384].rearrange("p (b d) -> p b d", d=D), ALU.add
                                        ).then_inc(s["sum"], 1)
            add(0, 0, 0, True)
            add(1, 1, 0, True)
            with dve.Fori(1, NB // 2) as j:
                for u in range(2):
                    add(2 * j + u, u, j, False)
            add(NB - 1, 0, NB // 2, False)

        @block.scalar
        def _(act):
            with act.Fori(0, NB) as k:
                act.wait_ge(s["row_ps"], k + 1)
                nc.scalar.copy(dis_row[:, ds(k * BW, 512)], w_ps[0][:, 0, :])
                nc.scalar.copy(dis_row[:, ds(k * BW + 512, BW - 512)], w_ps[0][:, 1, 0:384]).then_inc(s["row"], 1)
            act.wait_ge(s["const"], 1)
            with act.Fori(0, L) as l:
                act.wait_ge(s["ready"], l + 1)

                def rectify(k, u):
                    act.wait_ge(s["w_ps"], l * NB + k + 1)
                    nc.scalar.activation(stage[u][:].rearrange("f b p -> f (b p)"), hT[:, ds(k * BW, BW)], ACT.Relu,
                                         bias=shift[:], scale=scale[:]).then_inc(s["staged"], 1)

                def scaled(k, u):
                    n = l * NB + k
                    act.wait_ge(s["w_ps"], n + 3)
                    act.wait_ge(s["split"], n + 1)
                    for b in range(BATCH):
                        last = nc.scalar.activation(hs[u][:, b, :], w_ps[u][:, b // 4, (b % 4) * D:(b % 4 + 1) * D],
                                                    ACT.Copy, scale=dis_col[:, ds(k * BATCH + b, 1)])
                    last.then_inc(s["hs"], 1)
                in_pairs(act, rectify, scaled)
                act.wait_ge(s["y"], l * 7 + 2)
                act.wait_ge(s["var"], l + 1)
                nc.scalar.activation(sd[:], mv[:, 1:2], ACT.Sqrt, bias=eps[:]).then_inc(s["sd"], 1)
            act.wait_ge(s["ready"], L + 1)
            act.sem_inc(s["out_ps"], 2)

            def last_layer(k, u):
                act.wait_ge(s["out_ps"], k + 1)
                nc.scalar.copy(stage[u][:].rearrange("f b p -> f (b p)"), hT[:, ds(k * BW, BW)]).then_inc(s["staged"], 1)
            with act.Fori(0, NB // 2) as m:
                for u in range(2):
                    last_layer(2 * m + u, u)
            last_layer(NB - 1, 0)

        @block.tensor
        def _(pe):
            for q in range(3):
                pe.sem_inc(cnt_used[q], 1)
            pe.sem_inc(s["w_ps"], 2)

            def row(k, first):
                pe.wait_ge(s["dis7"], k + 1)
                if not first:
                    pe.wait_ge(s["row"], k)
                for b in range(BATCH):
                    last = nc.tensor.matmul(w_ps[0][:, b // 4, (b % 4) * P:(b % 4 + 1) * P],
                                            dis7[:, b:b + 1].to_broadcast([P, P]), ident[:], start=True, stop=True)
                last.then_inc(s["row_ps"], 1)
            rounds(pe, NB, row)
            flag = pe.value_load(irregular[0:1, 0:1], min_val=0, max_val=1)
            pe.wait_ge(s["row"], NB)
            pe.wait_ge(s["par_in"], 16 * 12)

            def group(l, n, a, tile0, width):
                for q, (b0, m) in enumerate(CHUNKS):
                    pe.wait_ge(cnt_in[q], (n + 1) * 16)
                    pe.wait_ge(s["split"], l * NB + -(-(b0 + m) // BATCH) + 2)
                    for b in range(b0, b0 + m):
                        for r in range(3):
                            last = nc.tensor.matmul(a[:, 0:width], parts[:, b, r, :],
                                                    cnt[q][:, 0:width // SUB, (b - b0) * SUB:(b - b0 + 1) * SUB],
                                                    start=(b == 0 and r == 0), stop=False)
                    last.then_inc(cnt_used[q], 1)
                for b in range(width // P):
                    for r in range(3):
                        w = parts[:, ds(tile0 + b, 1), r, :].rearrange("p a d -> p (a d)")
                        last = nc.tensor.matmul(a[:, b * P:(b + 1) * P], w, ident_bf[:], start=False,
                                                stop=(b == width // P - 1 and r == 2))
                last.then_inc(s["acc"], 1)

            pe.sem_inc(s["hs"], 2)
            with pe.Fori(0, L) as l:
                def product(k, u):
                    n = l * NB + k
                    pe.wait_ge(s["staged"], n + 1)
                    pe.wait_ge(s["hs"], n + 1)
                    for b in range(BATCH):
                        last = nc.tensor.matmul(w_ps[u][:, b // 4, (b % 4) * D:(b % 4 + 1) * D], stage[u][:, b, :],
                                                W[:, ds(l, 1), :].rearrange("f a d -> f (a d)"), start=True, stop=True)
                    last.then_inc(s["w_ps"], 1)
                in_pairs(pe, lambda k, u: None, product)
                with pe.If(flag):
                    pe.wait_ge(s["split"], (l + 1) * NB + 2)
                    settle(pe, s["tick_pe"])
                    with pe.Fori(0, NT) as k:
                        pe.wait_ge(s["loop_free"], l * NT + k + 1)
                        settle(pe, s["tick_pe"])
                        for r in range(3):
                            last = nc.tensor.matmul(acc[0][:, 0:P], parts[:, ds(k, 1), r, :].rearrange("p a d -> p (a d)"),
                                                    ident_bf[:], start=(r == 0), stop=(r == 2))
                        last.then_inc(s["part_ps"], 1)
                    with pe.Fori(0, NCH * NT) as k:
                        pe.wait_ge(s["oh"], l * (NCH * NT) + k + 1)
                        settle(pe, s["tick_pe"])
                        for r in range(3):
                            last = nc.tensor.matmul(acc[0][:, 0:P], rows[:, r, :], oh[:], start=(r == 0), stop=(r == 2))
                        last.then_inc(s["part_ps"], 1)
                with pe.Else():
                    with pe.Fori(0, NGR // 2) as j:
                        for u in range(2):
                            i = j * 2 + u
                            n = l * NGA + i
                            pe.wait_ge(acc_read[u], l * uses[u] + j + 1)
                            group(l, n, acc[u], i * (GRP // P), GRP)
                    pe.wait_ge(acc_read[0], l * uses[0] + NGR // 2 + 1)
                    group(l, l * NGA + NGR, acc[0], NGR * (GRP // P), LW)

            pe.sem_inc(s["sum"], 2)

            def turn(k, u):
                pe.wait_ge(s["staged"], L * NB + k + 1)
                pe.wait_ge(s["sum"], k + 1)
                for b in range(BATCH):
                    last = nc.tensor.transpose(w_ps[u][:, b // 4, (b % 4) * P:(b % 4 + 1) * P], stage[u][:, b, :],
                                               ident[:])
                last.then_inc(s["out_ps"], 1)
            with pe.Fori(0, NB // 2) as m:
                for u in range(2):
                    turn(2 * m + u, u)
            turn(NB - 1, 0)


_INS = ['x', 'src', 'dst', 'L0_gnn_ln1_w', 'L0_gnn_ln1_b', 'L0_gnn_W_att', 'L0_gnn_hr_w', 'L0_gnn_hr_b',
        'L0_gnn_in_w', 'L0_gnn_in_b', 'L0_gnn_w1', 'L0_gnn_b1', 'L0_gnn_w2', 'L0_gnn_b2', 'L1_gnn_W1', 'L1_gnn_b1',
        'L1_gnn_g1', 'L1_gnn_be1', 'L1_gnn_W2', 'L1_gnn_b2', 'L1_gnn_g2', 'L1_gnn_be2', 'L1_gnn_W3', 'L1_gnn_b3']


def kernel(**inputs):
    import numpy as _np
    import concourse.bacc as _bacc
    from concourse import mybir as _mybir
    from concourse.bass_utils import run_bass_kernel_spmd as _run

    nc = _bacc.Bacc("TRN2", target_bir_lowering=False, num_devices=1)
    arrays, aps = {}, {}
    for name in _INS:
        a = _np.ascontiguousarray(inputs[name])
        arrays[f"in_{name}"] = a
        aps[name] = nc.dram_tensor(f"in_{name}", a.shape, _mybir.dt.from_np(a.dtype), kind="ExternalInput").ap()
    aps["out"] = nc.dram_tensor("out_0", (6250, 128), _mybir.dt.float32, kind="ExternalOutput").ap()
    gnn_program(nc, aps)
    r = _run(nc, [arrays], core_ids=[0])
    return r.results[0]["out_0"]
```
